# Optimizing a Trainium2 kernel written in Bass

```python
import numpy as np
import jax
import jax.numpy as jnp

def _softmax(x, axis=-1):
    return jax.nn.softmax(x, axis=axis)

def _gelu(x):
    return jax.nn.gelu(x, approximate=True)

def _silu(x):
    return jax.nn.silu(x)

def _sigmoid(x):
    return jax.nn.sigmoid(x)

def _layernorm(x, axis=-1, eps=1e-05):
    m = jnp.mean(x, axis=axis, keepdims=True)
    v = jnp.var(x, axis=axis, keepdims=True)
    return (x - m) / jnp.sqrt(v + eps)

def _scatter_add(tgt, idx, src, axis=0):
    return tgt.at[idx].add(src)

def _segment_sum(src, seg, n):
    return jax.ops.segment_sum(src, seg, n)
kernel_name = 'mk_gnn_ffn_d1_gnn_r8_49a7ac'

def setup_inputs(seed: int=0):
    np.random.seed(seed)
    _w = jnp.asarray

    def _rec_inputs():
        import jax
        import jax.numpy as jnp
        _gk = jax.random.key(seed)
        x = -0.0003713 + 1 * jax.random.normal(jax.random.fold_in(_gk, 1), (6250, 256), jnp.float32)
        src = jax.random.randint(jax.random.fold_in(_gk, 2), (200000,), 0, 6250, jnp.int32)
        dst = jnp.minimum((6250 * jax.random.uniform(jax.random.fold_in(_gk, 3), (200000,)) ** 2.0).astype(jnp.int32), 49999)
        _o = jnp.argsort(dst, stable=True)
        src = src[_o]
        dst = dst[_o]
        return (x, src, dst)
    x, src, dst = _rec_inputs()

    def _L0_gnn_setup():
        import jax, jax.numpy as jnp
        import numpy as np
        N = 6250
        E = 50000
        DIN = 256
        H = 4
        C = 64
        ALPHA = 0.5
        SLOPE = 0.2

        def _gat_dir(x, src, dst, W, a_src, a_dst, b):
            h = (x @ W).reshape(N, H, C)
            es = jnp.sum(h * a_src, axis=-1)
            ed = jnp.sum(h * a_dst, axis=-1)
            e = jax.nn.leaky_relu(es[src] + ed[dst], SLOPE)
            emax = jax.ops.segment_max(e, dst, num_segments=N)
            p = jnp.exp(e - emax[dst])
            denom = jax.ops.segment_sum(p, dst, num_segments=N)
            alpha = p / denom[dst]
            out = jax.ops.segment_sum(alpha[:, :, None] * h[src], dst, num_segments=N)
            return out.reshape(N, H * C) + b
        key = jax.random.key(seed)
        ks = jax.random.split(key, 12)
        x = jax.random.normal(ks[0], (N, DIN), dtype=jnp.float32)
        edge_index = jax.random.randint(ks[1], (2, E), 0, N, dtype=jnp.int32)
        s = 1.0 / np.sqrt(DIN)
        sa = 1.0 / np.sqrt(C)

        def mk(i, shape, scale):
            return jax.random.normal(ks[i], shape, dtype=jnp.float32) * scale
        return {'x': x, 'edge_index': edge_index, 'W1': mk(2, (DIN, H * C), s), 'a_src1': mk(3, (H, C), sa), 'a_dst1': mk(4, (H, C), sa), 'b1': jnp.zeros((H * C,), jnp.float32), 'W2': mk(5, (DIN, H * C), s), 'a_src2': mk(6, (H, C), sa), 'a_dst2': mk(7, (H, C), sa), 'b2': jnp.zeros((H * C,), jnp.float32)}
    _L0_gnn_all = _L0_gnn_setup()
    _L0_gnn_in = {k: v for k, v in _L0_gnn_all.items() if k in ('W1', 'a_src1', 'a_dst1', 'b1', 'W2', 'a_src2', 'a_dst2', 'b2')}
    del _L0_gnn_all

    def _L0_ffn_setup():
        import jax, jax.numpy as jnp
        import numpy as np
        TOP_K = 2
        LN_EPS = 1e-05
        key = jax.random.key(seed)
        ks = jax.random.split(key, 8)
        B, S, D, E, H = (16, 1024, 256, 8, 1024)
        x = jax.random.normal(ks[0], (B, S, D), dtype=jnp.float32)
        Wr = jax.random.normal(ks[1], (D, E), dtype=jnp.float32) * 0.1
        br = jnp.zeros((E,), dtype=jnp.float32)
        ln_g = jnp.ones((E, D), dtype=jnp.float32)
        ln_b = jnp.zeros((E, D), dtype=jnp.float32)
        W1 = jax.random.normal(ks[2], (E, D, H), dtype=jnp.float32) * (1.0 / np.sqrt(D))
        b1 = jnp.zeros((E, H), dtype=jnp.float32)
        W2 = jax.random.normal(ks[3], (E, H, D), dtype=jnp.float32) * (1.0 / np.sqrt(H))
        b2 = jnp.zeros((E, D), dtype=jnp.float32)
        return {'x': x, 'Wr': Wr, 'br': br, 'ln_g': ln_g, 'ln_b': ln_b, 'W1': W1, 'b1': b1, 'W2': W2, 'b2': b2}
    _L0_ffn_all = _L0_ffn_setup()
    _L0_ffn_in = {k: v for k, v in _L0_ffn_all.items() if k in ('Wr', 'br', 'ln_g', 'ln_b', 'W1', 'b1', 'W2', 'b2')}
    del _L0_ffn_all
    return {'x': x, 'src': src, 'dst': dst, 'L0_gnn_W1': _L0_gnn_in['W1'], 'L0_gnn_a_src1': _L0_gnn_in['a_src1'], 'L0_gnn_a_dst1': _L0_gnn_in['a_dst1'], 'L0_gnn_b1': _L0_gnn_in['b1'], 'L0_gnn_W2': _L0_gnn_in['W2'], 'L0_gnn_a_src2': _L0_gnn_in['a_src2'], 'L0_gnn_a_dst2': _L0_gnn_in['a_dst2'], 'L0_gnn_b2': _L0_gnn_in['b2'], 'L0_ffn_Wr': _L0_ffn_in['Wr'], 'L0_ffn_br': _L0_ffn_in['br'], 'L0_ffn_ln_g': _L0_ffn_in['ln_g'], 'L0_ffn_ln_b': _L0_ffn_in['ln_b'], 'L0_ffn_W1': _L0_ffn_in['W1'], 'L0_ffn_b1': _L0_ffn_in['b1'], 'L0_ffn_W2': _L0_ffn_in['W2'], 'L0_ffn_b2': _L0_ffn_in['b2']}

def reference(x, src, dst, L0_gnn_W1, L0_gnn_a_src1, L0_gnn_a_dst1, L0_gnn_b1, L0_gnn_W2, L0_gnn_a_src2, L0_gnn_a_dst2, L0_gnn_b2, L0_ffn_Wr, L0_ffn_br, L0_ffn_ln_g, L0_ffn_ln_b, L0_ffn_W1, L0_ffn_b1, L0_ffn_W2, L0_ffn_b2):
    import jax
    import jax.numpy as jnp

    def _L0_gnn_ref(x, edge_index, W1, a_src1, a_dst1, b1, W2, a_src2, a_dst2, b2):
        import jax, jax.numpy as jnp
        import numpy as np
        N = 6250
        E = 50000
        DIN = 256
        H = 4
        C = 64
        ALPHA = 0.5
        SLOPE = 0.2

        def _gat_dir(x, src, dst, W, a_src, a_dst, b):
            h = (x @ W).reshape(N, H, C)
            es = jnp.sum(h * a_src, axis=-1)
            ed = jnp.sum(h * a_dst, axis=-1)
            e = jax.nn.leaky_relu(es[src] + ed[dst], SLOPE)
            emax = jax.ops.segment_max(e, dst, num_segments=N)
            p = jnp.exp(e - emax[dst])
            denom = jax.ops.segment_sum(p, dst, num_segments=N)
            alpha = p / denom[dst]
            out = jax.ops.segment_sum(alpha[:, :, None] * h[src], dst, num_segments=N)
            return out.reshape(N, H * C) + b
        loops = jnp.arange(N, dtype=edge_index.dtype)
        src = jnp.concatenate([edge_index[0], loops])
        dst = jnp.concatenate([edge_index[1], loops])
        out_s2d = _gat_dir(x, src, dst, W1, a_src1, a_dst1, b1)
        out_d2s = _gat_dir(x, dst, src, W2, a_src2, a_dst2, b2)
        return (1.0 - ALPHA) * out_s2d + ALPHA * out_d2s

    def _L0_ffn_ref(x, Wr, br, ln_g, ln_b, W1, b1, W2, b2):
        import jax, jax.numpy as jnp
        import numpy as np
        TOP_K = 2
        LN_EPS = 1e-05
        B, S, D = x.shape
        N = B * S
        xt = x.reshape(N, D)
        logits = xt @ Wr + br
        probs = jax.nn.softmax(logits, axis=-1)
        top_p, top_idx = jax.lax.top_k(probs, TOP_K)
        weights = top_p / top_p.sum(axis=-1, keepdims=True)
        mu = xt.mean(axis=-1, keepdims=True)
        var = ((xt - mu) ** 2).mean(axis=-1, keepdims=True)
        xn = (xt - mu) * jax.lax.rsqrt(var + LN_EPS)
        xe = xn[None, :, :] * ln_g[:, None, :] + ln_b[:, None, :]
        h = jax.nn.gelu(jnp.einsum('end,edh->enh', xe, W1) + b1[:, None, :], approximate=False)
        y = jnp.einsum('enh,ehd->end', h, W2) + b2[:, None, :]
        y_tok = jnp.transpose(y, (1, 0, 2))
        sel = jnp.take_along_axis(y_tok, top_idx[:, :, None], axis=1)
        out = (weights[:, :, None] * sel).sum(axis=1)
        return out.reshape(B, S, D)
    edge_index = jnp.stack([src, dst])
    x = x + _L0_gnn_ref(_layernorm(x, axis=-1), edge_index, L0_gnn_W1, L0_gnn_a_src1, L0_gnn_a_dst1, L0_gnn_b1, L0_gnn_W2, L0_gnn_a_src2, L0_gnn_a_dst2, L0_gnn_b2)
    x = x + _L0_ffn_ref(_layernorm(x, axis=-1)[None], L0_ffn_Wr, L0_ffn_br, L0_ffn_ln_g, L0_ffn_ln_b, L0_ffn_W1, L0_ffn_b1, L0_ffn_W2, L0_ffn_b2)[0]
    return x

_drawn_inputs = setup_inputs


def setup_inputs(seed=0):
    import zlib

    import numpy as np

    out = dict(_drawn_inputs(seed))
    spreads = {'L0_gnn_b1': (0.0, 0.1),
     'L0_gnn_b2': (0.0, 0.1),
     'L0_ffn_br': (0.0, 0.1),
     'L0_ffn_ln_g': (1.0, 0.2),
     'L0_ffn_ln_b': (0.0, 0.1),
     'L0_ffn_b1': (0.0, 0.1),
     'L0_ffn_b2': (0.0, 0.1)}
    factors = {}
    for name, (base, spread) in spreads.items():
        noise = np.random.default_rng([zlib.crc32(name.encode()), seed]).standard_normal(out[name].shape)
        drawn = base * np.exp(spread * noise) if base else spread * noise
        out[name] = jnp.asarray(drawn.astype(out[name].dtype))
    for name, factor in factors.items():
        out[name] = (out[name] * factor).astype(out[name].dtype)
    return out
```

```python
from contextlib import ExitStack

import concourse.bass as bass
from concourse import mybir

F32 = mybir.dt.float32
BF16 = mybir.dt.bfloat16
F16 = mybir.dt.float16
I32 = mybir.dt.int32
ALU = mybir.AluOpType
ACT = mybir.ActivationFunctionType
AX = mybir.AxisListType

P = 128
N_NODES = 6250
D = 256
HEADS = 4
C = D // HEADS
ROW = D + HEADS
N_EDGES = 200000
EXPERTS = 8
HID = 1024
EPS = 1e-5
SLOPE = 0.2

NB = -(-N_NODES // P)
TAIL = N_NODES - (NB - 1) * P
NPAD = NB * P
DIRS = 2

EP = 125
ECOLS = N_EDGES // EP
CHUNKS = 4
CC = ECOLS // CHUNKS
GC = 5
NG = CC // GC
ITEMS = -(-(EP * CC + NB * (P - 1)) // P)
ITEMS += -ITEMS % 8
N_ITEMS = DIRS * CHUNKS * ITEMS
PACK = 4
ACC_BITS = 7
assert DIRS * NB <= 1 << ACC_BITS
assert EP * ECOLS == N_EDGES and GC * NG == CC and NG <= P and ITEMS <= 512


class Kept:
    pass


class Count:

    def __init__(self, sem, eng):
        self.sem, self.eng, self.n = sem, eng, 0

    def mark(self, ins):
        ins.then_inc(self.sem, 1)
        self.n = self.n + 1

    def link(self, ins):
        self.mark(ins)
        self.eng.wait_ge(self.sem, self.n)


def after(eng, sem, value):
    if not isinstance(value, int) or value > 0:
        eng.wait_ge(sem, value)


class Scope(ExitStack):

    def __init__(self, nc, stage):
        super().__init__()
        self.nc, self.stage = nc, stage

    def sb(self, name, shape, dt):
        return self.enter_context(self.nc.sbuf_tensor(f"{self.stage}_{name}", shape, dt))

    def ps(self, name, shape, dt=F32):
        return self.enter_context(self.nc.psum_tensor(f"{self.stage}_{name}", shape, dt))

    def sem(self, name):
        return self.enter_context(self.nc.semaphore(f"{self.stage}_{name}"))


def make_constants(nc, s, k):
    k.row16 = s.sb("row16", [P, 512], F16)
    k.rowf = s.sb("rowf", [P, P], F32)
    k.colf = s.sb("colf", [P, 1], F32)
    k.row_bf = s.sb("row_bf", [P, P], BF16)
    k.ident = s.sb("ident", [P, P], F32)
    k.ident_bf = s.sb("ident_bf", [P, P], BF16)
    k.below = s.sb("below", [P, P], F32)
    k.upto = s.sb("upto", [P, P], F32)
    k.below_items = s.sb("below_items", [P, P], F32)
    k.below_bf = s.sb("below_bf", [P, P], BF16)
    k.ones = s.sb("ones", [P, P], F32)
    k.ones_bf = s.sb("ones_bf", [P, P], BF16)
    iota_done = s.sem("iota_done")
    const_done = s.sem("const_done")
    with Scope(nc, "const") as t, nc.Block() as block:
        row_i = t.sb("row_i", [P, 512], I32)
        col_i = t.sb("col_i", [P, 1], I32)

        @block.gpsimd
        def _(pool):
            nc.gpsimd.iota(row_i[:], [[1, 512]], base=0, channel_multiplier=0).then_inc(iota_done, 1)
            nc.gpsimd.iota(col_i[:], [[0, 1]], base=0, channel_multiplier=1).then_inc(iota_done, 1)

        @block.vector
        def _(dve):
            dve.wait_ge(iota_done, 2)
            nc.vector.tensor_copy(k.row16[:], row_i[:])
            nc.vector.tensor_copy(k.row_bf[:], row_i[:, 0:P])
            nc.vector.memset(k.ones[:], 1.0)
            nc.vector.memset(k.ones_bf[:], 1.0)
            nc.vector.tensor_copy(k.colf[:], col_i[:]).then_inc(const_done, 1)
            nc.vector.tensor_copy(k.rowf[:], row_i[:, 0:P]).then_inc(const_done, 1)
            dve.wait_ge(const_done, 2)
            for out, op in ((k.ident, ALU.is_equal), (k.ident_bf, ALU.is_equal), (k.below, ALU.is_gt),
                            (k.below_bf, ALU.is_gt), (k.upto, ALU.is_ge)):
                nc.vector.tensor_scalar(out[:], k.rowf[:], k.colf[:], None, op)
            nc.vector.tensor_scalar(k.below_items[:], k.rowf[:], k.colf[:], float(P), ALU.is_gt, ALU.mult)


def sort_edges(nc, s, k, edges):
    k.src_row = s.sb("src_row", [P, N_ITEMS], I32)
    k.target = s.sb("target", [P, N_ITEMS], BF16)
    k.item_acc = s.sb("item_acc", [1, N_ITEMS // PACK], I32)
    BLOCKS = CC // (2 * GC)
    RING = 4
    with Scope(nc, "sort") as t:
        tgt = t.sb("tgt", [EP, CC], I32)
        src = t.sb("src", [EP, CC], I32)
        bucket_i = t.sb("bucket_i", [EP, CC], I32)
        local_i = t.sb("local_i", [EP, CC], I32)
        src_hi = t.sb("src_hi", [EP, CC], I32)
        src_lo = t.sb("src_lo", [EP, CC], I32)
        bucket = t.sb("bucket", [EP, CC], BF16)
        local_1 = t.sb("local_1", [EP, CC], F32)
        load_a = t.sb("load_a", [EP, CC], F32)
        load_b = t.sb("load_b", [EP, CC], F32)
        in_bucket = t.sb("in_bucket", [EP, CC, NB], BF16)
        window = t.sb("window", [EP, 2 * NG - 1], BF16)
        totals = t.sb("totals", [NG, NB], F32)
        filled = t.sb("filled", [NB, P], I32)
        items_i = t.sb("items_i", [NB, P], I32)
        items = t.sb("items", [NB, P], F32)
        ends = t.sb("ends", [NB, 1], F32)
        base_i = t.sb("base_i", [NG, NB], I32)
        base_hi_i = t.sb("base_hi_i", [NG, NB], I32)
        base_lo_i = t.sb("base_lo_i", [NG, NB], I32)
        base_hi = t.sb("base_hi", [NG, NB], F32)
        base_lo = t.sb("base_lo", [NG, NB], F32)
        diag_hi = t.sb("diag_hi", [NG, NG, NB], BF16)
        diag_lo = t.sb("diag_lo", [NG, NG, NB], BF16)
        past_end = t.sb("past_end", [NB, ITEMS], BF16)
        chosen = t.sb("chosen", [EP, 2, 2 * GC, NB], F32)
        slot = t.sb("slot", [EP, CC], F32)
        slot_i = t.sb("slot_i", [EP, CC], I32)
        item_i = t.sb("item_i", [EP, CC], I32)
        part_i = t.sb("part_i", [EP, CC], I32)
        item_f = t.sb("item_f", [EP, CC], F32)
        part_f = t.sb("part_f", [EP, CC], F32)
        put_a = t.sb("put_a", [EP, RING, P], F16)
        put_b = t.sb("put_b", [EP, RING, P], F16)
        put_item = t.sb("put_item", [EP, RING, ITEMS], F16)
        moved_i = t.sb("moved_i", [P, ITEMS], I32)
        moved_lo = t.sb("moved_lo", [P, ITEMS], I32)
        moved_hi = t.sb("moved_hi", [P, ITEMS], I32)
        src_f = t.sb("src_f", [P, ITEMS], F32)
        acc_f = t.sb("acc_f", [1, ITEMS // PACK, PACK], F32)
        acc_pair = t.sb("acc_pair", [1, ITEMS // PACK, PACK // 2], I32)

        small = t.ps("small", [P, 512])
        bucket_tot = small[0:NB, 64:64 + P]
        group_base, bucket_end = small[0:NG, 256:256 + NB], small[0:NB, 448:450]
        rank = [t.ps(f"rank{i}", [EP, 2 * GC, NB]) for i in range(2)]
        got_a = t.ps("got_a", [P, ITEMS])
        got_b = t.ps("got_b", [P, ITEMS])
        bucket_row = t.ps("bucket_row", [P, ITEMS])
        column_tot = bucket_row[0:NG, 0:GC * NB].rearrange("p (c b) -> p c b", c=GC)

        tgt_landed, src_landed = t.sem("tgt_landed"), t.sem("src_landed")
        ids_used = t.sem("ids_used")
        sort_steps = t.sem("sort_steps")
        hot_made = t.sem("hot_made")
        totals_made, totals_read = t.sem("totals_made"), t.sem("totals_read")
        fill_made, items_made = t.sem("fill_made"), t.sem("items_made")
        base_made, ends_read, diag_made = t.sem("base_made"), t.sem("ends_read"), t.sem("diag_made")
        buckets_made = t.sem("buckets_made")
        rank_made, rank_read = t.sem("rank_made"), t.sem("rank_read")
        slots_picked = t.sem("slots_picked")
        puts_made, puts_used = t.sem("puts_made"), t.sem("puts_used")

        with nc.Block() as block:

            @block.sync
            def _(sp):
                for n in range(DIRS * CHUNKS):
                    r, q = divmod(n, CHUNKS)
                    by = [edges[x, :].rearrange("(p c) -> p c", p=EP) for x in (1 - r, r)]
                    if n:
                        sp.wait_ge(ids_used, n)
                    sp.dma_start(tgt[:], by[0][:, q * CC:(q + 1) * CC]).then_inc(tgt_landed, 16)
                    sp.dma_start(src[:], by[1][:, q * CC:(q + 1) * CC]).then_inc(src_landed, 16)

            @block.vector
            def _(dve):
                v = nc.vector
                steps = Count(sort_steps, dve)
                steps.link(v.memset(window[:], 0.0))
                steps.link(v.memset(window[:, NG - 1:NG], 1.0))

                def split_ids(n):
                    dve.wait_ge(tgt_landed, 16 * (n + 1))
                    dve.wait_ge(src_landed, 16 * (n + 1))
                    v.tensor_scalar(bucket_i[:], tgt[:], 7, None, ALU.arith_shift_right)
                    v.tensor_scalar(local_i[:], tgt[:], P - 1, None, ALU.bitwise_and)
                    v.tensor_scalar(src_hi[:], src[:], 10, None, ALU.arith_shift_right)
                    v.tensor_scalar(src_lo[:], src[:], 1023, None, ALU.bitwise_and).then_inc(ids_used, 1)
                    dve.wait_ge(ids_used, n + 1)
                    v.tensor_scalar(local_1[:], local_i[:], 1.0, None, ALU.add)
                    v.tensor_copy(load_b[:], src_lo[:])
                    steps.link(v.tensor_copy(bucket[:], bucket_i[:]))
                    v.scalar_tensor_tensor(out=load_a[:], in0=src_hi[:], scalar=256.0, in1=local_1[:],
                                           op0=ALU.mult, op1=ALU.add)
                    v.tensor_tensor(in_bucket[:], bucket[:].unsqueeze(2).to_broadcast([EP, CC, NB]),
                                    k.row_bf[0:EP, 0:NB].unsqueeze(1).to_broadcast([EP, CC, NB]),
                                    ALU.is_equal).then_inc(hot_made, 1)

                def place_buckets(n):
                    dve.wait_ge(totals_made, n + 1)
                    v.tensor_reduce(totals[:], column_tot.rearrange("p c b -> p b c"), AX.X,
                                    ALU.add).then_inc(totals_read, 1)
                    dve.wait_ge(fill_made, n + 1)
                    steps.link(v.tensor_scalar(filled[:], bucket_tot, float(P - 1), None, ALU.add))
                    steps.link(v.tensor_scalar(items_i[:], filled[:], 7, None, ALU.arith_shift_right))
                    v.tensor_copy(items[:], items_i[:]).then_inc(items_made, 1)
                    dve.wait_ge(base_made, n + 1)
                    v.tensor_copy(ends[:], bucket_end[:, 0:1])
                    steps.link(v.tensor_copy(base_i[:], group_base))
                    v.tensor_scalar(past_end[:], k.row16[0:NB, 0:ITEMS], ends[:], None,
                                    ALU.is_ge).then_inc(ends_read, 1)
                    v.tensor_scalar(base_hi_i[:], base_i[:], 0x1FF00, None, ALU.bitwise_and)
                    steps.link(v.tensor_scalar(base_lo_i[:], base_i[:], 255, None, ALU.bitwise_and))
                    v.tensor_copy(base_hi[:], base_hi_i[:])
                    steps.link(v.tensor_copy(base_lo[:], base_lo_i[:]))
                    for diag, of in ((diag_hi, base_hi), (diag_lo, base_lo)):
                        last = v.tensor_tensor(diag[:], of[:].unsqueeze(1).to_broadcast([NG, NG, NB]),
                                               k.ident[0:NG, 0:NG].unsqueeze(2).to_broadcast([NG, NG, NB]),
                                               ALU.mult)
                    last.then_inc(diag_made, 1)
                    dve.wait_ge(buckets_made, n + 1)
                    steps.link(v.tensor_scalar(acc_f[:].rearrange("o i p -> o (i p)"), bucket_row[0:1, :],
                                               float(NB - 1), float(n // CHUNKS * NB), ALU.min, ALU.add))
                    for h in range(2):
                        last = v.scalar_tensor_tensor(
                            out=acc_pair[:, :, h:h + 1], in0=acc_f[:, :, 2 * h + 1:2 * h + 2],
                            scalar=float(1 << ACC_BITS), in1=acc_f[:, :, 2 * h:2 * h + 1], op0=ALU.mult, op1=ALU.add)
                    steps.link(last)
                    steps.link(v.tensor_scalar(acc_pair[:, :, 1:2], acc_pair[:, :, 1:2], 2 * ACC_BITS, None,
                                               ALU.logical_shift_left))
                    v.tensor_tensor(k.item_acc[0:1, n * (ITEMS // PACK):(n + 1) * (ITEMS // PACK)].rearrange(
                        "o (i p) -> o i p", p=1), acc_pair[:, :, 0:1], acc_pair[:, :, 1:2], ALU.bitwise_or)

                def pick_slots(n):
                    def pair(i):
                        for u in range(2):
                            dve.wait_ge(rank_made, i * 2 + (n * BLOCKS + u + 1))
                            v.tensor_tensor(chosen[:, u], rank[u][:],
                                            in_bucket[:, bass.ds(i * (4 * GC) + u * 2 * GC, 2 * GC), :],
                                            ALU.mult).then_inc(rank_read, 1)
                        dve.wait_ge(rank_read, i * 2 + (n * BLOCKS + 2))
                        v.tensor_reduce(slot[:, bass.ds(i * (4 * GC), 4 * GC)],
                                        chosen[:].rearrange("p u c b -> p (u c) b"), AX.X,
                                        ALU.add).then_inc(slots_picked, 1)

                    pair(0)
                    with dve.Fori(1, BLOCKS // 2) as i:
                        dve.wait_ge(slots_picked, i + n * (BLOCKS // 2))
                        pair(i)
                    dve.wait_ge(slots_picked, (n + 1) * (BLOCKS // 2))
                    steps.link(v.tensor_copy(slot_i[:], slot[:]))
                    v.tensor_scalar(item_i[:], slot_i[:], 7, None, ALU.arith_shift_right)
                    steps.link(v.tensor_scalar(part_i[:], slot_i[:], P - 1, None, ALU.bitwise_and))
                    v.tensor_copy(item_f[:], item_i[:])
                    steps.link(v.tensor_copy(part_f[:], part_i[:]))

                def put_column(c, at, wait):
                    if wait is not None:
                        dve.wait_ge(puts_used, wait)
                    part, item = part_f[:, bass.ds(c, 1)], item_f[:, bass.ds(c, 1)]
                    v.tensor_scalar(put_a[:, at], k.row16[0:EP, 0:P], part, load_a[:, bass.ds(c, 1)],
                                    ALU.is_equal, ALU.mult)
                    v.tensor_scalar(put_b[:, at], k.row16[0:EP, 0:P], part, load_b[:, bass.ds(c, 1)],
                                    ALU.is_equal, ALU.mult)
                    v.tensor_scalar(put_item[:, at], k.row16[0:EP, 0:ITEMS], item, None,
                                    ALU.is_equal).then_inc(puts_made, 1)

                def put_columns(n):
                    for u in range(RING):
                        put_column(u, u, n * CC - RING + u + 1 if n else None)
                    with dve.Fori(1, CC // RING) as i:
                        for u in range(RING):
                            put_column(i * RING + u, u, i * RING + (n * CC - RING + u + 1))

                def unpack_items(n):
                    at = slice(n * ITEMS, (n + 1) * ITEMS)
                    dve.wait_ge(puts_used, (n + 1) * CC)
                    steps.link(v.tensor_copy(moved_i[:], got_a[:]))
                    v.tensor_scalar(moved_lo[:], moved_i[:], 255, None, ALU.bitwise_and)
                    steps.link(v.tensor_scalar(moved_hi[:], moved_i[:], 8, None, ALU.arith_shift_right))
                    v.tensor_scalar(k.target[:, at], moved_lo[:], -1.0, None, ALU.add)
                    steps.link(v.scalar_tensor_tensor(out=src_f[:], in0=moved_hi[:], scalar=1024.0,
                                                      in1=got_b[:], op0=ALU.mult, op1=ALU.add))
                    v.tensor_scalar(k.src_row[:, at], src_f[:], float(n // CHUNKS * NPAD), None, ALU.add)

                for n in range(DIRS * CHUNKS):
                    split_ids(n)
                    place_buckets(n)
                    pick_slots(n)
                    put_columns(n)
                    unpack_items(n)

            @block.tensor
            def _(pe):
                mm = nc.tensor.matmul

                def count_groups(n):
                    def group(g, first, last):
                        return mm(column_tot, window[:, bass.ds(g * -1 + (NG - 1), NG)],
                                  in_bucket[:, bass.ds(g * GC, GC), :], start=first, stop=last)

                    pe.wait_ge(hot_made, n + 1)
                    group(0, True, False)
                    with pe.Fori(1, NG - 1) as g:
                        group(g, False, False)
                    group(NG - 1, False, True).then_inc(totals_made, 1)

                def bases(n):
                    pe.wait_ge(totals_read, n + 1)
                    mm(bucket_tot, totals[:], k.ones[0:NG, :], start=True, stop=True).then_inc(fill_made, 1)
                    pe.wait_ge(items_made, n + 1)
                    mm(group_base, k.below[0:NG, 0:NG], totals[:], start=True, stop=False)
                    mm(group_base, items[:, 0:NG], k.below_items[0:NB, 0:NB], start=False, stop=True)
                    mm(bucket_end, k.upto[0:NB, 0:NB], items[:, 0:2], start=True,
                       stop=True).then_inc(base_made, 1)
                    pe.wait_ge(ends_read, n + 1)
                    mm(bucket_row[0:1, :], k.ones_bf[0:NB, 0:1], past_end[:], start=True,
                       stop=True).then_inc(buckets_made, 1)
                    pe.wait_ge(diag_made, n + 1)

                def rank_block(i, u):
                    c0 = i * (4 * GC) + u * 2 * GC
                    mm(rank[u][:], k.below_bf[0:EP, 0:EP], in_bucket[:, bass.ds(c0, 2 * GC), :], start=True,
                       stop=False)
                    for h in range(2):
                        for c in range(GC - 1):
                            more = GC - 1 - c
                            mm(rank[u][:, h * GC + c + 1:(h + 1) * GC, :], k.ones_bf[0:EP, 0:EP],
                               in_bucket[:, bass.ds(c0 + (h * GC + c), 1), :].to_broadcast([EP, more, NB]),
                               start=False, stop=False)
                        for diag in (diag_hi, diag_lo):
                            last = mm(rank[u][:, h * GC:(h + 1) * GC, :], k.ones_bf[0:NG, 0:EP],
                                      diag[:, bass.ds(i * 4 + (u * 2 + h), 1), :].to_broadcast([NG, GC, NB]),
                                      start=False, stop=h == 1 and diag is diag_lo)
                    last.then_inc(rank_made, 1)

                def ranks(n):
                    for u in range(2):
                        rank_block(0, u)
                    with pe.Fori(1, BLOCKS // 2) as i:
                        for u in range(2):
                            pe.wait_ge(rank_read, i * 2 + (n * BLOCKS + u - 1))
                            rank_block(i, u)

                def move(c, at, n, first=False, last=False):
                    pe.wait_ge(puts_made, c + (n * CC + 1))
                    mm(got_a[:], put_a[:, at], put_item[:, at], start=first, stop=last)
                    mm(got_b[:], put_b[:, at], put_item[:, at], start=first, stop=last).then_inc(puts_used, 1)

                for n in range(DIRS * CHUNKS):
                    count_groups(n)
                    bases(n)
                    ranks(n)
                    for u in range(RING):
                        move(u, u, n, first=u == 0)
                    with pe.Fori(1, CC // RING - 1) as i:
                        for u in range(RING):
                            move(i * RING + u, u, n)
                    for u in range(RING):
                        move(CC - RING + u, u, n, last=u == RING - 1)


def leaky(v, out, x):
    return v.scalar_tensor_tensor(out=out, in0=x, scalar=SLOPE, in1=x, op0=ALU.mult, op1=ALU.max)


def moments(nc, steps, stats, mean, tmp):
    v = nc.vector
    v.tensor_tensor(mean, stats[:, :, 1], stats[:, :, 4], ALU.add)
    steps.link(v.tensor_tensor(tmp, stats[:, :, 1], stats[:, :, 4], ALU.subtract))
    v.tensor_scalar(mean, mean, 0.5, None, ALU.mult)
    steps.link(v.scalar_tensor_tensor(out=tmp, in0=tmp, scalar=D / 4, in1=tmp, op0=ALU.mult, op1=ALU.mult))
    steps.link(v.tensor_tensor(tmp, tmp, stats[:, :, 2], ALU.add))
    steps.link(v.tensor_tensor(tmp, tmp, stats[:, :, 5], ALU.add))
    return v.tensor_scalar(tmp, tmp, 1.0 / D, EPS, ALU.mult, ALU.add)


def node_tables(nc, s, k, x, weights, table):
    k.acc = s.sb("acc", [P, DIRS * NB, ROW], F32)
    k.pieces = s.sb("pieces", [P, DIRS * NB, 2 * HEADS, 3], BF16)
    WIDE = ROW + HEADS
    with Scope(nc, "nodes") as t:
        xs = k.acc[:, 0:NB, 0:D]
        w = t.sb("w", [P, DIRS, 2, WIDE], F32)
        a = t.sb("a", [P, DIRS, 2, D], F32)
        prod = t.sb("prod", [P, D], F32)
        stats = t.sb("stats", [P, NB, 6], F32)
        mean = t.sb("mean", [P, NB], F32)
        tmp = t.sb("tmp", [P, NB], F32)
        std = t.sb("std", [P, NB], F32)
        rstd = t.sb("rstd", [P, NB], F32)
        xn = t.sb("xn", [P, 2, D], F32)
        xt = t.sb("xt", [P, 2, 2, P], F32)
        logit_t = t.sb("logit_t", [P, DIRS * NB, HEADS], F32)
        tops = t.sb("tops", [P, DIRS, HEADS], F32)
        bound0 = t.sb("bound0", [P, DIRS, HEADS], F32)
        z = t.sb("z", [P, DIRS * NB, HEADS], F32)
        bound = t.sb("bound", [P, DIRS * NB, HEADS], F32)
        turned = [t.ps(f"turned{i}", [P, 2, P]) for i in range(2)]
        hs = [[t.ps(f"hs{i}{r}", [P, WIDE]) for r in range(DIRS)] for i in range(2)]

        XG = 7
        x_landed = [t.sem(f"x_landed{i}") for i in range(NB // XG + 1)]
        w_landed, a_landed = t.sem("w_landed"), t.sem("a_landed")
        node_steps = t.sem("node_steps")
        stats_made = t.sem("stats_made")
        var_made, std_made = t.sem("var_made"), t.sem("std_made")
        normed, turned_made, turned_read = t.sem("normed"), t.sem("turned_made"), t.sem("turned_read")
        h_made, h0_read, h1_read = t.sem("h_made"), t.sem("h0_read"), t.sem("h1_read")
        w_made, table_written = t.sem("w_made"), t.sem("table_written")
        tops_made, bound_made = t.sem("tops_made"), t.sem("bound_made")
        z_made, p_made, acc_started = t.sem("z_made"), t.sem("p_made"), t.sem("acc_started")
        pad_cleared = t.sem("pad_cleared")
        FULL = NB - 1

        with nc.Block() as block:

            @block.sync
            def _(sp):
                for r in range(DIRS):
                    sp.dma_start(w[:, r, :, 0:D], weights[r][0].rearrange("(k p) n -> p k n", p=P)).then_inc(w_landed, 16)
                    for y in range(2):
                        row = weights[r][1 + y].rearrange("(o h) c -> o (h c)", o=1)
                        sp.dma_start(a[:, r, y, :], row.to_broadcast([P, D])).then_inc(a_landed, 16)
                for i in range(NB // XG + 1):
                    if i * XG < FULL:
                        end = min((i + 1) * XG, FULL)
                        sp.dma_start(xs[:, i * XG:end, :], x[i * XG * P:end * P, :].rearrange(
                            "(b p) n -> p b n", p=P)).then_inc(x_landed[i], 16)
                sp.wait_ge(pad_cleared, 1)
                sp.dma_start(xs[0:TAIL, FULL, :], x[FULL * P:N_NODES, :]).then_inc(x_landed[NB // XG], 16)
                for r in range(DIRS):
                    sp.wait_ge((h0_read, h1_read)[r], NB)
                    sp.dma_start(table[r * NPAD:(r + 1) * NPAD, :].rearrange("(b p) n -> p b n", p=P),
                                 k.acc[:, r * NB:(r + 1) * NB, :]).then_inc(table_written, 16)
                sp.wait_ge(table_written, 16 * DIRS)

            @block.gpsimd
            def _(pool):
                pool.wait_ge(tops_made, 1)
                nc.gpsimd.partition_all_reduce(bound0[:].rearrange("p r h -> p (r h)"),
                                               tops[:].rearrange("p r h -> p (r h)"), P,
                                               bass.bass_isa.ReduceOp.max).then_inc(bound_made, 1)

            @block.vector
            def _(dve):
                v = nc.vector
                steps = Count(node_steps, dve)
                v.memset(xs[:, FULL, :], 0.0).then_inc(pad_cleared, 1)
                dve.wait_ge(w_landed, 16 * DIRS)
                dve.wait_ge(a_landed, 16 * 2 * DIRS)
                for r in range(DIRS):
                    for kt in range(2):
                        for y in range(2):
                            steps.link(v.tensor_tensor(prod[:], w[:, r, kt, 0:D], a[:, r, y, :], ALU.mult))
                            v.tensor_reduce(w[:, r, kt, D + y * HEADS:D + (y + 1) * HEADS],
                                            prod[:].rearrange("p (h c) -> p h c", h=HEADS),
                                            AX.X, ALU.add).then_inc(w_made, 1)
                            dve.wait_ge(w_made, (r * 2 + kt) * 2 + y + 1)
                for i in range(NB // XG + 1):
                    dve.wait_ge(x_landed[i], 16)
                with dve.Fori(0, NB) as i:
                    v.bn_stats(stats[:, bass.ds(i, 1), :].rearrange("p o n -> p (o n)"),
                               xs[:, bass.ds(i, 1), :].rearrange("p o n -> p (o n)")).then_inc(stats_made, 1)
                dve.wait_ge(stats_made, NB)
                moments(nc, steps, stats, mean[:], tmp[:]).then_inc(var_made, 1)
                dve.wait_ge(std_made, 1)
                steps.link(v.reciprocal(rstd[:], std[:]))

                def normalise(m, u):
                    after(dve, turned_made, m - 1)
                    v.tensor_scalar(xn[:, u], xs[:, bass.ds(m, 1), :].rearrange("p o n -> p (o n)"),
                                    mean[:, bass.ds(m, 1)], rstd[:, bass.ds(m, 1)],
                                    ALU.subtract, ALU.mult).then_inc(normed, 1)

                def keep_h0(m, u):
                    dve.wait_ge(h_made, m + 1)
                    v.tensor_copy(logit_t[:, bass.ds(m, 1), :].rearrange("p o h -> p (o h)"),
                                  hs[u][0][:, ROW:WIDE])
                    v.tensor_copy(k.acc[:, bass.ds(m, 1), :].rearrange("p o n -> p (o n)"),
                                  hs[u][0][:, 0:ROW]).then_inc(h0_read, 1)

                normalise(0, 0)
                normalise(1, 1)
                keep_h0(0, 0)
                with dve.Fori(1, FULL // 2) as i:
                    for u in range(2):
                        normalise(i * 2 + u, u)
                        keep_h0(i * 2 + (u - 1), (u + 1) % 2)
                normalise(FULL, 0)
                keep_h0(FULL - 1, 1)
                keep_h0(FULL, 0)
                dve.wait_ge(h0_read, NB)
                dve.wait_ge(h1_read, NB)
                for r in range(DIRS):
                    last = v.tensor_reduce(tops[:, r, :], k.acc[:, r * NB:r * NB + FULL, D:ROW].rearrange(
                        "p b h -> p h b"), AX.X, ALU.max)
                steps.link(last)
                for r in range(DIRS):
                    last = v.tensor_tensor(tops[0:TAIL, r, :], tops[0:TAIL, r, :],
                                           k.acc[0:TAIL, r * NB + FULL, D:ROW], ALU.max)
                last.then_inc(tops_made, 1)
                dve.wait_ge(bound_made, 1)
                for r in range(DIRS):
                    at = slice(r * NB, (r + 1) * NB)
                    last = v.tensor_tensor(bound[:, at, :], logit_t[:, at, :],
                                           bound0[:, r:r + 1, :].to_broadcast([P, NB, HEADS]), ALU.add)
                steps.link(v.tensor_tensor(z[:], logit_t[:], k.acc[:, :, D:ROW], ALU.add))
                leaky(v, bound[:], bound[:])
                steps.link(leaky(v, z[:], z[:]))
                v.tensor_tensor(z[:], z[:], bound[:], ALU.subtract).then_inc(z_made, 1)
                for y, of in enumerate((logit_t, bound)):
                    for piece in range(3):
                        part = k.pieces[:, :, y * HEADS:(y + 1) * HEADS, piece]
                        steps.link(v.tensor_copy(part, of[:]))
                        if piece < 2:
                            steps.link(v.tensor_tensor(of[:], of[:], part, ALU.subtract))
                dve.wait_ge(p_made, 1)
                dve.wait_ge(table_written, 16 * DIRS)
                for r in range(DIRS):
                    at = slice(r * NB, (r + 1) * NB)
                    h = k.acc[:, at, 0:D].rearrange("p b (h c) -> p b h c", h=HEADS)
                    v.tensor_tensor(h, h, z[:, at, :].unsqueeze(3).to_broadcast([P, NB, HEADS, C]), ALU.mult)
                v.tensor_copy(k.acc[:, :, D:ROW], z[:])

            @block.scalar
            def _(act):
                act.wait_ge(var_made, 1)
                nc.scalar.activation(std[:], tmp[:], ACT.Sqrt).then_inc(std_made, 1)

                def keep_h1(m, u):
                    act.wait_ge(h_made, m + 1)
                    nc.scalar.copy(logit_t[:, bass.ds(m + NB, 1), :].rearrange("p o h -> p (o h)"),
                                   hs[u][1][:, ROW:WIDE])
                    nc.scalar.copy(k.acc[:, bass.ds(m + NB, 1), :].rearrange("p o n -> p (o n)"),
                                   hs[u][1][:, 0:ROW]).then_inc(h1_read, 1)

                def keep_turned(m, u):
                    act.wait_ge(turned_made, m + 1)
                    after(act, h_made, m - 1)
                    nc.scalar.copy(xt[:, u], turned[u][:]).then_inc(turned_read, 1)

                keep_turned(0, 0)
                keep_turned(1, 1)
                keep_h1(0, 0)
                with act.Fori(1, FULL // 2) as i:
                    for u in range(2):
                        keep_turned(i * 2 + u, u)
                        keep_h1(i * 2 + (u - 1), (u + 1) % 2)
                keep_turned(FULL, 0)
                keep_h1(FULL - 1, 1)
                keep_h1(FULL, 0)
                act.wait_ge(z_made, 1)
                nc.scalar.activation(z[:], z[:], ACT.Exp).then_inc(p_made, 1)

            @block.tensor
            def _(pe):
                def turn(m, u):
                    pe.wait_ge(normed, m + 1)
                    after(pe, turned_read, m - 1)
                    for kt in range(2):
                        last = nc.tensor.transpose(turned[u][:, kt, :], xn[:, u, kt * P:(kt + 1) * P],
                                                   k.ident[:])
                    last.then_inc(turned_made, 1)

                def product(m, u):
                    pe.wait_ge(turned_read, m + 1)
                    after(pe, h0_read, m - 1)
                    after(pe, h1_read, m - 1)
                    for r in range(DIRS):
                        for kt in range(2):
                            last = nc.tensor.matmul(hs[u][r][:], xt[:, u, kt, :], w[:, r, kt, :],
                                                    start=kt == 0, stop=kt == 1)
                    last.then_inc(h_made, 1)

                pe.wait_ge(w_made, DIRS * 4)
                turn(0, 0)
                turn(1, 1)
                product(0, 0)
                with pe.Fori(1, FULL // 2) as i:
                    for u in range(2):
                        turn(i * 2 + u, u)
                        product(i * 2 + (u - 1), (u + 1) % 2)
                turn(FULL, 0)
                product(FULL - 1, 1)
                product(FULL, 0)


def edge_sums(nc, s, k, table):
    J = PACK
    R = 8
    STEPS = N_ITEMS // J
    assert N_ITEMS % (J * R) == 0
    with Scope(nc, "edges") as t:
        rows = t.sb("rows", [P, R, J, ROW], F32)
        idx = t.sb("idx", [P, R, J], I32)
        hot = t.sb("hot", [P, R, J, P], F32)
        hot_t = t.sb("hot_t", [P, 2, J, P], BF16)
        logit = t.sb("logit", [P, 2, J, 2 * HEADS], F32)
        z = t.sb("z_edge", [P, 2, J, HEADS], F32)
        lz = t.sb("lz", [P, 2, J, HEADS], F32)
        turned = [t.ps(f"turned_hot{i}", [P, J, P]) for i in range(2)]
        found = [t.ps(f"found{i}", [P, J, 2 * HEADS, 3]) for i in range(2)]
        sums = [t.ps(f"sums{j}", [P, ROW]) for j in range(J)]

        idx_made, pool_gate = t.sem("idx_made"), t.sem("pool_gate")
        gathered = [t.sem(f"gathered{i}") for i in range(R)]
        hot_made, turned_made, turned_read = t.sem("hot_made"), t.sem("hot_turned"), t.sem("hot_kept")
        found_made, found_read = t.sem("found_made"), t.sem("found_read")
        z_made, p_made, weighed = t.sem("z_made"), t.sem("p_made"), t.sem("weighed")
        summed, added = t.sem("summed"), t.sem("added")
        logit_made, leaky_made = t.sem("logit_made"), t.sem("leaky_made")

        with nc.Block() as block:

            def loop(eng, step):
                for n in range(R):
                    step(n, n, 0)
                with eng.Fori(1, STEPS // R - 1) as i:
                    for u in range(R):
                        step(i * R + u, u, i)
                for n in range(STEPS - R, STEPS):
                    step(n, n % R, n // R)

            def comes(n):
                return not isinstance(n, int) or n < STEPS

            def item_accs(eng, n):
                return eng.value_load(k.item_acc[0:1, bass.ds(n, 1)], min_val=0,
                                      max_val=(1 << PACK * ACC_BITS) - 1)

            def item_acc(accs, j):
                return nc.s_assert_within(
                    accs >> j * ACC_BITS & (1 << ACC_BITS) - 1, 0, DIRS * NB - 1,
                    skip_runtime_bounds_check_because="sort_edges keeps every number below DIRS * NB")

            @block.gpsimd
            def _(pool):
                def step(n, u, i):
                    pool.wait_ge(idx_made, n + 1)
                    after(pool, summed, (n - (R - 1)) * J)
                    pool.sem_inc(pool_gate, 1)
                    for j in range(J):
                        nc.gpsimd.indirect_dma_start(
                            out=rows[:, u, j, :], out_offset=None, in_=table,
                            in_offset=bass.IndirectOffsetOnAxis(ap=idx[:, u, j:j + 1], axis=0),
                        ).then_inc(gathered[u], 16)

                loop(pool, step)

            @block.scalar
            def _(act):
                def copy_idx(n, u):
                    nc.scalar.copy(idx[:, u, :], k.src_row[:, bass.ds(n * J, J)]).then_inc(idx_made, 1)

                def keep_turned(n, u):
                    act.wait_ge(turned_made, n + 1)
                    after(act, found_made, n - 1)
                    nc.scalar.copy(hot_t[:, u % 2], turned[u % 2][:]).then_inc(turned_read, 1)

                def weights(n, u):
                    act.wait_ge(z_made, n + 1)
                    nc.scalar.activation(rows[:, u % R, :, D:ROW], z[:, u % 2], ACT.Exp).then_inc(p_made, 1)

                def step(n, u, i):
                    if comes(n + 3):
                        keep_turned(n + 3, u + 3)
                    if comes(n + 2):
                        weights(n + 2, u + 2)
                    if comes(n + R):
                        copy_idx(n + R, u)

                for n in range(R):
                    copy_idx(n, n)
                for n in range(3):
                    keep_turned(n, n)
                for n in range(2):
                    weights(n, n)
                loop(act, step)

            @block.tensor
            def _(pe):
                def turn(n, u):
                    pe.wait_ge(hot_made, n + 1)
                    after(pe, turned_read, n - 1)
                    for j in range(J):
                        last = nc.tensor.transpose(turned[u % 2][:, j, :], hot[:, u % R, j, :], k.ident[:])
                    last.then_inc(turned_made, 1)

                def look_up(n, u):
                    pe.wait_ge(turned_read, n + 1)
                    after(pe, found_read, n - 1)
                    accs = item_accs(pe, n)
                    for j in range(J):
                        acc = item_acc(accs, j)
                        last = nc.tensor.matmul(found[u % 2][:, j].rearrange("p v t -> p (v t)"), hot_t[:, u % 2, j, :],
                                                k.pieces[:, bass.ds(acc, 1), :, :].rearrange(
                                                    "p o v t -> p (o v t)"), start=True, stop=True)
                    last.then_inc(found_made, 1)

                def step(n, u, i):
                    if comes(n + 3):
                        turn(n + 3, u + 3)
                    if comes(n + 2):
                        look_up(n + 2, u + 2)
                    for j in range(J):
                        pe.wait_ge(weighed, n * J + (j + 1))
                        after(pe, added, n * J + (j + 1 - J))
                        nc.tensor.matmul(sums[j][:], hot[:, u % R, j, :], rows[:, u, j, :], start=True,
                                         stop=True).then_inc(summed, 1)

                turn(0, 0)
                turn(1, 1)
                look_up(0, 0)
                turn(2, 2)
                look_up(1, 1)
                loop(pe, step)

            @block.vector
            def _(dve):
                v = nc.vector

                def make_hot(n, u):
                    v.tensor_tensor(hot[:, u % R], k.row_bf[:].unsqueeze(1).to_broadcast([P, J, P]),
                                    k.target[:, bass.ds(n * J, J)].unsqueeze(2).to_broadcast([P, J, P]),
                                    ALU.is_equal).then_inc(hot_made, 1)

                def find_logits(n, u):
                    dve.wait_ge(found_made, n + 1)
                    v.tensor_reduce(logit[:, u % 2].rearrange("p j v -> p (j v)"), found[u % 2][:].rearrange(
                        "p j v t -> p (j v) t"), AX.X, ALU.add).then_inc(found_read, 1)

                def add_source(n, u, i):
                    dve.wait_ge(found_read, n + 1)
                    dve.wait_ge(gathered[u % R], i * (16 * J) + 16 * J * (1 + u // R))
                    v.tensor_tensor(z[:, u % 2], rows[:, u % R, :, D:ROW], logit[:, u % 2, :, 0:HEADS],
                                    ALU.add).then_inc(logit_made, 1)

                def make_leaky(n, u):
                    dve.wait_ge(logit_made, n + 1)
                    leaky(v, lz[:, u % 2], z[:, u % 2]).then_inc(leaky_made, 1)

                def less_bound(n, u):
                    dve.wait_ge(leaky_made, n + 1)
                    v.tensor_tensor(z[:, u % 2], lz[:, u % 2], logit[:, u % 2, :, HEADS:],
                                    ALU.subtract).then_inc(z_made, 1)

                def weigh(n, u, j):
                    if j == 0:
                        dve.wait_ge(p_made, n + 1)
                    h = rows[:, u % R, j, 0:D].rearrange("p (h c) -> p h c", h=HEADS)
                    weight = rows[:, u % R, j, D:ROW].unsqueeze(2).to_broadcast([P, HEADS, C])
                    v.tensor_tensor(h, h, weight, ALU.mult).then_inc(weighed, 1)

                def step(n, u, i):
                    between = [(lambda: find_logits(n + 2, u + 2)), (lambda: add_source(n + 2, u + 2, i)),
                               (lambda: make_leaky(n + 2, u + 2)), (lambda: less_bound(n + 2, u + 2))]
                    accs = item_accs(dve, n)
                    for j in range(J):
                        dve.wait_ge(summed, n * J + (j + 1))
                        after(dve, added, n * J + j)
                        a = k.acc[:, bass.ds(item_acc(accs, j), 1), :].rearrange("p o n -> p (o n)")
                        v.tensor_tensor(a, a, sums[j][:], ALU.add).then_inc(added, 1)
                        if comes(n + 2):
                            between[j]()
                        if comes(n + 1):
                            weigh(n + 1, u + 1, j)
                    if comes(n + 5):
                        make_hot(n + 5, u + 5)

                for n in range(5):
                    make_hot(n, n)
                for n in range(2):
                    find_logits(n, n)
                    add_source(n, n, 0)
                    make_leaky(n, n)
                    less_bound(n, n)
                for j in range(J):
                    weigh(0, 0, j)
                loop(dve, step)


def combine(nc, s, k, x, gnn_bias, router_w, router_b, bias2):
    k.route = s.sb("route", [P, NB, EXPERTS], F32)
    FULL = NB - 1
    with Scope(nc, "mix") as t:
        u_all = t.sb("u_all", [P, NB, D], F32)
        bias = t.sb("bias", [P, DIRS, D], F32)
        wr = t.sb("wr", [P, 2, EXPERTS], F32)
        br = t.sb("br", [P, EXPERTS], F32)
        b2 = t.sb("b2", [EXPERTS, D], F32)
        stats = t.sb("stats", [P, 2, NB, 6], F32)
        mean = t.sb("mean", [P, 2, NB], F32)
        tmp = t.sb("tmp", [P, 2, NB], F32)
        std = t.sb("std", [P, 2, NB], F32)
        rstd = t.sb("rstd", [P, 2, NB], F32)
        inv = k.acc[:, :, D:ROW]
        xn = t.sb("xn2", [P, 2, D], F32)
        un = t.sb("un", [P, 2, D], F32)
        routed = t.sb("routed", [P, 2, EXPERTS], F32)
        ut = t.sb("ut", [P, 2, 2, P], F32)
        lg = t.sb("lg", [P, NB, EXPERTS], F32)
        lower = k.route
        first = t.sb("first", [P, NB, EXPERTS], F32)
        second = t.sb("second", [P, NB, EXPERTS], F32)
        top = t.sb("top", [P, NB], F32)
        top2 = t.sb("top2", [P, NB], F32)
        at1 = t.sb("at1", [P, NB], F32)
        wt = t.sb("wt", [EXPERTS, 2, P], F32)
        turned = [t.ps(f"turned_u{i}", [P, 2, P]) for i in range(2)]
        turned_n = [t.ps(f"turned_n{i}", [P, 2, P]) for i in range(2)]
        scores = [t.ps(f"scores{i}", [P, EXPERTS]) for i in range(2)]
        plus = [t.ps(f"plus{i}", [P, D]) for i in range(2)]

        x_landed, small_landed = t.sem("x2_landed"), t.sem("small_landed")
        tail_landed = t.sem("tail_landed")
        pad_cleared = t.sem("pad_cleared2")
        mix = t.sem("mix_steps")
        stats_made, var_made, std_made = t.sem("stats2_made"), t.sem("var2_made"), t.sem("std2_made")
        normed, turned_made, turned_read = t.sem("normed2"), t.sem("turned2_made"), t.sem("turned2_read")
        kept, scored, scores_read = t.sem("kept"), t.sem("scored"), t.sem("scores_read")
        diff_made, exp_made, route_made = t.sem("diff_made"), t.sem("exp_made"), t.sem("route_made")
        routed_made = t.sem("routed_made")
        wt_made, wt_read, plus_made, plus_read = t.sem("wt_made"), t.sem("wt_read"), t.sem("plus_made"), t.sem("plus_read")

        def over_tiles(eng, step):
            for n in range(2):
                step(n, n)
            with eng.Fori(1, FULL // 2) as i:
                for u in range(2):
                    step(i * 2 + u, u)
            step(FULL, 0)

        def tile(a, n):
            return a[:, bass.ds(n, 1), 0:D].rearrange("p o n -> p (o n)")

        with nc.Block() as block:

            @block.sync
            def _(sp):
                sp.dma_start(u_all[:, 0:FULL, :], x[0:FULL * P, :].rearrange(
                    "(b p) n -> p b n", p=P)).then_inc(x_landed, 16)
                sp.wait_ge(pad_cleared, 1)
                sp.dma_start(u_all[0:TAIL, FULL, :], x[FULL * P:N_NODES, :]).then_inc(tail_landed, 16)
                for r in range(DIRS):
                    sp.dma_start(bias[:, r, :], gnn_bias[r].rearrange("(o n) -> o n", o=1).to_broadcast(
                        [P, D])).then_inc(small_landed, 16)
                sp.dma_start(wr[:], router_w.rearrange("(k p) e -> p k e", p=P)).then_inc(small_landed, 16)
                sp.dma_start(br[:], router_b.rearrange("(o n) -> o n", o=1).to_broadcast(
                    [P, EXPERTS])).then_inc(small_landed, 16)
                sp.dma_start(b2[:], bias2).then_inc(small_landed, 16)

            @block.vector
            def _(dve):
                v = nc.vector
                steps = Count(mix, dve)
                v.memset(u_all[:, FULL, :], 0.0).then_inc(pad_cleared, 1)
                steps.link(v.reciprocal(inv, inv))
                steps.link(v.tensor_scalar(inv, inv, 0.5, None, ALU.mult))
                for r in range(DIRS):
                    at = slice(r * NB, (r + 1) * NB)
                    h = k.acc[:, at, 0:D].rearrange("p b (h c) -> p b h c", h=HEADS)
                    steps.link(v.tensor_tensor(h, h, inv[:, at, :].unsqueeze(3).to_broadcast([P, NB, HEADS, C]),
                                               ALU.mult))
                x2 = k.acc[:, 0:NB, 0:D]
                steps.link(v.tensor_tensor(x2, x2, k.acc[:, NB:, 0:D], ALU.add))
                dve.wait_ge(small_landed, 16 * (DIRS + 3))
                steps.link(v.tensor_tensor(bias[:, 0, :], bias[:, 0, :], bias[:, 1, :], ALU.add))
                steps.link(v.tensor_scalar(bias[:, 0, :], bias[:, 0, :], 0.5, None, ALU.mult))
                steps.link(v.tensor_tensor(x2, x2, bias[:, 0:1, :].to_broadcast([P, NB, D]), ALU.add))
                dve.wait_ge(x_landed, 16)
                dve.wait_ge(tail_landed, 16)
                steps.link(v.tensor_tensor(x2, x2, u_all[:], ALU.add))

                with dve.Fori(0, NB) as i:
                    v.bn_stats(stats[:, 0, bass.ds(i, 1), :].rearrange("p o n -> p (o n)"),
                               tile(k.acc, i)).then_inc(stats_made, 1)
                dve.wait_ge(stats_made, NB)
                moments(nc, steps, stats[:, 0], mean[:, 0], tmp[:, 0]).then_inc(var_made, 1)
                dve.wait_ge(std_made, 1)
                steps.link(v.reciprocal(rstd[:, 0], std[:, 0]))
                with dve.Fori(0, NB) as i:
                    v.tensor_scalar(tile(u_all, i), tile(k.acc, i), mean[:, 0, bass.ds(i, 1)],
                                    rstd[:, 0, bass.ds(i, 1)], ALU.subtract, ALU.mult).then_inc(stats_made, 1)
                dve.wait_ge(stats_made, 2 * NB)
                with dve.Fori(0, NB) as i:
                    v.bn_stats(stats[:, 1, bass.ds(i, 1), :].rearrange("p o n -> p (o n)"),
                               tile(u_all, i)).then_inc(stats_made, 1)
                dve.wait_ge(stats_made, 3 * NB)
                moments(nc, steps, stats[:, 1], mean[:, 1], tmp[:, 1]).then_inc(var_made, 1)
                dve.wait_ge(std_made, 2)
                steps.link(v.reciprocal(rstd[:, 1], std[:, 1]))

                def step(n, u):
                    after(dve, turned_made, n - 1)
                    v.tensor_copy(un[:, u], tile(u_all, n))
                    v.tensor_scalar(xn[:, u], tile(u_all, n), mean[:, 1, bass.ds(n, 1)],
                                    rstd[:, 1, bass.ds(n, 1)], ALU.subtract, ALU.mult).then_inc(normed, 1)
                    dve.wait_ge(scored, n + 1)
                    v.tensor_tensor(lg[:, bass.ds(n, 1), :].rearrange("p o n -> p (o n)"), scores[u][:], br[:],
                                    ALU.add).then_inc(scores_read, 1)

                over_tiles(dve, step)
                dve.wait_ge(scores_read, NB)

                wide = [P, NB, EXPERTS]
                number = k.rowf[:, 0:EXPERTS].unsqueeze(1).to_broadcast(wide)

                def pick(of, best, out):
                    steps.link(v.tensor_reduce(best[:], of[:], AX.X, ALU.max))
                    steps.link(v.tensor_tensor(out[:], of[:], best[:].unsqueeze(2).to_broadcast(wide), ALU.is_lt))
                    steps.link(v.scalar_tensor_tensor(out=out[:], in0=out[:], scalar=float(P), in1=number,
                                                      op0=ALU.mult, op1=ALU.add))
                    steps.link(v.tensor_reduce(at1[:], out[:], AX.X, ALU.min))
                    steps.link(v.tensor_tensor(out[:], at1[:].unsqueeze(2).to_broadcast(wide), number,
                                               ALU.is_equal))

                pick(lg, top, first)
                steps.link(v.scalar_tensor_tensor(out=lower[:], in0=first[:], scalar=-1e30, in1=lg[:],
                                                  op0=ALU.mult, op1=ALU.add))
                pick(lower, top2, second)
                v.tensor_tensor(lg[:], lg[:], top[:].unsqueeze(2).to_broadcast(wide),
                                ALU.subtract).then_inc(diff_made, 1)
                steps.link(v.tensor_tensor(first[:], first[:], second[:], ALU.add))
                dve.wait_ge(exp_made, 1)
                steps.link(v.tensor_tensor(first[:], first[:], lg[:], ALU.mult))
                steps.link(v.tensor_reduce(top[:], first[:], AX.X, ALU.add))
                steps.link(v.reciprocal(top2[:], top[:]))
                v.tensor_tensor(k.route[:], first[:], top2[:].unsqueeze(2).to_broadcast(wide),
                                ALU.mult).then_inc(route_made, 1)

                def add_bias(n, u):
                    dve.wait_ge(plus_made, n + 1)
                    v.tensor_tensor(tile(k.acc, n), tile(k.acc, n), plus[u][:], ALU.add).then_inc(plus_read, 1)

                over_tiles(dve, add_bias)

            @block.scalar
            def _(act):
                for y in range(2):
                    act.wait_ge(var_made, y + 1)
                    nc.scalar.activation(std[:, y], tmp[:, y], ACT.Sqrt).then_inc(std_made, 1)

                def step(n, u):
                    act.wait_ge(turned_made, n + 1)
                    after(act, scored, n - 1)
                    nc.scalar.copy(ut[:, u], turned[u][:]).then_inc(turned_read, 1)
                    nc.scalar.copy(tile(k.acc, n + NB), turned_n[u][:].rearrange("p k n -> p (k n)")).then_inc(kept, 1)

                over_tiles(act, step)
                act.wait_ge(diff_made, 1)
                nc.scalar.activation(lg[:], lg[:], ACT.Exp).then_inc(exp_made, 1)

                act.wait_ge(route_made, 1)

                def keep_wt(n, u):
                    after(act, wt_made, n - 1)
                    nc.scalar.copy(routed[:, u, :], k.route[:, bass.ds(n, 1), :].rearrange(
                        "p o e -> p (o e)")).then_inc(routed_made, 1)
                    act.wait_ge(wt_made, n + 1)
                    after(act, plus_made, n - 1)
                    nc.scalar.copy(wt[:, u, :], turned[u][0:EXPERTS, 0, :]).then_inc(wt_read, 1)

                over_tiles(act, keep_wt)

            @block.tensor
            def _(pe):
                pe.wait_ge(small_landed, 16 * (DIRS + 3))

                def step(n, u):
                    pe.wait_ge(normed, n + 1)
                    after(pe, kept, n - 1)
                    for kt in range(2):
                        nc.tensor.transpose(turned[u][:, kt, :], un[:, u, kt * P:(kt + 1) * P], k.ident[:])
                    for kt in range(2):
                        last = nc.tensor.transpose(turned_n[u][:, kt, :], xn[:, u, kt * P:(kt + 1) * P], k.ident[:])
                    last.then_inc(turned_made, 1)
                    pe.wait_ge(turned_read, n + 1)
                    after(pe, scores_read, n - 1)
                    for kt in range(2):
                        last = nc.tensor.matmul(scores[u][:], ut[:, u, kt, :], wr[:, kt, :], start=kt == 0,
                                                stop=kt == 1)
                    last.then_inc(scored, 1)

                over_tiles(pe, step)
                def bias_term(n, u):
                    pe.wait_ge(routed_made, n + 1)
                    after(pe, wt_read, n - 1)
                    nc.tensor.transpose(turned[u][0:EXPERTS, 0, :], routed[:, u, :], k.ident[:]).then_inc(wt_made, 1)
                    pe.wait_ge(wt_read, n + 1)
                    after(pe, plus_read, n - 1)
                    nc.tensor.matmul(plus[u][:], wt[:, u, :], b2[:], start=True, stop=True).then_inc(plus_made, 1)

                pe.wait_ge(kept, NB)
                over_tiles(pe, bias_term)


def experts(nc, s, k, ln_g, ln_b, w1, b1, w2, out):
    HB = HID // P
    GT = 4
    GROUPS = NB // GT
    PER = GROUPS + 1
    FULL = NB - 1
    NH = 4
    with Scope(nc, "ffn") as t:
        w1s = [t.sb(f"w1_{i}", [P, 2, HID], F32) for i in range(2)]
        w2s = [t.sb(f"w2_{i}", [P, HB, D], F32) for i in range(2)]
        hid = t.sb("hid", [P, HB, GT * P], F32)
        lg = t.sb("ln_g_sb", [P, EXPERTS, 2], F32)
        lb = t.sb("ln_b_sb", [P, EXPERTS, 2], F32)
        b1s = t.sb("b1_sb", [P, EXPERTS, HB], F32)
        bias = t.sb("hid_bias", [P, 2, HB], F32)
        hps = [t.ps(f"hps{i}", [P, GT * P]) for i in range(NH)]
        yps = [t.ps(f"yps{i}", [P, D]) for i in range(2)]
        bps = t.ps("bps", [P, HB])

        w1_landed = [t.sem(f"w1_landed{i}") for i in range(2)]
        w2_landed = [t.sem(f"w2_landed{i}") for i in range(2)]
        small_landed = t.sem("ffn_small_landed")
        bias_made, bias_ready = t.sem("bias_made"), t.sem("bias_ready")
        h_made, pe_gate = t.sem("hid_made"), t.sem("pe_gate")
        y_made1 = t.sem("y_made1")
        h_kept, y_added = t.sem("h_kept_and_free"), t.sem("y_added_and_free")
        out_written = t.sem("out_written")

        with nc.Block() as block:

            def over_groups(eng, e, group):
                with eng.Fori(0, GROUPS) as g:
                    group(g * GT, GT, e * (PER * HB) + g * HB, e * NB + g * GT)
                group(FULL, 1, e * (PER * HB) + GROUPS * HB, e * NB + FULL)

            def over_experts(eng, expert):
                with eng.Fori(0, EXPERTS // 2) as i:
                    for u in range(2):
                        expert(i * 2 + u, u, i)

            @block.sync
            def _(sp):
                sp.dma_start(lg[:], ln_g).then_inc(small_landed, 16)
                sp.dma_start(lb[:], ln_b).then_inc(small_landed, 16)
                sp.dma_start(b1s[:], b1).then_inc(small_landed, 16)

                def load(e, u):
                    sp.dma_start(w1s[u][:], w1[bass.ds(e, 1), :, :].rearrange(
                        "o (k p) n -> p (o k) n", p=P)).then_inc(w1_landed[u], 16)
                    sp.dma_start(w2s[u][:], w2[bass.ds(e, 1), :, :].rearrange(
                        "o (k p) n -> p (o k) n", p=P)).then_inc(w2_landed[u], 16)

                for u in range(2):
                    load(u, u)
                with sp.Fori(1, EXPERTS // 2) as i:
                    for u in range(2):
                        sp.wait_ge(y_made1, (i * 2 + (u - 1)) * NB + 1)
                        load(i * 2 + u, u)
                sp.wait_ge(y_added, EXPERTS * NB + 2)
                sp.dma_start(out[0:FULL * P, :].rearrange("(b p) n -> p b n", p=P),
                             k.acc[:, 0:FULL, 0:D]).then_inc(out_written, 16)
                sp.dma_start(out[FULL * P:N_NODES, :], k.acc[0:TAIL, FULL, 0:D]).then_inc(out_written, 16)
                sp.wait_ge(out_written, 32)

            @block.tensor
            def _(pe):
                mm = nc.tensor.matmul
                pe.sem_inc(y_made1, 1)
                pe.wait_ge(small_landed, 48)

                def expert(e, u, i):
                    pe.wait_ge(w1_landed[u], i * 16 + 16)
                    for hb in range(HB):
                        for kt in range(2):
                            last = mm(bps[:, hb:hb + 1], w1s[u][:, kt, hb * P:(hb + 1) * P],
                                      lb[:, bass.ds(e, 1), kt:kt + 1].rearrange("p o k -> p (o k)"),
                                      start=kt == 0, stop=kt == 1)
                    last.then_inc(bias_made, 1)
                    pe.wait_ge(bias_ready, e + 1)
                    pe.wait_ge(w2_landed[u], i * 16 + 16)
                    pe.sem_inc(pe_gate, 1)

                    def group(tile0, tiles, h0, t0):
                        for hb in range(HB):
                            pe.wait_ge(h_kept, h0 + (hb + 1))
                            for kt in range(2):
                                last = mm(hps[hb % NH][:, 0:tiles * P].rearrange("p (b n) -> p b n", b=tiles),
                                          w1s[u][:, kt, hb * P:(hb + 1) * P],
                                          k.acc[:, bass.ds(tile0 + NB, tiles), kt * P:(kt + 1) * P],
                                          start=kt == 0, stop=kt == 1)
                            last.then_inc(h_made, 1)
                        for b in range(tiles):
                            pe.wait_ge(y_added, t0 + (b + (2 if b == 0 else 1)))
                            for hb in range(HB):
                                if b == 0:
                                    pe.wait_ge(h_kept, h0 + (hb + 1 + NH))
                                last = mm(yps[b % 2][:], hid[:, hb, b * P:(b + 1) * P], w2s[u][:, hb, :],
                                          start=hb == 0, stop=hb == HB - 1)
                            last.then_inc(y_made1, 1)

                    over_groups(pe, e, group)

                over_experts(pe, expert)

            @block.scalar
            def _(act):
                act.sem_inc(h_kept, NH)

                def expert(e, u, i):
                    act.wait_ge(bias_ready, e + 1)

                    def group(tile0, tiles, h0, t0):
                        for hb in range(HB):
                            act.wait_ge(h_made, h0 + (hb + 1))
                            if hb == 0:
                                act.wait_ge(y_made1, t0 + 1)
                            nc.scalar.activation(hid[:, hb, 0:tiles * P], hps[hb % NH][:, 0:tiles * P], ACT.Gelu,
                                                 bias=bias[:, u, hb:hb + 1]).then_inc(h_kept, 1)

                    over_groups(act, e, group)

                over_experts(act, expert)

            @block.vector
            def _(dve):
                v = nc.vector
                dve.sem_inc(y_added, 2)

                def expert(e, u, i):
                    dve.wait_ge(bias_made, e + 1)
                    v.tensor_tensor(bias[:, u, :], bps[:], b1s[:, bass.ds(e, 1), :].rearrange("p o h -> p (o h)"),
                                    ALU.add)
                    for kt in range(2):
                        last = v.tensor_scalar(w1s[u][:, kt, :], w1s[u][:, kt, :],
                                               lg[:, bass.ds(e, 1), kt:kt + 1].rearrange("p o k -> p (o k)"),
                                               None, ALU.mult)
                    last.then_inc(bias_ready, 1)

                    def group(tile0, tiles, h0, t0):
                        for b in range(tiles):
                            dve.wait_ge(y_made1, t0 + (b + 2))
                            x2 = k.acc[:, bass.ds(tile0 + b, 1), 0:D].rearrange("p o n -> p (o n)")
                            part = k.route[:, bass.ds(tile0 + b, 1), bass.ds(e, 1)].rearrange("p o e -> p (o e)")
                            v.scalar_tensor_tensor(out=x2, in0=yps[b % 2][:], scalar=part, in1=x2,
                                                   op0=ALU.mult, op1=ALU.add).then_inc(y_added, 1)

                    over_groups(dve, e, group)

                over_experts(dve, expert)


def build_program(nc, a, out):
    table = nc.dram_tensor("h_table", [DIRS * NPAD, ROW], F32, kind="Internal").ap()
    k = Kept()
    with Scope(nc, "all") as s:
        make_constants(nc, s, k)
        sort_edges(nc, s, k, a["edges"])
        weights = [[a[f"L0_gnn_{w}{r + 1}"] for w in ("W", "a_src", "a_dst")] for r in range(DIRS)]
        node_tables(nc, s, k, a["x"], weights, table)
        edge_sums(nc, s, k, table)
        combine(nc, s, k, a["x"], [a["L0_gnn_b1"], a["L0_gnn_b2"]], a["L0_ffn_Wr"], a["L0_ffn_br"],
                a["L0_ffn_b2"])
        experts(nc, s, k, a["L0_ffn_ln_g"], a["L0_ffn_ln_b"], a["L0_ffn_W1"], a["L0_ffn_b1"],
                a["L0_ffn_W2"], out)


def kernel(**inputs):
    import numpy as np
    import concourse.bacc as bacc
    from concourse.bass_utils import run_bass_kernel_spmd

    nc = bacc.Bacc("TRN2", target_bir_lowering=False, num_devices=1)
    host = {name: np.ascontiguousarray(a) for name, a in inputs.items() if name not in ("src", "dst")}
    host["edges"] = np.stack([np.asarray(inputs["src"]), np.asarray(inputs["dst"])])
    for name in ("L0_ffn_ln_g", "L0_ffn_ln_b", "L0_ffn_b1"):
        host[name] = np.ascontiguousarray(host[name].reshape(EXPERTS, -1, P).transpose(2, 0, 1))
    arrays, aps = {}, {}
    for name, a in host.items():
        arrays[f"in_{name}"] = a
        aps[name] = nc.dram_tensor(f"in_{name}", a.shape, mybir.dt.from_np(a.dtype), kind="ExternalInput").ap()
    out = nc.dram_tensor("out", [N_NODES, D], F32, kind="ExternalOutput").ap()
    build_program(nc, aps, out)
    result = run_bass_kernel_spmd(nc, [arrays], core_ids=[0])
    return result.results[0]["out"]
```

```python
from contextlib import ExitStack

import concourse.bass as bass
from concourse import mybir

F32 = mybir.dt.float32
BF16 = mybir.dt.bfloat16
F16 = mybir.dt.float16
I32 = mybir.dt.int32
ALU = mybir.AluOpType
ACT = mybir.ActivationFunctionType
AX = mybir.AxisListType

P = 128
N_NODES = 6250
D = 256
HEADS = 4
C = D // HEADS
ROW = D + HEADS
N_EDGES = 200000
EXPERTS = 8
HID = 1024
EPS = 1e-5
SLOPE = 0.2

TOP = 2
NB = -(-N_NODES // P)
TAIL = N_NODES - (NB - 1) * P
NPAD = NB * P
DIRS = 2

EP = 125
ECOLS = N_EDGES // EP
CHUNKS = 4
CC = ECOLS // CHUNKS
GC = 5
NG = CC // GC
ITEMS = -(-(EP * CC + NB * (P - 1)) // P)
ITEMS += -ITEMS % 8
N_ITEMS = DIRS * CHUNKS * ITEMS
PACK = 4
ACC_BITS = 7
assert DIRS * NB <= 1 << ACC_BITS
TILE_BITS = 9
TILE = 1 << TILE_BITS
TILES = (TOP * NPAD + EXPERTS * (TILE - 1)) // TILE
SUB = TILE // P
assert EP * ECOLS == N_EDGES and GC * NG == CC and NG <= P and ITEMS <= 512


class Kept:
    pass


class Count:

    def __init__(self, sem, eng):
        self.sem, self.eng, self.n = sem, eng, 0

    def mark(self, ins):
        ins.then_inc(self.sem, 1)
        self.n = self.n + 1

    def link(self, ins):
        self.mark(ins)
        self.eng.wait_ge(self.sem, self.n)


def after(eng, sem, value):
    if not isinstance(value, int) or value > 0:
        eng.wait_ge(sem, value)


class Scope(ExitStack):

    def __init__(self, nc, stage):
        super().__init__()
        self.nc, self.stage = nc, stage

    def sb(self, name, shape, dt):
        return self.enter_context(self.nc.sbuf_tensor(f"{self.stage}_{name}", shape, dt))

    def ps(self, name, shape, dt=F32):
        return self.enter_context(self.nc.psum_tensor(f"{self.stage}_{name}", shape, dt))

    def sem(self, name):
        return self.enter_context(self.nc.semaphore(f"{self.stage}_{name}"))


def make_constants(nc, s, k):
    k.row16 = s.sb("row16", [P, 512], F16)
    k.rowf = s.sb("rowf", [P, P], F32)
    k.colf = s.sb("colf", [P, 1], F32)
    k.row_bf = s.sb("row_bf", [P, P], BF16)
    k.ident = s.sb("ident", [P, P], F32)
    k.ident_bf = s.sb("ident_bf", [P, P], BF16)
    k.below = s.sb("below", [P, P], F32)
    k.upto = s.sb("upto", [P, P], F32)
    k.below_items = s.sb("below_items", [P, P], F32)
    k.below_bf = s.sb("below_bf", [P, P], BF16)
    k.ones = s.sb("ones", [P, P], F32)
    k.ones_bf = s.sb("ones_bf", [P, P], BF16)
    iota_done = s.sem("iota_done")
    const_done = s.sem("const_done")
    with Scope(nc, "const") as t, nc.Block() as block:
        row_i = t.sb("row_i", [P, 512], I32)
        col_i = t.sb("col_i", [P, 1], I32)

        @block.gpsimd
        def _(pool):
            nc.gpsimd.iota(row_i[:], [[1, 512]], base=0, channel_multiplier=0).then_inc(iota_done, 1)
            nc.gpsimd.iota(col_i[:], [[0, 1]], base=0, channel_multiplier=1).then_inc(iota_done, 1)

        @block.vector
        def _(dve):
            dve.wait_ge(iota_done, 2)
            nc.vector.tensor_copy(k.row16[:], row_i[:])
            nc.vector.tensor_copy(k.row_bf[:], row_i[:, 0:P])
            nc.vector.memset(k.ones[:], 1.0)
            nc.vector.memset(k.ones_bf[:], 1.0)
            nc.vector.tensor_copy(k.colf[:], col_i[:]).then_inc(const_done, 1)
            nc.vector.tensor_copy(k.rowf[:], row_i[:, 0:P]).then_inc(const_done, 1)
            dve.wait_ge(const_done, 2)
            for out, op in ((k.ident, ALU.is_equal), (k.ident_bf, ALU.is_equal), (k.below, ALU.is_gt),
                            (k.below_bf, ALU.is_gt), (k.upto, ALU.is_ge)):
                nc.vector.tensor_scalar(out[:], k.rowf[:], k.colf[:], None, op)
            nc.vector.tensor_scalar(k.below_items[:], k.rowf[:], k.colf[:], float(P), ALU.is_gt, ALU.mult)


def sort_edges(nc, s, k, edges, slot_rows):
    k.src_row = s.sb("src_row", [P, N_ITEMS], I32)
    k.target = s.sb("target", [P, N_ITEMS], BF16)
    k.item_acc = s.sb("item_acc", [1, N_ITEMS // PACK], I32)
    BLOCKS = CC // (2 * GC)
    RING = GC
    BY_DVE = 2
    BY_ACT = RING - BY_DVE
    with Scope(nc, "sort") as t:
        zeros = t.sb("zeros", [P, TILES * TILE * D // P // 8], F32)
        tgt = t.sb("tgt", [EP, CC], I32)
        src = t.sb("src", [EP, CC], I32)
        bucket_i = t.sb("bucket_i", [EP, CC], I32)
        local_i = t.sb("local_i", [EP, CC], I32)
        src_hi = t.sb("src_hi", [EP, CC], I32)
        src_lo = t.sb("src_lo", [EP, CC], I32)
        bucket = t.sb("bucket", [EP, CC], BF16)
        local_1 = t.sb("local_1", [EP, CC], F32)
        load = t.sb("load", [EP, 2, CC, 2], F16)
        in_bucket = [t.sb(f"in_bucket{i}", [EP, CC, NB], BF16) for i in range(2)]
        window = t.sb("window", [EP, 2 * NG - 1], BF16)
        totals = t.sb("totals", [NG, NB], F32)
        filled = t.sb("filled", [NB, P], I32)
        items_i = t.sb("items_i", [NB, P], I32)
        items = t.sb("items", [NB, P], F32)
        ends = t.sb("ends", [NB, 1], F32)
        base_i = t.sb("base_i", [NG, NB], I32)
        base_hi_i = t.sb("base_hi_i", [NG, NB], I32)
        base_lo_i = t.sb("base_lo_i", [NG, NB], I32)
        base_hi = t.sb("base_hi", [NG, NB], F32)
        base_lo = t.sb("base_lo", [NG, NB], F32)
        diag_hi = t.sb("diag_hi", [NG, NG, NB], BF16)
        diag_lo = t.sb("diag_lo", [NG, NG, NB], BF16)
        past_end = t.sb("past_end", [NB, ITEMS], BF16)
        chosen = t.sb("chosen", [EP, 2, 2 * GC, NB], F32)
        slot = t.sb("slot", [EP, CC], F32)
        slot_i = t.sb("slot_i", [EP, CC], I32)
        item_i = t.sb("item_i", [EP, CC], I32)
        part_i = t.sb("part_i", [EP, CC], I32)
        item_f = t.sb("item_f", [EP, CC], F32)
        part_f = t.sb("part_f", [EP, CC], F32)
        half_less = t.sb("half_less", [EP, CC], F32)
        put_load = t.sb("put_load", [EP, RING, P], F32)
        put_item = t.sb("put_item", [EP, RING, ITEMS], F16)
        signed = t.sb("signed", [P, 2, ITEMS + 1], F32)
        moved = t.sb("moved", [P, 2, ITEMS], F32)
        moved_i = t.sb("moved_i", [P, ITEMS], I32)
        moved_lo = t.sb("moved_lo", [P, ITEMS], I32)
        moved_hi = t.sb("moved_hi", [P, ITEMS], I32)
        src_f = t.sb("src_f", [P, ITEMS], F32)
        acc_f = t.sb("acc_f", [1, ITEMS // PACK, PACK], F32)
        acc_pair = t.sb("acc_pair", [1, ITEMS // PACK, PACK // 2], I32)

        small = t.ps("small", [P, 512])
        bucket_tot = small[0:NB, 64:64 + P]
        group_base, bucket_end = small[0:NG, 256:256 + NB], small[0:NB, 448:450]
        rank = [t.ps(f"rank{i}", [EP, 2 * GC, NB]) for i in range(2)]
        got = [t.ps(f"got{h}", [P, ITEMS]) for h in range(2)]
        got_signed = [t.ps(f"got_signed{h}", [P, ITEMS]) for h in range(2)]
        bucket_row = t.ps("bucket_row", [P, ITEMS])
        column_tot = bucket_row[0:NG, 0:GC * NB].rearrange("p (c b) -> p c b", c=GC)

        zeros_made, slots_cleared = t.sem("zeros_made"), t.sem("slots_cleared")
        tgt_landed, src_landed = t.sem("tgt_landed"), t.sem("src_landed")
        ids_used = t.sem("ids_used")
        sort_steps = t.sem("sort_steps")
        hot_made = t.sem("hot_made")
        totals_made, totals_read = t.sem("totals_made"), t.sem("totals_read")
        fill_made, items_made = t.sem("fill_made"), t.sem("items_made")
        base_made, ends_read, diag_made = t.sem("base_made"), t.sem("ends_read"), t.sem("diag_made")
        buckets_made = t.sem("buckets_made")
        rank_made, rank_read = t.sem("rank_made"), t.sem("rank_read")
        slots_picked = t.sem("slots_picked")
        slots_ready, signs_made = t.sem("slots_ready"), t.sem("signs_made")
        puts_made, puts_used = t.sem("puts_made"), t.sem("puts_used")

        with nc.Block() as block:

            @block.sync
            def _(sp):
                for n in range(DIRS * CHUNKS):
                    r, q = divmod(n, CHUNKS)
                    by = [edges[x, :].rearrange("(p c) -> p c", p=EP) for x in (1 - r, r)]
                    if n:
                        sp.wait_ge(ids_used, n)
                    sp.dma_start(tgt[:], by[0][:, q * CC:(q + 1) * CC]).then_inc(tgt_landed, 16)
                    sp.dma_start(src[:], by[1][:, q * CC:(q + 1) * CC]).then_inc(src_landed, 16)
                    sp.wait_ge(zeros_made, 1)
                    cleared = slot_rows[n * (TILES * TILE // 8):(n + 1) * (TILES * TILE // 8), :]
                    sp.dma_start(cleared.rearrange("(p r) n -> p (r n)", p=P), zeros[:]).then_inc(slots_cleared, 16)
                sp.wait_ge(slots_cleared, 16 * DIRS * CHUNKS)

            @block.vector
            def _(dve):
                v = nc.vector
                steps = Count(sort_steps, dve)
                v.memset(zeros[:], 0.0).then_inc(zeros_made, 1)
                steps.link(v.memset(window[:], 0.0))
                steps.link(v.memset(window[:, NG - 1:NG], 1.0))

                def split_ids(n):
                    dve.wait_ge(tgt_landed, 16 * (n + 1))
                    dve.wait_ge(src_landed, 16 * (n + 1))
                    v.tensor_scalar(bucket_i[:], tgt[:], 7, None, ALU.arith_shift_right)
                    v.tensor_scalar(local_i[:], tgt[:], P - 1, None, ALU.bitwise_and)
                    v.tensor_scalar(src_hi[:], src[:], 10, None, ALU.arith_shift_right)
                    v.tensor_scalar(src_lo[:], src[:], 1023, None, ALU.bitwise_and).then_inc(ids_used, 1)
                    dve.wait_ge(ids_used, n + 1)
                    v.tensor_scalar(local_1[:], local_i[:], 1.0, None, ALU.add)
                    v.tensor_copy(load[:, n % 2, :, 0:1], src_lo[:].unsqueeze(2))
                    steps.link(v.tensor_copy(bucket[:], bucket_i[:]))
                    v.scalar_tensor_tensor(out=load[:, n % 2, :, 1:2], in0=src_hi[:].unsqueeze(2), scalar=256.0,
                                           in1=local_1[:].unsqueeze(2), op0=ALU.mult, op1=ALU.add)
                    v.tensor_tensor(in_bucket[n % 2][:], bucket[:].unsqueeze(2).to_broadcast([EP, CC, NB]),
                                    k.row_bf[0:EP, 0:NB].unsqueeze(1).to_broadcast([EP, CC, NB]),
                                    ALU.is_equal).then_inc(hot_made, 1)

                def place_buckets(n):
                    dve.wait_ge(totals_made, n + 1)
                    v.tensor_reduce(totals[:], column_tot.rearrange("p c b -> p b c"), AX.X,
                                    ALU.add).then_inc(totals_read, 1)
                    dve.wait_ge(fill_made, n + 1)
                    steps.link(v.tensor_scalar(filled[:], bucket_tot, float(P - 1), None, ALU.add))
                    steps.link(v.tensor_scalar(items_i[:], filled[:], 7, None, ALU.arith_shift_right))
                    v.tensor_copy(items[:], items_i[:]).then_inc(items_made, 1)
                    dve.wait_ge(base_made, n + 1)
                    v.tensor_copy(ends[:], bucket_end[:, 0:1])
                    steps.link(v.tensor_copy(base_i[:], group_base))
                    v.tensor_scalar(past_end[:], k.row16[0:NB, 0:ITEMS], ends[:], None,
                                    ALU.is_ge).then_inc(ends_read, 1)
                    v.tensor_scalar(base_hi_i[:], base_i[:], 0x1FF00, None, ALU.bitwise_and)
                    steps.link(v.tensor_scalar(base_lo_i[:], base_i[:], 255, None, ALU.bitwise_and))
                    v.tensor_copy(base_hi[:], base_hi_i[:])
                    steps.link(v.tensor_copy(base_lo[:], base_lo_i[:]))
                    for diag, of in ((diag_hi, base_hi), (diag_lo, base_lo)):
                        last = v.tensor_tensor(diag[:], of[:].unsqueeze(1).to_broadcast([NG, NG, NB]),
                                               k.ident[0:NG, 0:NG].unsqueeze(2).to_broadcast([NG, NG, NB]),
                                               ALU.mult)
                    last.then_inc(diag_made, 1)
                    dve.wait_ge(buckets_made, n + 1)
                    steps.link(v.tensor_scalar(acc_f[:].rearrange("o i p -> o (i p)"), bucket_row[0:1, :],
                                               float(NB - 1), float(n // CHUNKS * NB), ALU.min, ALU.add))
                    for h in range(2):
                        last = v.scalar_tensor_tensor(
                            out=acc_pair[:, :, h:h + 1], in0=acc_f[:, :, 2 * h + 1:2 * h + 2],
                            scalar=float(1 << ACC_BITS), in1=acc_f[:, :, 2 * h:2 * h + 1], op0=ALU.mult, op1=ALU.add)
                    steps.link(last)
                    steps.link(v.tensor_scalar(acc_pair[:, :, 1:2], acc_pair[:, :, 1:2], 2 * ACC_BITS, None,
                                               ALU.logical_shift_left))
                    v.tensor_tensor(k.item_acc[0:1, n * (ITEMS // PACK):(n + 1) * (ITEMS // PACK)].rearrange(
                        "o (i p) -> o i p", p=1), acc_pair[:, :, 0:1], acc_pair[:, :, 1:2], ALU.bitwise_or)

                def pick_slots(n):
                    def pair(i):
                        for u in range(2):
                            dve.wait_ge(rank_made, i * 2 + (n * BLOCKS + u + 1))
                            v.tensor_tensor(chosen[:, u], rank[u][:],
                                            in_bucket[n % 2][:, bass.ds(i * (4 * GC) + u * 2 * GC, 2 * GC), :],
                                            ALU.mult).then_inc(rank_read, 1)
                        dve.wait_ge(rank_read, i * 2 + (n * BLOCKS + 2))
                        v.tensor_reduce(slot[:, bass.ds(i * (4 * GC), 4 * GC)],
                                        chosen[:].rearrange("p u c b -> p (u c) b"), AX.X,
                                        ALU.add).then_inc(slots_picked, 1)

                    pair(0)
                    with dve.Fori(1, BLOCKS // 2) as i:
                        dve.wait_ge(slots_picked, i + n * (BLOCKS // 2))
                        pair(i)
                    dve.wait_ge(slots_picked, (n + 1) * (BLOCKS // 2))
                    steps.link(v.tensor_copy(slot_i[:], slot[:]))
                    v.tensor_scalar(item_i[:], slot_i[:], 7, None, ALU.arith_shift_right)
                    steps.link(v.tensor_scalar(part_i[:], slot_i[:], P - 1, None, ALU.bitwise_and))
                    steps.link(v.tensor_copy(item_f[:], item_i[:]))
                    v.tensor_scalar(half_less[:], item_f[:], -1.0, 0.5, ALU.mult, ALU.add)
                    steps.link(v.tensor_copy(part_f[:], part_i[:]))
                    dve.sem_inc(slots_ready, 1)

                def put_columns(n):
                    words = load[:, n % 2].rearrange("p c h -> p (c h)").bitcast(F32)

                    def columns(i):
                        for u in range(RING):
                            c = i * RING + u
                            after(dve, puts_used, c + (n * CC - RING + 1))
                            last = v.tensor_scalar(put_load[:, u], k.row16[0:EP, 0:P], part_f[:, bass.ds(c, 1)],
                                                   words[:, bass.ds(c, 1)], ALU.is_equal, ALU.mult)
                            if u < BY_DVE:
                                last = v.tensor_scalar(put_item[:, u], k.row16[0:EP, 0:ITEMS],
                                                       item_f[:, bass.ds(c, 1)], None, ALU.is_equal)
                            last.then_inc(puts_made, 1)

                    columns(0)
                    with dve.Fori(1, NG) as i:
                        columns(i)

                def unpack_items(n):
                    at = slice(n * ITEMS, (n + 1) * ITEMS)
                    dve.wait_ge(puts_used, (n + 1) * CC)
                    for h in range(2):
                        v.tensor_scalar(signed[:, h, 0:1], got_signed[h][:, ITEMS - 1:ITEMS], -1.0, None, ALU.mult)
                        last = v.tensor_copy(signed[:, h, 1:], got_signed[h][:])
                    steps.link(last)
                    steps.link(v.tensor_tensor(moved[:], signed[:, :, 1:], signed[:, :, 0:ITEMS], ALU.subtract))
                    for h in range(2):
                        last = v.scalar_tensor_tensor(out=moved[:, h], in0=moved[:, h], scalar=0.5, in1=got[h][:],
                                                      op0=ALU.mult, op1=ALU.add)
                    steps.link(last)
                    steps.link(v.tensor_copy(moved_i[:], moved[:, 1]))
                    v.tensor_scalar(moved_lo[:], moved_i[:], 255, None, ALU.bitwise_and)
                    steps.link(v.tensor_scalar(moved_hi[:], moved_i[:], 8, None, ALU.arith_shift_right))
                    v.tensor_scalar(k.target[:, at], moved_lo[:], -1.0, None, ALU.add)
                    steps.link(v.scalar_tensor_tensor(out=src_f[:], in0=moved_hi[:], scalar=1024.0,
                                                      in1=moved[:, 0], op0=ALU.mult, op1=ALU.add))
                    v.tensor_scalar(k.src_row[:, at], src_f[:], float(n // CHUNKS * NPAD), None, ALU.add)

                split_ids(0)
                for n in range(DIRS * CHUNKS):
                    place_buckets(n)
                    pick_slots(n)
                    if n + 1 < DIRS * CHUNKS:
                        split_ids(n + 1)
                    put_columns(n)
                    unpack_items(n)

            @block.scalar
            def _(act):
                for n in range(DIRS * CHUNKS):

                    def columns(i):
                        for u in range(BY_DVE, RING):
                            c = i * RING + u
                            after(act, puts_used, c + (n * CC - RING + 1))
                            nc.scalar.activation(put_item[:, u], k.row16[0:EP, 0:ITEMS], ACT.Sign,
                                                 bias=half_less[:, bass.ds(c, 1)]).then_inc(signs_made, 1)

                    act.wait_ge(slots_ready, n + 1)
                    columns(0)
                    with act.Fori(1, NG) as i:
                        columns(i)

            @block.tensor
            def _(pe):
                mm = nc.tensor.matmul

                def count_group(n, g, first=False, last=False):
                    return mm(column_tot, window[:, bass.ds(g * -1 + (NG - 1), NG)],
                              in_bucket[n % 2][:, bass.ds(g * GC, GC), :], start=first, stop=last)

                def count_groups(n):
                    pe.wait_ge(hot_made, n + 1)
                    count_group(n, 0, first=True)
                    with pe.Fori(1, NG - 1) as g:
                        count_group(n, g)
                    count_group(n, NG - 1, last=True).then_inc(totals_made, 1)

                def bases(n):
                    pe.wait_ge(totals_read, n + 1)
                    mm(bucket_tot, totals[:], k.ones[0:NG, :], start=True, stop=True).then_inc(fill_made, 1)
                    pe.wait_ge(items_made, n + 1)
                    mm(group_base, k.below[0:NG, 0:NG], totals[:], start=True, stop=False)
                    mm(group_base, items[:, 0:NG], k.below_items[0:NB, 0:NB], start=False, stop=True)
                    mm(bucket_end, k.upto[0:NB, 0:NB], items[:, 0:2], start=True,
                       stop=True).then_inc(base_made, 1)
                    pe.wait_ge(ends_read, n + 1)
                    mm(bucket_row[0:1, :], k.ones_bf[0:NB, 0:1], past_end[:], start=True,
                       stop=True).then_inc(buckets_made, 1)
                    pe.wait_ge(diag_made, n + 1)

                def rank_block(n, i, u):
                    c0 = i * (4 * GC) + u * 2 * GC
                    mm(rank[u][:], k.below_bf[0:EP, 0:EP], in_bucket[n % 2][:, bass.ds(c0, 2 * GC), :], start=True,
                       stop=False)
                    for h in range(2):
                        for c in range(GC - 1):
                            more = GC - 1 - c
                            mm(rank[u][:, h * GC + c + 1:(h + 1) * GC, :], k.ones_bf[0:EP, 0:EP],
                               in_bucket[n % 2][:, bass.ds(c0 + (h * GC + c), 1), :].to_broadcast([EP, more, NB]),
                               start=False, stop=False)
                        for diag in (diag_hi, diag_lo):
                            last = mm(rank[u][:, h * GC:(h + 1) * GC, :], k.ones_bf[0:NG, 0:EP],
                                      diag[:, bass.ds(i * 4 + (u * 2 + h), 1), :].to_broadcast([NG, GC, NB]),
                                      start=False, stop=h == 1 and diag is diag_lo)
                    last.then_inc(rank_made, 1)

                def ranks(n):
                    for u in range(2):
                        rank_block(n, 0, u)
                    with pe.Fori(1, BLOCKS // 2) as i:
                        for u in range(2):
                            pe.wait_ge(rank_read, i * 2 + (n * BLOCKS + u - 1))
                            rank_block(n, i, u)

                def move_columns(n, i, first=False, last=False):
                    for u in range(RING):
                        pe.wait_ge(puts_made, i * RING + (n * CC + u + 1))
                        signs, to = u >= BY_DVE, got_signed if u >= BY_DVE else got
                        if signs:
                            pe.wait_ge(signs_made, i * BY_ACT + (n * NG * BY_ACT + u - BY_DVE + 1))
                        halves = put_load[:, u].bitcast(F16).rearrange("p (m h) -> p h m", h=2)
                        for h in range(2):
                            ins = mm(to[h][:], halves[:, h], put_item[:, u],
                                     start=first and u in (0, BY_DVE), stop=last and u in (BY_DVE - 1, RING - 1))
                        ins.then_inc(puts_used, 1)
                    if n + 1 < DIRS * CHUNKS:
                        if first:
                            pe.wait_ge(hot_made, n + 2)
                        ins = count_group(n + 1, i, first=first, last=last)
                        if last:
                            ins.then_inc(totals_made, 1)

                count_groups(0)
                for n in range(DIRS * CHUNKS):
                    bases(n)
                    ranks(n)
                    move_columns(n, 0, first=True)
                    with pe.Fori(1, NG - 1) as i:
                        move_columns(n, i)
                    move_columns(n, NG - 1, last=True)


def leaky(v, out, x):
    return v.scalar_tensor_tensor(out=out, in0=x, scalar=SLOPE, in1=x, op0=ALU.mult, op1=ALU.max)


def moments(nc, steps, stats, mean, tmp):
    v = nc.vector
    v.tensor_tensor(mean, stats[:, :, 1], stats[:, :, 4], ALU.add)
    steps.link(v.tensor_tensor(tmp, stats[:, :, 1], stats[:, :, 4], ALU.subtract))
    v.tensor_scalar(mean, mean, 0.5, None, ALU.mult)
    steps.link(v.scalar_tensor_tensor(out=tmp, in0=tmp, scalar=D / 4, in1=tmp, op0=ALU.mult, op1=ALU.mult))
    steps.link(v.tensor_tensor(tmp, tmp, stats[:, :, 2], ALU.add))
    steps.link(v.tensor_tensor(tmp, tmp, stats[:, :, 5], ALU.add))
    return v.tensor_scalar(tmp, tmp, 1.0 / D, EPS, ALU.mult, ALU.add)


def node_tables(nc, s, k, x, weights, table):
    k.acc = s.sb("acc", [P, DIRS * NB, ROW], F32)
    k.pieces = s.sb("pieces", [P, DIRS * NB, 2 * HEADS, 3], BF16)
    WIDE = ROW + HEADS
    with Scope(nc, "nodes") as t:
        xs = k.acc[:, 0:NB, 0:D]
        w = t.sb("w", [P, DIRS, 2, WIDE], F32)
        a = t.sb("a", [P, DIRS, 2, D], F32)
        prod = t.sb("prod", [P, D], F32)
        stats = t.sb("stats", [P, NB, 6], F32)
        mean = t.sb("mean", [P, NB], F32)
        tmp = t.sb("tmp", [P, NB], F32)
        std = t.sb("std", [P, NB], F32)
        rstd = t.sb("rstd", [P, NB], F32)
        xn = t.sb("xn", [P, 2, D], F32)
        xt = t.sb("xt", [P, 2, 2, P], F32)
        logit_t = t.sb("logit_t", [P, DIRS * NB, HEADS], F32)
        tops = t.sb("tops", [P, DIRS, HEADS], F32)
        bound0 = t.sb("bound0", [P, DIRS, HEADS], F32)
        z = t.sb("z", [P, DIRS * NB, HEADS], F32)
        bound = t.sb("bound", [P, DIRS * NB, HEADS], F32)
        turned = [t.ps(f"turned{i}", [P, 2, P]) for i in range(2)]
        hs = [[t.ps(f"hs{i}{r}", [P, WIDE]) for r in range(DIRS)] for i in range(2)]

        XG = 7
        x_landed = [t.sem(f"x_landed{i}") for i in range(NB // XG + 1)]
        w_landed, a_landed = t.sem("w_landed"), t.sem("a_landed")
        node_steps = t.sem("node_steps")
        stats_made = t.sem("stats_made")
        var_made, std_made = t.sem("var_made"), t.sem("std_made")
        normed, turned_made, turned_read = t.sem("normed"), t.sem("turned_made"), t.sem("turned_read")
        h_made, h0_read, h1_read = t.sem("h_made"), t.sem("h0_read"), t.sem("h1_read")
        w_made, table_written = t.sem("w_made"), t.sem("table_written")
        tops_made, bound_made = t.sem("tops_made"), t.sem("bound_made")
        z_made, p_made, acc_started = t.sem("z_made"), t.sem("p_made"), t.sem("acc_started")
        pad_cleared = t.sem("pad_cleared")
        FULL = NB - 1

        with nc.Block() as block:

            @block.sync
            def _(sp):
                for r in range(DIRS):
                    sp.dma_start(w[:, r, :, 0:D], weights[r][0].rearrange("(k p) n -> p k n", p=P)).then_inc(w_landed, 16)
                    for y in range(2):
                        row = weights[r][1 + y].rearrange("(o h) c -> o (h c)", o=1)
                        sp.dma_start(a[:, r, y, :], row.to_broadcast([P, D])).then_inc(a_landed, 16)
                for i in range(NB // XG + 1):
                    if i * XG < FULL:
                        end = min((i + 1) * XG, FULL)
                        sp.dma_start(xs[:, i * XG:end, :], x[i * XG * P:end * P, :].rearrange(
                            "(b p) n -> p b n", p=P)).then_inc(x_landed[i], 16)
                sp.wait_ge(pad_cleared, 1)
                sp.dma_start(xs[0:TAIL, FULL, :], x[FULL * P:N_NODES, :]).then_inc(x_landed[NB // XG], 16)
                for r in range(DIRS):
                    sp.wait_ge((h0_read, h1_read)[r], NB)
                    sp.dma_start(table[r * NPAD:(r + 1) * NPAD, :].rearrange("(b p) n -> p b n", p=P),
                                 k.acc[:, r * NB:(r + 1) * NB, :]).then_inc(table_written, 16)
                sp.wait_ge(table_written, 16 * DIRS)

            @block.gpsimd
            def _(pool):
                pool.wait_ge(tops_made, 1)
                nc.gpsimd.partition_all_reduce(bound0[:].rearrange("p r h -> p (r h)"),
                                               tops[:].rearrange("p r h -> p (r h)"), P,
                                               bass.bass_isa.ReduceOp.max).then_inc(bound_made, 1)

            @block.vector
            def _(dve):
                v = nc.vector
                steps = Count(node_steps, dve)
                v.memset(xs[:, FULL, :], 0.0).then_inc(pad_cleared, 1)
                dve.wait_ge(w_landed, 16 * DIRS)
                dve.wait_ge(a_landed, 16 * 2 * DIRS)
                for r in range(DIRS):
                    for kt in range(2):
                        for y in range(2):
                            steps.link(v.tensor_tensor(prod[:], w[:, r, kt, 0:D], a[:, r, y, :], ALU.mult))
                            v.tensor_reduce(w[:, r, kt, D + y * HEADS:D + (y + 1) * HEADS],
                                            prod[:].rearrange("p (h c) -> p h c", h=HEADS),
                                            AX.X, ALU.add).then_inc(w_made, 1)
                            dve.wait_ge(w_made, (r * 2 + kt) * 2 + y + 1)
                for i in range(NB // XG + 1):
                    dve.wait_ge(x_landed[i], 16)
                with dve.Fori(0, NB) as i:
                    v.bn_stats(stats[:, bass.ds(i, 1), :].rearrange("p o n -> p (o n)"),
                               xs[:, bass.ds(i, 1), :].rearrange("p o n -> p (o n)")).then_inc(stats_made, 1)
                dve.wait_ge(stats_made, NB)
                moments(nc, steps, stats, mean[:], tmp[:]).then_inc(var_made, 1)
                dve.wait_ge(std_made, 1)
                steps.link(v.reciprocal(rstd[:], std[:]))

                def normalise(m, u):
                    after(dve, turned_made, m - 1)
                    v.tensor_scalar(xn[:, u], xs[:, bass.ds(m, 1), :].rearrange("p o n -> p (o n)"),
                                    mean[:, bass.ds(m, 1)], rstd[:, bass.ds(m, 1)],
                                    ALU.subtract, ALU.mult).then_inc(normed, 1)

                def keep_h0(m, u):
                    dve.wait_ge(h_made, m + 1)
                    v.tensor_copy(logit_t[:, bass.ds(m, 1), :].rearrange("p o h -> p (o h)"),
                                  hs[u][0][:, ROW:WIDE])
                    v.tensor_copy(k.acc[:, bass.ds(m, 1), :].rearrange("p o n -> p (o n)"),
                                  hs[u][0][:, 0:ROW]).then_inc(h0_read, 1)

                normalise(0, 0)
                normalise(1, 1)
                keep_h0(0, 0)
                with dve.Fori(1, FULL // 2) as i:
                    for u in range(2):
                        normalise(i * 2 + u, u)
                        keep_h0(i * 2 + (u - 1), (u + 1) % 2)
                normalise(FULL, 0)
                keep_h0(FULL - 1, 1)
                keep_h0(FULL, 0)
                dve.wait_ge(h0_read, NB)
                dve.wait_ge(h1_read, NB)
                for r in range(DIRS):
                    last = v.tensor_reduce(tops[:, r, :], k.acc[:, r * NB:r * NB + FULL, D:ROW].rearrange(
                        "p b h -> p h b"), AX.X, ALU.max)
                steps.link(last)
                for r in range(DIRS):
                    last = v.tensor_tensor(tops[0:TAIL, r, :], tops[0:TAIL, r, :],
                                           k.acc[0:TAIL, r * NB + FULL, D:ROW], ALU.max)
                last.then_inc(tops_made, 1)
                dve.wait_ge(bound_made, 1)
                for r in range(DIRS):
                    at = slice(r * NB, (r + 1) * NB)
                    last = v.tensor_tensor(bound[:, at, :], logit_t[:, at, :],
                                           bound0[:, r:r + 1, :].to_broadcast([P, NB, HEADS]), ALU.add)
                steps.link(v.tensor_tensor(z[:], logit_t[:], k.acc[:, :, D:ROW], ALU.add))
                leaky(v, bound[:], bound[:])
                steps.link(leaky(v, z[:], z[:]))
                v.tensor_tensor(z[:], z[:], bound[:], ALU.subtract).then_inc(z_made, 1)
                for y, of in enumerate((logit_t, bound)):
                    for piece in range(3):
                        part = k.pieces[:, :, y * HEADS:(y + 1) * HEADS, piece]
                        steps.link(v.tensor_copy(part, of[:]))
                        if piece < 2:
                            steps.link(v.tensor_tensor(of[:], of[:], part, ALU.subtract))
                dve.wait_ge(p_made, 1)
                dve.wait_ge(table_written, 16 * DIRS)
                for r in range(DIRS):
                    at = slice(r * NB, (r + 1) * NB)
                    h = k.acc[:, at, 0:D].rearrange("p b (h c) -> p b h c", h=HEADS)
                    v.tensor_tensor(h, h, z[:, at, :].unsqueeze(3).to_broadcast([P, NB, HEADS, C]), ALU.mult)
                v.tensor_copy(k.acc[:, :, D:ROW], z[:])

            @block.scalar
            def _(act):
                act.wait_ge(var_made, 1)
                nc.scalar.activation(std[:], tmp[:], ACT.Sqrt).then_inc(std_made, 1)

                def keep_h1(m, u):
                    act.wait_ge(h_made, m + 1)
                    nc.scalar.copy(logit_t[:, bass.ds(m + NB, 1), :].rearrange("p o h -> p (o h)"),
                                   hs[u][1][:, ROW:WIDE])
                    nc.scalar.copy(k.acc[:, bass.ds(m + NB, 1), :].rearrange("p o n -> p (o n)"),
                                   hs[u][1][:, 0:ROW]).then_inc(h1_read, 1)

                def keep_turned(m, u):
                    act.wait_ge(turned_made, m + 1)
                    after(act, h_made, m - 1)
                    nc.scalar.copy(xt[:, u], turned[u][:]).then_inc(turned_read, 1)

                keep_turned(0, 0)
                keep_turned(1, 1)
                keep_h1(0, 0)
                with act.Fori(1, FULL // 2) as i:
                    for u in range(2):
                        keep_turned(i * 2 + u, u)
                        keep_h1(i * 2 + (u - 1), (u + 1) % 2)
                keep_turned(FULL, 0)
                keep_h1(FULL - 1, 1)
                keep_h1(FULL, 0)
                act.wait_ge(z_made, 1)
                nc.scalar.activation(z[:], z[:], ACT.Exp).then_inc(p_made, 1)

            @block.tensor
            def _(pe):
                def turn(m, u):
                    pe.wait_ge(normed, m + 1)
                    after(pe, turned_read, m - 1)
                    for kt in range(2):
                        last = nc.tensor.transpose(turned[u][:, kt, :], xn[:, u, kt * P:(kt + 1) * P],
                                                   k.ident[:])
                    last.then_inc(turned_made, 1)

                def product(m, u):
                    pe.wait_ge(turned_read, m + 1)
                    after(pe, h0_read, m - 1)
                    after(pe, h1_read, m - 1)
                    for r in range(DIRS):
                        for kt in range(2):
                            last = nc.tensor.matmul(hs[u][r][:], xt[:, u, kt, :], w[:, r, kt, :],
                                                    start=kt == 0, stop=kt == 1)
                    last.then_inc(h_made, 1)

                pe.wait_ge(w_made, DIRS * 4)
                turn(0, 0)
                turn(1, 1)
                product(0, 0)
                with pe.Fori(1, FULL // 2) as i:
                    for u in range(2):
                        turn(i * 2 + u, u)
                        product(i * 2 + (u - 1), (u + 1) % 2)
                turn(FULL, 0)
                product(FULL - 1, 1)
                product(FULL, 0)


def edge_sums(nc, s, k, table):
    J = PACK
    R = 8
    STEPS = N_ITEMS // J
    assert N_ITEMS % (J * R) == 0
    with Scope(nc, "edges") as t:
        rows = t.sb("rows", [P, R, J, ROW], F32)
        idx = t.sb("idx", [P, R, J], I32)
        hot = t.sb("hot", [P, R, J, P], F32)
        hot_t = t.sb("hot_t", [P, 2, J, P], BF16)
        logit = t.sb("logit", [P, 2, J, 2 * HEADS], F32)
        z = t.sb("z_edge", [P, 2, J, HEADS], F32)
        lz = t.sb("lz", [P, 2, J, HEADS], F32)
        turned = [t.ps(f"turned_hot{i}", [P, J, P]) for i in range(2)]
        found = [t.ps(f"found{i}", [P, J, 2 * HEADS, 3]) for i in range(2)]
        sums = [t.ps(f"sums{j}", [P, ROW]) for j in range(J)]

        idx_made, pool_gate = t.sem("idx_made"), t.sem("pool_gate")
        gathered = [t.sem(f"gathered{i}") for i in range(R)]
        hot_made, turned_made, turned_read = t.sem("hot_made"), t.sem("hot_turned"), t.sem("hot_kept")
        found_made, found_read = t.sem("found_made"), t.sem("found_read")
        z_made, p_made, weighed = t.sem("z_made"), t.sem("p_made"), t.sem("weighed")
        summed, added = t.sem("summed"), t.sem("added")
        logit_made, leaky_made = t.sem("logit_made"), t.sem("leaky_made")

        with nc.Block() as block:

            def loop(eng, step):
                for n in range(R):
                    step(n, n, 0)
                with eng.Fori(1, STEPS // R - 1) as i:
                    for u in range(R):
                        step(i * R + u, u, i)
                for n in range(STEPS - R, STEPS):
                    step(n, n % R, n // R)

            def comes(n):
                return not isinstance(n, int) or n < STEPS

            def item_accs(eng, n):
                return eng.value_load(k.item_acc[0:1, bass.ds(n, 1)], min_val=0,
                                      max_val=(1 << PACK * ACC_BITS) - 1)

            def item_acc(accs, j):
                return nc.s_assert_within(
                    accs >> j * ACC_BITS & (1 << ACC_BITS) - 1, 0, DIRS * NB - 1,
                    skip_runtime_bounds_check_because="sort_edges keeps every number below DIRS * NB")

            @block.gpsimd
            def _(pool):
                def step(n, u, i):
                    pool.wait_ge(idx_made, n + 1)
                    after(pool, summed, (n - (R - 1)) * J)
                    pool.sem_inc(pool_gate, 1)
                    for j in range(J):
                        nc.gpsimd.indirect_dma_start(
                            out=rows[:, u, j, :], out_offset=None, in_=table,
                            in_offset=bass.IndirectOffsetOnAxis(ap=idx[:, u, j:j + 1], axis=0),
                        ).then_inc(gathered[u], 16)

                loop(pool, step)

            @block.scalar
            def _(act):
                def copy_idx(n, u):
                    nc.scalar.copy(idx[:, u, :], k.src_row[:, bass.ds(n * J, J)]).then_inc(idx_made, 1)

                def keep_turned(n, u):
                    act.wait_ge(turned_made, n + 1)
                    after(act, found_made, n - 1)
                    nc.scalar.copy(hot_t[:, u % 2], turned[u % 2][:]).then_inc(turned_read, 1)

                def weights(n, u):
                    act.wait_ge(z_made, n + 1)
                    nc.scalar.activation(rows[:, u % R, :, D:ROW], z[:, u % 2], ACT.Exp).then_inc(p_made, 1)

                def step(n, u, i):
                    if comes(n + 3):
                        keep_turned(n + 3, u + 3)
                    if comes(n + 2):
                        weights(n + 2, u + 2)
                    if comes(n + R):
                        copy_idx(n + R, u)

                for n in range(R):
                    copy_idx(n, n)
                for n in range(3):
                    keep_turned(n, n)
                for n in range(2):
                    weights(n, n)
                loop(act, step)

            @block.tensor
            def _(pe):
                def turn(n, u):
                    pe.wait_ge(hot_made, n + 1)
                    after(pe, turned_read, n - 1)
                    for j in range(J):
                        last = nc.tensor.transpose(turned[u % 2][:, j, :], hot[:, u % R, j, :], k.ident[:])
                    last.then_inc(turned_made, 1)

                def look_up(n, u):
                    pe.wait_ge(turned_read, n + 1)
                    after(pe, found_read, n - 1)
                    accs = item_accs(pe, n)
                    for j in range(J):
                        acc = item_acc(accs, j)
                        last = nc.tensor.matmul(found[u % 2][:, j].rearrange("p v t -> p (v t)"), hot_t[:, u % 2, j, :],
                                                k.pieces[:, bass.ds(acc, 1), :, :].rearrange(
                                                    "p o v t -> p (o v t)"), start=True, stop=True)
                    last.then_inc(found_made, 1)

                def step(n, u, i):
                    if comes(n + 3):
                        turn(n + 3, u + 3)
                    if comes(n + 2):
                        look_up(n + 2, u + 2)
                    for j in range(J):
                        pe.wait_ge(weighed, n * J + (j + 1))
                        after(pe, added, n * J + (j + 1 - J))
                        nc.tensor.matmul(sums[j][:], hot[:, u % R, j, :], rows[:, u, j, :], start=True,
                                         stop=True).then_inc(summed, 1)

                turn(0, 0)
                turn(1, 1)
                look_up(0, 0)
                turn(2, 2)
                look_up(1, 1)
                loop(pe, step)

            @block.vector
            def _(dve):
                v = nc.vector

                def make_hot(n, u):
                    v.tensor_tensor(hot[:, u % R], k.row_bf[:].unsqueeze(1).to_broadcast([P, J, P]),
                                    k.target[:, bass.ds(n * J, J)].unsqueeze(2).to_broadcast([P, J, P]),
                                    ALU.is_equal).then_inc(hot_made, 1)

                def find_logits(n, u):
                    dve.wait_ge(found_made, n + 1)
                    v.tensor_reduce(logit[:, u % 2].rearrange("p j v -> p (j v)"), found[u % 2][:].rearrange(
                        "p j v t -> p (j v) t"), AX.X, ALU.add).then_inc(found_read, 1)

                def add_source(n, u, i):
                    dve.wait_ge(found_read, n + 1)
                    dve.wait_ge(gathered[u % R], i * (16 * J) + 16 * J * (1 + u // R))
                    v.tensor_tensor(z[:, u % 2], rows[:, u % R, :, D:ROW], logit[:, u % 2, :, 0:HEADS],
                                    ALU.add).then_inc(logit_made, 1)

                def make_leaky(n, u):
                    dve.wait_ge(logit_made, n + 1)
                    leaky(v, lz[:, u % 2], z[:, u % 2]).then_inc(leaky_made, 1)

                def less_bound(n, u):
                    dve.wait_ge(leaky_made, n + 1)
                    v.tensor_tensor(z[:, u % 2], lz[:, u % 2], logit[:, u % 2, :, HEADS:],
                                    ALU.subtract).then_inc(z_made, 1)

                def weigh(n, u, j):
                    if j == 0:
                        dve.wait_ge(p_made, n + 1)
                    h = rows[:, u % R, j, 0:D].rearrange("p (h c) -> p h c", h=HEADS)
                    weight = rows[:, u % R, j, D:ROW].unsqueeze(2).to_broadcast([P, HEADS, C])
                    v.tensor_tensor(h, h, weight, ALU.mult).then_inc(weighed, 1)

                def step(n, u, i):
                    between = [(lambda: find_logits(n + 2, u + 2)), (lambda: add_source(n + 2, u + 2, i)),
                               (lambda: make_leaky(n + 2, u + 2)), (lambda: less_bound(n + 2, u + 2))]
                    accs = item_accs(dve, n)
                    for j in range(J):
                        dve.wait_ge(summed, n * J + (j + 1))
                        after(dve, added, n * J + j)
                        a = k.acc[:, bass.ds(item_acc(accs, j), 1), :].rearrange("p o n -> p (o n)")
                        v.tensor_tensor(a, a, sums[j][:], ALU.add).then_inc(added, 1)
                        if comes(n + 2):
                            between[j]()
                        if comes(n + 1):
                            weigh(n + 1, u + 1, j)
                    if comes(n + 5):
                        make_hot(n + 5, u + 5)

                for n in range(5):
                    make_hot(n, n)
                for n in range(2):
                    find_logits(n, n)
                    add_source(n, n, 0)
                    make_leaky(n, n)
                    less_bound(n, n)
                for j in range(J):
                    weigh(0, 0, j)
                loop(dve, step)


def combine(nc, s, k, x, gnn_bias, router_w, router_b, bias2):
    k.share = s.sb("share", [P, TOP, NB], F32)
    k.slot = s.sb("slot", [P, TOP * NB], I32)
    k.tile_expert = s.sb("tile_expert", [1, TILES], I32)
    FULL = NB - 1
    with Scope(nc, "mix") as t:
        u_all = t.sb("u_all", [P, NB, D], F32)
        bias = t.sb("bias", [P, DIRS, D], F32)
        wr = t.sb("wr", [P, 2, EXPERTS], F32)
        br = t.sb("br", [P, EXPERTS], F32)
        b2 = t.sb("b2", [EXPERTS, D], F32)
        stats = t.sb("stats", [P, 2, NB, 6], F32)
        mean = t.sb("mean", [P, 2, NB], F32)
        tmp = t.sb("tmp", [P, 2, NB], F32)
        std = t.sb("std", [P, 2, NB], F32)
        rstd = t.sb("rstd", [P, 2, NB], F32)
        inv = k.acc[:, :, D:ROW]
        un = t.sb("un", [P, 2, D], F32)
        routed = t.sb("routed", [P, 2, EXPERTS], F32)
        ut = t.sb("ut", [P, 2, 2, P], F32)
        lg = t.sb("lg", [P, NB, EXPERTS], F32)
        route = t.sb("route", [P, NB, EXPERTS], F32)
        lower = route
        both = t.sb("both", [P, NB, EXPERTS], F32)
        chosen = t.sb("chosen", [P, TOP, NB, EXPERTS], F32)
        first, second = chosen[:, 0], chosen[:, 1]
        spare = u_all[:].rearrange("p b n -> p (b n)")
        total, *upto = [spare[:, i * TOP * NB * EXPERTS:(i + 1) * TOP * NB * EXPERTS].rearrange(
            "p (b e) -> p b e", e=EXPERTS) for i in range(3)]
        count_i = t.sb("count_i", [P, EXPERTS], I32)
        tiles_i = t.sb("tiles_i", [P, EXPERTS], I32)
        tiles = t.sb("tiles", [P, EXPERTS], F32)
        ends = [t.sb(f"ends{i}", [P, EXPERTS], F32) for i in range(2)]
        start = t.sb("start", [P, EXPERTS], F32)
        past = t.sb("past", [1, TILES, EXPERTS], F32)
        owner = t.sb("owner", [1, TILES], F32)
        slot_f = t.sb("slot_f", [P, TOP * NB], F32)
        top = t.sb("top", [P, NB], F32)
        top2 = t.sb("top2", [P, NB], F32)
        at1 = t.sb("at1", [P, NB], F32)
        wt = t.sb("wt", [EXPERTS, 2, P], F32)
        turned = [t.ps(f"turned_u{i}", [P, 2, P]) for i in range(2)]
        counts = [t.ps(f"counts{i}", [P, NB, EXPERTS]) for i in range(TOP)]
        scores = [t.ps(f"scores{i}", [P, EXPERTS]) for i in range(2)]
        plus = [t.ps(f"plus{i}", [P, D]) for i in range(2)]

        x_landed, small_landed = t.sem("x2_landed"), t.sem("small_landed")
        tail_landed = t.sem("tail_landed")
        pad_cleared = t.sem("pad_cleared2")
        mix = t.sem("mix_steps")
        stats_made, var_made, std_made = t.sem("stats2_made"), t.sem("var2_made"), t.sem("std2_made")
        normed, turned_made, turned_read = t.sem("normed2"), t.sem("turned2_made"), t.sem("turned2_read")
        scored, scores_read = t.sem("scored"), t.sem("scores_read")
        chosen_made, counted, counts_read = t.sem("chosen_made"), t.sem("counted"), t.sem("counts_read")
        diff_made, exp_made, route_made = t.sem("diff_made"), t.sem("exp_made"), t.sem("route_made")
        routed_made = t.sem("routed_made")
        wt_made, wt_read, plus_made, plus_read = t.sem("wt_made"), t.sem("wt_read"), t.sem("plus_made"), t.sem("plus_read")

        def over_tiles(eng, step):
            for n in range(2):
                step(n, n)
            with eng.Fori(1, FULL // 2) as i:
                for u in range(2):
                    step(i * 2 + u, u)
            step(FULL, 0)

        def tile(a, n):
            return a[:, bass.ds(n, 1), 0:D].rearrange("p o n -> p (o n)")

        with nc.Block() as block:

            @block.sync
            def _(sp):
                sp.dma_start(u_all[:, 0:FULL, :], x[0:FULL * P, :].rearrange(
                    "(b p) n -> p b n", p=P)).then_inc(x_landed, 16)
                sp.wait_ge(pad_cleared, 1)
                sp.dma_start(u_all[0:TAIL, FULL, :], x[FULL * P:N_NODES, :]).then_inc(tail_landed, 16)
                for r in range(DIRS):
                    sp.dma_start(bias[:, r, :], gnn_bias[r].rearrange("(o n) -> o n", o=1).to_broadcast(
                        [P, D])).then_inc(small_landed, 16)
                sp.dma_start(wr[:], router_w.rearrange("(k p) e -> p k e", p=P)).then_inc(small_landed, 16)
                sp.dma_start(br[:], router_b.rearrange("(o n) -> o n", o=1).to_broadcast(
                    [P, EXPERTS])).then_inc(small_landed, 16)
                sp.dma_start(b2[:], bias2).then_inc(small_landed, 16)

            @block.vector
            def _(dve):
                v = nc.vector
                steps = Count(mix, dve)
                v.memset(u_all[:, FULL, :], 0.0).then_inc(pad_cleared, 1)
                steps.link(v.reciprocal(inv, inv))
                steps.link(v.tensor_scalar(inv, inv, 0.5, None, ALU.mult))
                for r in range(DIRS):
                    at = slice(r * NB, (r + 1) * NB)
                    h = k.acc[:, at, 0:D].rearrange("p b (h c) -> p b h c", h=HEADS)
                    steps.link(v.tensor_tensor(h, h, inv[:, at, :].unsqueeze(3).to_broadcast([P, NB, HEADS, C]),
                                               ALU.mult))
                x2 = k.acc[:, 0:NB, 0:D]
                steps.link(v.tensor_tensor(x2, x2, k.acc[:, NB:, 0:D], ALU.add))
                dve.wait_ge(small_landed, 16 * (DIRS + 3))
                steps.link(v.tensor_tensor(bias[:, 0, :], bias[:, 0, :], bias[:, 1, :], ALU.add))
                steps.link(v.tensor_scalar(bias[:, 0, :], bias[:, 0, :], 0.5, None, ALU.mult))
                steps.link(v.tensor_tensor(x2, x2, bias[:, 0:1, :].to_broadcast([P, NB, D]), ALU.add))
                dve.wait_ge(x_landed, 16)
                dve.wait_ge(tail_landed, 16)
                steps.link(v.tensor_tensor(x2, x2, u_all[:], ALU.add))

                with dve.Fori(0, NB) as i:
                    v.bn_stats(stats[:, 0, bass.ds(i, 1), :].rearrange("p o n -> p (o n)"),
                               tile(k.acc, i)).then_inc(stats_made, 1)
                dve.wait_ge(stats_made, NB)
                moments(nc, steps, stats[:, 0], mean[:, 0], tmp[:, 0]).then_inc(var_made, 1)
                dve.wait_ge(std_made, 1)
                steps.link(v.reciprocal(rstd[:, 0], std[:, 0]))
                with dve.Fori(0, NB) as i:
                    v.tensor_scalar(tile(u_all, i), tile(k.acc, i), mean[:, 0, bass.ds(i, 1)],
                                    rstd[:, 0, bass.ds(i, 1)], ALU.subtract, ALU.mult).then_inc(stats_made, 1)
                dve.wait_ge(stats_made, 2 * NB)
                with dve.Fori(0, NB) as i:
                    v.bn_stats(stats[:, 1, bass.ds(i, 1), :].rearrange("p o n -> p (o n)"),
                               tile(u_all, i)).then_inc(stats_made, 1)
                dve.wait_ge(stats_made, 3 * NB)
                moments(nc, steps, stats[:, 1], mean[:, 1], tmp[:, 1]).then_inc(var_made, 1)
                dve.wait_ge(std_made, 2)
                steps.link(v.reciprocal(rstd[:, 1], std[:, 1]))

                def step(n, u):
                    after(dve, turned_made, n - 1)
                    v.tensor_copy(un[:, u], tile(u_all, n))
                    v.tensor_scalar(tile(k.acc, n + NB), tile(u_all, n), mean[:, 1, bass.ds(n, 1)],
                                    rstd[:, 1, bass.ds(n, 1)], ALU.subtract, ALU.mult).then_inc(normed, 1)
                    dve.wait_ge(scored, n + 1)
                    v.tensor_tensor(lg[:, bass.ds(n, 1), :].rearrange("p o n -> p (o n)"), scores[u][:], br[:],
                                    ALU.add).then_inc(scores_read, 1)

                over_tiles(dve, step)
                dve.wait_ge(scores_read, NB)

                wide = [P, NB, EXPERTS]
                number = k.rowf[:, 0:EXPERTS].unsqueeze(1).to_broadcast(wide)

                def pick(of, best, out):
                    steps.link(v.tensor_reduce(best[:], of[:], AX.X, ALU.max))
                    steps.link(v.tensor_tensor(out, of[:], best[:].unsqueeze(2).to_broadcast(wide), ALU.is_lt))
                    steps.link(v.scalar_tensor_tensor(out=out, in0=out, scalar=float(P), in1=number,
                                                      op0=ALU.mult, op1=ALU.add))
                    steps.link(v.tensor_reduce(at1[:], out, AX.X, ALU.min))
                    steps.link(v.tensor_tensor(out, at1[:].unsqueeze(2).to_broadcast(wide), number,
                                               ALU.is_equal))

                pick(lg, top, first)
                steps.link(v.scalar_tensor_tensor(out=lower[:], in0=first, scalar=-1e30, in1=lg[:],
                                                  op0=ALU.mult, op1=ALU.add))
                pick(lower, top2, second)
                v.tensor_tensor(lg[:], lg[:], top[:].unsqueeze(2).to_broadcast(wide),
                                ALU.subtract).then_inc(diff_made, 1)
                v.tensor_tensor(both[:], first, second, ALU.add).then_inc(chosen_made, 1)
                dve.wait_ge(chosen_made, 1)
                dve.wait_ge(exp_made, 1)
                steps.link(v.tensor_tensor(both[:], both[:], lg[:], ALU.mult))
                steps.link(v.tensor_reduce(top[:], both[:], AX.X, ALU.add))
                steps.link(v.reciprocal(top2[:], top[:]))
                v.tensor_tensor(route[:], both[:], top2[:].unsqueeze(2).to_broadcast(wide),
                                ALU.mult).then_inc(route_made, 1)
                dve.wait_ge(route_made, 1)
                for y in range(TOP):
                    steps.link(v.tensor_tensor(both[:], route[:], chosen[:, y], ALU.mult))
                    steps.link(v.tensor_reduce(k.share[:, y, :], both[:], AX.X, ALU.add))

                dve.wait_ge(counted, 1)
                for y in range(TOP):
                    last = v.tensor_copy(total[:, y * NB:(y + 1) * NB, :], counts[y][:])
                last.then_inc(counts_read, 1)
                dve.wait_ge(counts_read, 1)
                of, n_cols, reach, turn = total, TOP * NB, 1, 0
                while reach < n_cols:
                    v.tensor_copy(upto[turn][:, 0:reach, :], of[:, 0:reach, :])
                    steps.link(v.tensor_tensor(upto[turn][:, reach:, :], of[:, reach:, :],
                                               of[:, 0:n_cols - reach, :], ALU.add))
                    of, reach, turn = upto[turn], reach * 2, 1 - turn
                steps.link(v.tensor_scalar(count_i[:], of[:, n_cols - 1, :], float(TILE - 1), None, ALU.add))
                steps.link(v.tensor_scalar(tiles_i[:], count_i[:], TILE_BITS, None, ALU.arith_shift_right))
                steps.link(v.tensor_copy(tiles[:], tiles_i[:]))
                end, reach, turn_e = tiles, 1, 0
                while reach < EXPERTS:
                    v.tensor_copy(ends[turn_e][:, 0:reach], end[:, 0:reach])
                    steps.link(v.tensor_tensor(ends[turn_e][:, reach:], end[:, reach:],
                                               end[:, 0:EXPERTS - reach], ALU.add))
                    end, reach, turn_e = ends[turn_e], reach * 2, 1 - turn_e
                steps.link(v.tensor_tensor(start[:], end[:], tiles[:], ALU.subtract))
                steps.link(v.tensor_scalar(start[:], start[:], float(TILE), None, ALU.mult))
                shape = [1, TILES, EXPERTS]
                steps.link(v.tensor_tensor(past[:], k.rowf[0:1, 0:TILES].unsqueeze(2).to_broadcast(shape),
                                           end[0:1, :].unsqueeze(1).to_broadcast(shape), ALU.is_ge))
                steps.link(v.tensor_reduce(owner[:], past[:], AX.X, ALU.add))
                steps.link(v.tensor_scalar(k.tile_expert[:], owner[:], float(EXPERTS - 1), None, ALU.min))
                steps.link(v.tensor_tensor(total, of, total, ALU.subtract))
                shape = [P, TOP * NB, EXPERTS]
                steps.link(v.tensor_tensor(total, total, start[:].unsqueeze(1).to_broadcast(shape), ALU.add))
                dve.wait_ge(counted, 2)
                for y in range(TOP):
                    last = v.tensor_tensor(upto[turn][:, y * NB:(y + 1) * NB, :], total[:, y * NB:(y + 1) * NB, :],
                                           counts[y][:], ALU.add)
                steps.link(last)
                steps.link(v.tensor_tensor(total, upto[turn], chosen[:].rearrange("p y b e -> p (y b) e"),
                                           ALU.mult))
                steps.link(v.tensor_reduce(slot_f[:], total, AX.X, ALU.add))
                steps.link(v.tensor_copy(k.slot[:], slot_f[:]))

                def add_bias(n, u):
                    dve.wait_ge(plus_made, n + 1)
                    v.tensor_tensor(tile(k.acc, n), tile(k.acc, n), plus[u][:], ALU.add).then_inc(plus_read, 1)

                over_tiles(dve, add_bias)

            @block.scalar
            def _(act):
                for y in range(2):
                    act.wait_ge(var_made, y + 1)
                    nc.scalar.activation(std[:, y], tmp[:, y], ACT.Sqrt).then_inc(std_made, 1)

                def step(n, u):
                    act.wait_ge(turned_made, n + 1)
                    after(act, scored, n - 1)
                    nc.scalar.copy(ut[:, u], turned[u][:]).then_inc(turned_read, 1)

                over_tiles(act, step)
                act.wait_ge(diff_made, 1)
                nc.scalar.activation(lg[:], lg[:], ACT.Exp).then_inc(exp_made, 1)

                act.wait_ge(route_made, 1)

                def keep_wt(n, u):
                    after(act, wt_made, n - 1)
                    nc.scalar.copy(routed[:, u, :], route[:, bass.ds(n, 1), :].rearrange(
                        "p o e -> p (o e)")).then_inc(routed_made, 1)
                    act.wait_ge(wt_made, n + 1)
                    after(act, plus_made, n - 1)
                    nc.scalar.copy(wt[:, u, :], turned[u][0:EXPERTS, 0, :]).then_inc(wt_read, 1)

                over_tiles(act, keep_wt)

            @block.tensor
            def _(pe):
                pe.wait_ge(small_landed, 16 * (DIRS + 3))

                def step(n, u):
                    pe.wait_ge(normed, n + 1)
                    after(pe, turned_read, n - 1)
                    for kt in range(2):
                        last = nc.tensor.transpose(turned[u][:, kt, :], un[:, u, kt * P:(kt + 1) * P], k.ident[:])
                    last.then_inc(turned_made, 1)
                    pe.wait_ge(turned_read, n + 1)
                    after(pe, scores_read, n - 1)
                    for kt in range(2):
                        last = nc.tensor.matmul(scores[u][:], ut[:, u, kt, :], wr[:, kt, :], start=kt == 0,
                                                stop=kt == 1)
                    last.then_inc(scored, 1)

                over_tiles(pe, step)

                pe.wait_ge(chosen_made, 1)
                for at, of in enumerate((k.ones, k.below)):
                    if at:
                        pe.wait_ge(counts_read, at)
                    for y in range(TOP):
                        last = nc.tensor.matmul(counts[y][:], of[:], chosen[:, y], start=True, stop=True)
                    last.then_inc(counted, 1)

                def bias_term(n, u):
                    pe.wait_ge(routed_made, n + 1)
                    after(pe, wt_read, n - 1)
                    nc.tensor.transpose(turned[u][0:EXPERTS, 0, :], routed[:, u, :], k.ident[:]).then_inc(wt_made, 1)
                    pe.wait_ge(wt_read, n + 1)
                    after(pe, plus_read, n - 1)
                    nc.tensor.matmul(plus[u][:], wt[:, u, :], b2[:], start=True, stop=True).then_inc(plus_made, 1)

                pe.wait_ge(turned_read, NB)
                over_tiles(pe, bias_term)


def experts(nc, s, k, slot_rows, result_rows, vectors, w1, w2, out):
    HB = HID // P
    VEC = vectors.shape[2]
    FULL = NB - 1
    NH = 4
    LN_B, B1 = 2, 4

    with Scope(nc, "move") as t, nc.Block() as block:
        scattered = t.sem("scattered")

        @block.gpsimd
        def _(pool):
            for c in range(TOP * NB):
                nc.gpsimd.indirect_dma_start(
                    out=slot_rows, out_offset=bass.IndirectOffsetOnAxis(ap=k.slot[:, c:c + 1], axis=0),
                    in_=k.acc[:, NB + c % NB, 0:D], in_offset=None).then_inc(scattered, 16)
            pool.wait_ge(scattered, 16 * TOP * NB)

    with Scope(nc, "ffn") as t:
        xs = t.sb("xs", [P, 2, SUB, D], F32)
        xe = t.sb("xe", [P, 2, TILE], F32)
        w1s = [t.sb(f"w1_{i}", [P, 2, HID], F32) for i in range(2)]
        w2s = [t.sb(f"w2_{i}", [P, HB, D], F32) for i in range(2)]
        hid = t.sb("hid", [P, HB, TILE], F32)
        table = t.sb("table", [P, EXPERTS, VEC], F32)
        vec = t.sb("vec", [P, 2, VEC], F32)
        ys = [k.acc[:, NB + u * SUB:NB + (u + 1) * SUB, 0:D] for u in range(2)]
        turned = [t.ps(f"turned_x{i}", [P, TILE]) for i in range(2)]
        hps = [t.ps(f"hps{i}", [P, TILE]) for i in range(NH)]
        yps = [t.ps(f"yps{i}", [P, D]) for i in range(2)]

        table_landed = t.sem("table_landed")
        xs_landed = [t.sem(f"xs_landed{i}") for i in range(2)]
        w1_landed = [t.sem(f"w1_landed{i}") for i in range(2)]
        w2_landed = [t.sem(f"w2_landed{i}") for i in range(2)]
        vec_made, turned_made, xe_made = t.sem("vec_made"), t.sem("x_turned"), t.sem("xe_made")
        h_made, h_kept = t.sem("hid_made"), t.sem("hid_kept")
        y_made, y_kept = t.sem("y_made"), t.sem("y_kept")
        y_written = [t.sem(f"y_written{i}") for i in range(2)]

        with nc.Block() as block:

            def over_slot_tiles(eng, step):
                for n in range(2):
                    step(n, n, 0)
                with eng.Fori(1, TILES // 2 - 1) as i:
                    for u in range(2):
                        step(i * 2 + u, u, i)
                for n in range(TILES - 2, TILES):
                    step(n, n % 2, n // 2)

            def comes(n):
                return not isinstance(n, int) or n < TILES

            def slots_of(rows, n):
                return rows[bass.ds(n * TILE, TILE), :].rearrange("(p b) n -> p b n", b=SUB)

            def expert_of(eng, n):
                return eng.value_load(k.tile_expert[0:1, bass.ds(n, 1)], min_val=0, max_val=EXPERTS - 1)

            @block.sync
            def _(sp):
                sp.dma_start(table[:], vectors).then_inc(table_landed, 16)

                def load(n, u):
                    u = u % 2
                    after(sp, turned_made, n - 1)
                    sp.dma_start(xs[:, u], slots_of(slot_rows, n)).then_inc(xs_landed[u], 16)
                    e = expert_of(sp, n)
                    after(sp, h_made, (n - 1) * HB)
                    sp.dma_start(w1s[u][:], w1[bass.ds(e, 1), :, :].rearrange(
                        "o (k p) n -> p (o k) n", p=P)).then_inc(w1_landed[u], 16)
                    after(sp, y_made, (n - 1) * SUB)
                    sp.dma_start(w2s[u][:], w2[bass.ds(e, 1), :, :].rearrange(
                        "o (k p) n -> p (o k) n", p=P)).then_inc(w2_landed[u], 16)

                def step(n, u, i):
                    if comes(n + 1):
                        load(n + 1, u + 1)
                    sp.wait_ge(y_kept, (n + 1) * SUB)
                    sp.dma_start(slots_of(result_rows, n), ys[u]).then_inc(y_written[u], 16)

                load(0, 0)
                over_slot_tiles(sp, step)
                for u in range(2):
                    sp.wait_ge(y_written[u], 16 * (TILES // 2))

            @block.tensor
            def _(pe):
                mm = nc.tensor.matmul

                def turn(n, u, i):
                    pe.wait_ge(xs_landed[u % 2], (i + (1 + u // 2)) * 16)
                    after(pe, xe_made, n)
                    for b in range(SUB):
                        for kt in range(2):
                            last = nc.tensor.transpose(turned[kt][:, b * P:(b + 1) * P],
                                                       xs[:, u % 2, b, kt * P:(kt + 1) * P], k.ident[:])
                    last.then_inc(turned_made, 1)

                def step(n, u, i):
                    pe.wait_ge(xe_made, n + 1)
                    pe.wait_ge(w1_landed[u], (i + 1) * 16)
                    for hb in range(HB):
                        after(pe, h_kept, n * HB + (hb + 1 - NH))
                        for kt in range(2):
                            last = mm(hps[hb % NH][:], w1s[u][:, kt, hb * P:(hb + 1) * P], xe[:, kt, :],
                                      start=kt == 0, stop=kt == 1)
                        last.then_inc(h_made, 1)
                    if comes(n + 1):
                        turn(n + 1, u + 1, i)
                    pe.wait_ge(w2_landed[u], (i + 1) * 16)
                    for b in range(SUB):
                        after(pe, y_kept, n * SUB + (b - 1))
                        for hb in range(HB):
                            if b == 0:
                                pe.wait_ge(h_kept, n * HB + (hb + 1))
                            last = mm(yps[b % 2][:], hid[:, hb, b * P:(b + 1) * P], w2s[u][:, hb, :],
                                      start=hb == 0, stop=hb == HB - 1)
                        last.then_inc(y_made, 1)

                turn(0, 0, 0)
                over_slot_tiles(pe, step)

            @block.scalar
            def _(act):
                def scale(n, u):
                    act.wait_ge(vec_made, n + 1)
                    act.wait_ge(turned_made, n + 1)
                    for kt in range(2):
                        last = nc.scalar.activation(xe[:, kt, :], turned[kt][:], ACT.Identity,
                                                    scale=vec[:, u % 2, kt:kt + 1],
                                                    bias=vec[:, u % 2, LN_B + kt:LN_B + kt + 1])
                    last.then_inc(xe_made, 1)

                def step(n, u, i):
                    for hb in range(HB):
                        act.wait_ge(h_made, n * HB + (hb + 1))
                        if hb == 0:
                            after(act, y_made, n * SUB)
                        nc.scalar.activation(hid[:, hb, :], hps[hb % NH][:], ACT.Gelu,
                                             bias=vec[:, u, B1 + hb:B1 + hb + 1]).then_inc(h_kept, 1)
                    if comes(n + 1):
                        scale(n + 1, u + 1)

                scale(0, 0)
                over_slot_tiles(act, step)

            @block.vector
            def _(dve):
                v = nc.vector

                def take_vectors(n, u):
                    after(dve, h_kept, (n - 1) * HB)
                    v.tensor_copy(vec[:, u % 2, :], table[:, bass.ds(expert_of(dve, n), 1), :].rearrange(
                        "p o n -> p (o n)")).then_inc(vec_made, 1)

                def step(n, u, i):
                    if comes(n + 1):
                        take_vectors(n + 1, u + 1)
                    after(dve, y_written[u], i * 16)
                    for b in range(SUB):
                        dve.wait_ge(y_made, n * SUB + (b + 1))
                        v.tensor_copy(ys[u][:, b, :], yps[b % 2][:]).then_inc(y_kept, 1)

                dve.wait_ge(table_landed, 16)
                take_vectors(0, 0)
                over_slot_tiles(dve, step)

    with Scope(nc, "back") as t:
        BATCH = 7
        RING = 4
        BATCHES = TOP * NB // BATCH
        assert NB % BATCH == 0 and RING * BATCH <= NB
        fetched = [t.sem(f"fetched{i}") for i in range(RING)]
        added, out_written = t.sem("result_added"), t.sem("out_written")

        with nc.Block() as block:

            @block.gpsimd
            def _(pool):
                for m in range(BATCHES):
                    if m >= RING:
                        pool.wait_ge(added, (m - RING + 1) * BATCH)
                    for j in range(BATCH):
                        c = m * BATCH + j
                        nc.gpsimd.indirect_dma_start(
                            out=k.acc[:, NB + m % RING * BATCH + j, 0:D], out_offset=None, in_=result_rows,
                            in_offset=bass.IndirectOffsetOnAxis(ap=k.slot[:, c:c + 1], axis=0),
                        ).then_inc(fetched[m % RING], 16)

            @block.vector
            def _(dve):
                for m in range(BATCHES):
                    dve.wait_ge(fetched[m % RING], 16 * BATCH * (m // RING + 1))
                    y, first = divmod(m * BATCH, NB)
                    if y:
                        dve.wait_ge(added, (m - NB // BATCH + 1) * BATCH)
                    for j in range(BATCH):
                        n = first + j
                        nc.vector.scalar_tensor_tensor(
                            out=k.acc[:, n, 0:D], in0=k.acc[:, NB + m % RING * BATCH + j, 0:D],
                            scalar=k.share[:, y, n:n + 1], in1=k.acc[:, n, 0:D],
                            op0=ALU.mult, op1=ALU.add).then_inc(added, 1)

            @block.sync
            def _(sp):
                sp.wait_ge(added, TOP * NB)
                sp.dma_start(out[0:FULL * P, :].rearrange("(b p) n -> p b n", p=P),
                             k.acc[:, 0:FULL, 0:D]).then_inc(out_written, 16)
                sp.dma_start(out[FULL * P:N_NODES, :], k.acc[0:TAIL, FULL, 0:D]).then_inc(out_written, 16)
                sp.wait_ge(out_written, 32)


def build_program(nc, a, out):
    table = nc.dram_tensor("h_table", [DIRS * NPAD, ROW], F32, kind="Internal").ap()
    slot_rows, result_rows = [nc.dram_tensor(name, [TILES * TILE, D], F32, kind="Internal").ap()
                              for name in ("slot_rows", "result_rows")]
    k = Kept()
    with Scope(nc, "all") as s:
        make_constants(nc, s, k)
        sort_edges(nc, s, k, a["edges"], slot_rows)
        weights = [[a[f"L0_gnn_{w}{r + 1}"] for w in ("W", "a_src", "a_dst")] for r in range(DIRS)]
        node_tables(nc, s, k, a["x"], weights, table)
        edge_sums(nc, s, k, table)
        combine(nc, s, k, a["x"], [a["L0_gnn_b1"], a["L0_gnn_b2"]], a["L0_ffn_Wr"], a["L0_ffn_br"],
                a["L0_ffn_b2"])
        experts(nc, s, k, slot_rows, result_rows, a["vectors"], a["L0_ffn_W1"], a["L0_ffn_W2"], out)


def kernel(**inputs):
    import numpy as np
    import concourse.bacc as bacc
    from concourse.bass_utils import run_bass_kernel_spmd

    nc = bacc.Bacc("TRN2", target_bir_lowering=False, num_devices=1)
    host = {name: np.ascontiguousarray(a) for name, a in inputs.items() if name not in ("src", "dst")}
    host["edges"] = np.stack([np.asarray(inputs["src"]), np.asarray(inputs["dst"])])
    host["vectors"] = np.ascontiguousarray(np.concatenate(
        [host.pop(name).reshape(EXPERTS, -1, P).transpose(2, 0, 1)
         for name in ("L0_ffn_ln_g", "L0_ffn_ln_b", "L0_ffn_b1")], axis=2))
    arrays, aps = {}, {}
    for name, a in host.items():
        arrays[f"in_{name}"] = a
        aps[name] = nc.dram_tensor(f"in_{name}", a.shape, mybir.dt.from_np(a.dtype), kind="ExternalInput").ap()
    out = nc.dram_tensor("out", [N_NODES, D], F32, kind="ExternalOutput").ap()
    build_program(nc, aps, out)
    result = run_bass_kernel_spmd(nc, [arrays], core_ids=[0])
    return result.results[0]["out"]
```

```python
from contextlib import ExitStack

import concourse.bass as bass
from concourse import mybir

F32 = mybir.dt.float32
BF16 = mybir.dt.bfloat16
F16 = mybir.dt.float16
I32 = mybir.dt.int32
ALU = mybir.AluOpType
ACT = mybir.ActivationFunctionType
AX = mybir.AxisListType

P = 128
N_NODES = 6250
D = 256
HEADS = 4
C = D // HEADS
ROW = D + HEADS
N_EDGES = 200000
EXPERTS = 8
HID = 1024
EPS = 1e-5
SLOPE = 0.2

TOP = 2
NB = -(-N_NODES // P)
TAIL = N_NODES - (NB - 1) * P
NPAD = NB * P
DIRS = 2

EP = 125
ECOLS = N_EDGES // EP
CHUNKS = 4
CC = ECOLS // CHUNKS
GC = 5
NG = CC // GC
ITEMS = -(-(EP * CC + NB * (P - 1)) // P)
ITEMS += -ITEMS % 8
N_ITEMS = DIRS * CHUNKS * ITEMS
PACK = 4
ACC_BITS = 7
assert DIRS * NB <= 1 << ACC_BITS
TILE = 3 * P
TILES = (TOP * NPAD + EXPERTS * (TILE - 1)) // TILE
SUB = TILE // P
assert EP * ECOLS == N_EDGES and GC * NG == CC and NG <= P and ITEMS <= 512


def over_columns(eng, step):
    PER = 7
    assert NB % PER == 0
    with eng.Fori(0, NB // PER) as i:
        for j in range(PER):
            step(i * PER + j)


class Kept:
    pass


class Count:

    def __init__(self, sem, eng):
        self.sem, self.eng, self.n = sem, eng, 0

    def mark(self, ins):
        ins.then_inc(self.sem, 1)
        self.n = self.n + 1

    def link(self, ins):
        self.mark(ins)
        self.eng.wait_ge(self.sem, self.n)


def after(eng, sem, value):
    if not isinstance(value, int) or value > 0:
        eng.wait_ge(sem, value)


class Scope(ExitStack):

    def __init__(self, nc, stage):
        super().__init__()
        self.nc, self.stage = nc, stage

    def sb(self, name, shape, dt):
        return self.enter_context(self.nc.sbuf_tensor(f"{self.stage}_{name}", shape, dt))

    def ps(self, name, shape, dt=F32):
        return self.enter_context(self.nc.psum_tensor(f"{self.stage}_{name}", shape, dt))

    def sem(self, name):
        return self.enter_context(self.nc.semaphore(f"{self.stage}_{name}"))


def make_constants(nc, s, k):
    k.row16 = s.sb("row16", [P, 512], F16)
    k.rowf = s.sb("rowf", [P, P], F32)
    k.colf = s.sb("colf", [P, 1], F32)
    k.row_bf = s.sb("row_bf", [P, P], BF16)
    k.ident = s.sb("ident", [P, P], F32)
    k.ident_bf = s.sb("ident_bf", [P, P], BF16)
    k.below = s.sb("below", [P, P], F32)
    k.upto = s.sb("upto", [P, P], F32)
    k.below_items = s.sb("below_items", [P, P], F32)
    k.below_bf = s.sb("below_bf", [P, P], BF16)
    k.ones = s.sb("ones", [P, P], F32)
    k.ones_bf = s.sb("ones_bf", [P, P], BF16)
    iota_done = s.sem("iota_done")
    const_done = s.sem("const_done")
    with Scope(nc, "const") as t, nc.Block() as block:
        row_i = t.sb("row_i", [P, 512], I32)
        col_i = t.sb("col_i", [P, 1], I32)

        @block.gpsimd
        def _(pool):
            nc.gpsimd.iota(row_i[:], [[1, 512]], base=0, channel_multiplier=0).then_inc(iota_done, 1)
            nc.gpsimd.iota(col_i[:], [[0, 1]], base=0, channel_multiplier=1).then_inc(iota_done, 1)

        @block.vector
        def _(dve):
            dve.wait_ge(iota_done, 2)
            nc.vector.tensor_copy(k.row16[:], row_i[:])
            nc.vector.tensor_copy(k.row_bf[:], row_i[:, 0:P])
            nc.vector.memset(k.ones[:], 1.0)
            nc.vector.memset(k.ones_bf[:], 1.0)
            nc.vector.tensor_copy(k.colf[:], col_i[:]).then_inc(const_done, 1)
            nc.vector.tensor_copy(k.rowf[:], row_i[:, 0:P]).then_inc(const_done, 1)
            dve.wait_ge(const_done, 2)
            for out, op in ((k.ident, ALU.is_equal), (k.ident_bf, ALU.is_equal), (k.below, ALU.is_gt),
                            (k.below_bf, ALU.is_gt), (k.upto, ALU.is_ge)):
                nc.vector.tensor_scalar(out[:], k.rowf[:], k.colf[:], None, op)
            nc.vector.tensor_scalar(k.below_items[:], k.rowf[:], k.colf[:], float(P), ALU.is_gt, ALU.mult)


def sort_edges(nc, s, k, edges, slot_rows):
    k.src_row = s.sb("src_row", [P, N_ITEMS], I32)
    k.target = s.sb("target", [P, N_ITEMS], BF16)
    k.item_acc = s.sb("item_acc", [1, N_ITEMS // PACK], I32)
    BLOCKS = CC // (2 * GC)
    BY_DVE = 2
    OWN = 1 << 16
    assert ITEMS * P <= OWN
    with Scope(nc, "sort") as t:
        zeros = t.sb("zeros", [P, TILES * TILE * D // P // 8], F32)
        tgt = t.sb("tgt", [EP, CC], I32)
        src = t.sb("src", [EP, CC], I32)
        bucket_i = t.sb("bucket_i", [EP, CC], I32)
        local_i = t.sb("local_i", [EP, CC], I32)
        src_hi = t.sb("src_hi", [EP, CC], I32)
        src_lo = t.sb("src_lo", [EP, CC], I32)
        bucket = t.sb("bucket", [EP, CC], BF16)
        local_1 = t.sb("local_1", [EP, CC], F32)
        src_256 = t.sb("src_256", [EP, CC], F32)
        load = t.sb("load", [EP, 2, CC, 2], F16)
        in_bucket = [t.sb(f"in_bucket{i}", [EP, CC, NB], BF16) for i in range(2)]
        window = t.sb("window", [EP, 2 * NG - 1], BF16)
        totals = t.sb("totals", [NG, NB], F32)
        filled = t.sb("filled", [NB, P], I32)
        items_i = t.sb("items_i", [NB, P], I32)
        items = t.sb("items", [NB, P], F32)
        ends = t.sb("ends", [NB, 1], F32)
        base_i = t.sb("base_i", [NG, NB], I32)
        base_hi_i = t.sb("base_hi_i", [NG, NB], I32)
        base_lo_i = t.sb("base_lo_i", [NG, NB], I32)
        base_hi = t.sb("base_hi", [NG, NB], F32)
        base_lo = t.sb("base_lo", [NG, NB], F32)
        diag_hi = t.sb("diag_hi", [NG, NG, NB], BF16)
        diag_lo = t.sb("diag_lo", [NG, NG, NB], BF16)
        past_end = t.sb("past_end", [NB, ITEMS], BF16)
        below_own = t.sb("below_own", [EP, EP], BF16)
        slot = t.sb("slot", [EP, CC], F32)
        slot_i = t.sb("slot_i", [EP, CC], I32)
        item_i = t.sb("item_i", [EP, CC], I32)
        part_i = t.sb("part_i", [EP, CC], I32)
        item_f = t.sb("item_f", [EP, CC], F32)
        part_f = t.sb("part_f", [EP, CC], F32)
        half_less = t.sb("half_less", [EP, CC], F32)
        put_load = t.sb("put_load", [EP, 2, GC, P], F32)
        put_item = t.sb("put_item", [EP, 2, GC, ITEMS], F16)
        signed = t.sb("signed", [P, 2, ITEMS + 1], F32)
        moved = t.sb("moved", [P, 2, ITEMS], F32)
        moved_i = t.sb("moved_i", [P, ITEMS], I32)
        moved_lo = t.sb("moved_lo", [P, ITEMS], I32)
        moved_hi = t.sb("moved_hi", [P, ITEMS], I32)
        src_f = t.sb("src_f", [P, ITEMS], F32)
        acc_f = t.sb("acc_f", [1, ITEMS // PACK, PACK], F32)
        acc_pair = t.sb("acc_pair", [1, ITEMS // PACK, PACK // 2], I32)

        small = t.ps("small", [P, 512])
        bucket_tot = small[0:NB, 64:64 + P]
        group_base, bucket_end = small[0:NG, 256:256 + NB], small[0:NB, 448:450]
        rank = [t.ps(f"rank{i}", [EP, 2 * GC, NB]) for i in range(2)]
        got = [t.ps(f"got{h}", [P, ITEMS]) for h in range(2)]
        got_signed = [t.ps(f"got_signed{h}", [P, ITEMS]) for h in range(2)]
        bucket_row = t.ps("bucket_row", [P, ITEMS])
        column_tot = bucket_row[0:NG, 0:GC * NB].rearrange("p (c b) -> p c b", c=GC)

        zeros_made, slots_cleared = t.sem("zeros_made"), t.sem("slots_cleared")
        tgt_landed, src_landed = t.sem("tgt_landed"), t.sem("src_landed")
        ids_used, ids_ready, pool_steps = t.sem("ids_used"), t.sem("ids_ready"), t.sem("pool_steps")
        bases_split, lo_made = t.sem("bases_split"), t.sem("lo_made")
        sort_steps = t.sem("sort_steps")
        hot_made = t.sem("hot_made")
        totals_made, totals_read = t.sem("totals_made"), t.sem("totals_read")
        fill_made, items_made = t.sem("fill_made"), t.sem("items_made")
        base_made, ends_read, diag_made = t.sem("base_made"), t.sem("ends_read"), t.sem("diag_made")
        buckets_made = t.sem("buckets_made")
        rank_made, rank_read = t.sem("rank_made"), t.sem("rank_read")
        slots_ready, signs_made = t.sem("slots_ready"), t.sem("signs_made")
        puts_made, puts_used = t.sem("puts_made"), t.sem("puts_used")

        with nc.Block() as block:

            def over_groups(eng, group):
                for g in range(2):
                    group(g, g)
                with eng.Fori(1, NG // 2 - 1) as i:
                    for w in range(2):
                        group(i * 2 + w, w)
                for g in range(NG - 2, NG):
                    group(g, g % 2)

            @block.sync
            def _(sp):
                for n in range(DIRS * CHUNKS):
                    r, q = divmod(n, CHUNKS)
                    by = [edges[x, :].rearrange("(p c) -> p c", p=EP) for x in (1 - r, r)]
                    if n:
                        sp.wait_ge(ids_used, n)
                    sp.dma_start(tgt[:], by[0][:, q * CC:(q + 1) * CC]).then_inc(tgt_landed, 16)
                    sp.dma_start(src[:], by[1][:, q * CC:(q + 1) * CC]).then_inc(src_landed, 16)
                    sp.wait_ge(zeros_made, 1)
                    cleared = slot_rows[n * (TILES * TILE // 8):(n + 1) * (TILES * TILE // 8), :]
                    sp.dma_start(cleared.rearrange("(p r) n -> p (r n)", p=P), zeros[:]).then_inc(slots_cleared, 16)
                sp.wait_ge(slots_cleared, 16 * DIRS * CHUNKS)

            def spread_base(engine, diag, of):
                shape = [NG, NG, NB]
                return engine.tensor_tensor(diag[:], of[:].unsqueeze(1).to_broadcast(shape),
                                            k.ident[0:NG, 0:NG].unsqueeze(2).to_broadcast(shape), ALU.mult)

            @block.gpsimd
            def _(pool):
                g = nc.gpsimd
                steps = Count(pool_steps, pool)

                def ready_loads(n):
                    pool.wait_ge(ids_used, n + 1)
                    if n:
                        pool.wait_ge(hot_made, n * NG)
                    if n > 1:
                        pool.wait_ge(puts_made, (n - 1) * NG)
                    g.tensor_copy(load[:, n % 2, :, 0:1], src_lo[:].unsqueeze(2))
                    g.tensor_copy(bucket[:], bucket_i[:])
                    g.tensor_scalar(local_1[:], local_i[:], 1.0, None, ALU.add)
                    steps.link(g.tensor_scalar(src_256[:], src_hi[:], 256.0, None, ALU.mult))
                    g.tensor_tensor(load[:, n % 2, :, 1:2], src_256[:].unsqueeze(2), local_1[:].unsqueeze(2),
                                    ALU.add).then_inc(ids_ready, 1)

                ready_loads(0)
                for n in range(DIRS * CHUNKS):
                    pool.wait_ge(bases_split, n + 1)
                    spread_base(g, diag_lo, base_lo).then_inc(lo_made, 1)
                    if n + 1 < DIRS * CHUNKS:
                        ready_loads(n + 1)

            @block.vector
            def _(dve):
                v = nc.vector
                steps = Count(sort_steps, dve)
                v.memset(zeros[:], 0.0).then_inc(zeros_made, 1)
                steps.link(v.scalar_tensor_tensor(out=below_own[:], in0=k.ident_bf[0:EP, 0:EP], scalar=float(OWN),
                                                  in1=k.below_bf[0:EP, 0:EP], op0=ALU.mult, op1=ALU.add))
                steps.link(v.memset(window[:], 0.0))
                steps.link(v.memset(window[:, NG - 1:NG], 1.0))

                def split_ids(n):
                    dve.wait_ge(tgt_landed, 16 * (n + 1))
                    dve.wait_ge(src_landed, 16 * (n + 1))
                    if n:
                        dve.wait_ge(ids_ready, n)
                    v.tensor_scalar(bucket_i[:], tgt[:], 7, None, ALU.arith_shift_right)
                    v.tensor_scalar(local_i[:], tgt[:], P - 1, None, ALU.bitwise_and)
                    v.tensor_scalar(src_hi[:], src[:], 10, None, ALU.arith_shift_right)
                    v.tensor_scalar(src_lo[:], src[:], 1023, None, ALU.bitwise_and).then_inc(ids_used, 1)

                def make_in_bucket(n, c0, cols):
                    shape = [EP, cols, NB]
                    v.tensor_tensor(in_bucket[n % 2][:, bass.ds(c0, cols), :],
                                    bucket[:, bass.ds(c0, cols)].unsqueeze(2).to_broadcast(shape),
                                    k.row_bf[0:EP, 0:NB].unsqueeze(1).to_broadcast(shape),
                                    ALU.is_equal).then_inc(hot_made, cols // GC)

                def place_buckets(n):
                    dve.wait_ge(totals_made, n + 1)
                    v.tensor_reduce(totals[:], column_tot.rearrange("p c b -> p b c"), AX.X,
                                    ALU.add).then_inc(totals_read, 1)
                    dve.wait_ge(fill_made, n + 1)
                    steps.link(v.tensor_scalar(filled[:], bucket_tot, float(P - 1), None, ALU.add))
                    steps.link(v.tensor_scalar(items_i[:], filled[:], 7, None, ALU.arith_shift_right))
                    v.tensor_copy(items[:], items_i[:]).then_inc(items_made, 1)
                    dve.wait_ge(base_made, n + 1)
                    v.tensor_copy(ends[:], bucket_end[:, 0:1])
                    steps.link(v.tensor_copy(base_i[:], group_base))
                    v.tensor_scalar(past_end[:], k.row16[0:NB, 0:ITEMS], ends[:], None,
                                    ALU.is_ge).then_inc(ends_read, 1)
                    v.tensor_scalar(base_hi_i[:], base_i[:], 0x1FF00, None, ALU.bitwise_and)
                    steps.link(v.tensor_scalar(base_lo_i[:], base_i[:], 255, None, ALU.bitwise_and))
                    v.tensor_copy(base_hi[:], base_hi_i[:])
                    steps.link(v.tensor_copy(base_lo[:], base_lo_i[:]))
                    dve.sem_inc(bases_split, 1)
                    spread_base(v, diag_hi, base_hi).then_inc(diag_made, 1)
                    dve.wait_ge(buckets_made, n + 1)
                    steps.link(v.tensor_scalar(acc_f[:].rearrange("o i p -> o (i p)"), bucket_row[0:1, :],
                                               float(NB - 1), float(n // CHUNKS * NB), ALU.min, ALU.add))
                    for h in range(2):
                        last = v.scalar_tensor_tensor(
                            out=acc_pair[:, :, h:h + 1], in0=acc_f[:, :, 2 * h + 1:2 * h + 2],
                            scalar=float(1 << ACC_BITS), in1=acc_f[:, :, 2 * h:2 * h + 1], op0=ALU.mult, op1=ALU.add)
                    steps.link(last)
                    steps.link(v.tensor_scalar(acc_pair[:, :, 1:2], acc_pair[:, :, 1:2], 2 * ACC_BITS, None,
                                               ALU.logical_shift_left))
                    v.tensor_tensor(k.item_acc[0:1, n * (ITEMS // PACK):(n + 1) * (ITEMS // PACK)].rearrange(
                        "o (i p) -> o i p", p=1), acc_pair[:, :, 0:1], acc_pair[:, :, 1:2], ALU.bitwise_or)

                def pick_slots(n):
                    PER = 4
                    with dve.Fori(0, BLOCKS // PER) as i:
                        for j in range(PER):
                            dve.wait_ge(rank_made, i * PER + (n * BLOCKS + j + 1))
                            v.tensor_reduce(slot[:, bass.ds((i * PER + j) * (2 * GC), 2 * GC)], rank[j % 2][:],
                                            AX.X, ALU.max).then_inc(rank_read, 1)
                    dve.wait_ge(rank_read, (n + 1) * BLOCKS)
                    steps.link(v.tensor_copy(slot_i[:], slot[:]))
                    v.tensor_scalar(item_i[:], slot_i[:], 7, OWN // P - 1, ALU.arith_shift_right, ALU.bitwise_and)
                    steps.link(v.tensor_scalar(part_i[:], slot_i[:], P - 1, None, ALU.bitwise_and))
                    steps.link(v.tensor_copy(item_f[:], item_i[:]))
                    v.tensor_scalar(half_less[:], item_f[:], -1.0, 0.5, ALU.mult, ALU.add)
                    steps.link(v.tensor_copy(part_f[:], part_i[:]))
                    dve.sem_inc(slots_ready, 1)

                def put_columns(n):
                    words = load[:, n % 2].rearrange("p c h -> p (c h)").bitcast(F32)

                    def group(g, w):
                        after(dve, puts_used, g + (n * NG - 1))
                        for u in range(GC):
                            c = g * GC + u
                            last = v.tensor_scalar(put_load[:, w, u], k.row16[0:EP, 0:P], part_f[:, bass.ds(c, 1)],
                                                   words[:, bass.ds(c, 1)], ALU.is_equal, ALU.mult)
                            if u < BY_DVE:
                                last = v.tensor_scalar(put_item[:, w, u], k.row16[0:EP, 0:ITEMS],
                                                       item_f[:, bass.ds(c, 1)], None, ALU.is_equal)
                        last.then_inc(puts_made, 1)
                        if n + 1 < DIRS * CHUNKS:
                            make_in_bucket(n + 1, g * GC, GC)

                    over_groups(dve, group)

                def unpack_items(n):
                    at = slice(n * ITEMS, (n + 1) * ITEMS)
                    dve.wait_ge(puts_used, (n + 1) * NG)
                    for h in range(2):
                        v.tensor_scalar(signed[:, h, 0:1], got_signed[h][:, ITEMS - 1:ITEMS], -1.0, None, ALU.mult)
                        last = v.tensor_copy(signed[:, h, 1:], got_signed[h][:])
                    steps.link(last)
                    steps.link(v.tensor_tensor(moved[:], signed[:, :, 1:], signed[:, :, 0:ITEMS], ALU.subtract))
                    for h in range(2):
                        last = v.scalar_tensor_tensor(out=moved[:, h], in0=moved[:, h], scalar=0.5, in1=got[h][:],
                                                      op0=ALU.mult, op1=ALU.add)
                    steps.link(last)
                    steps.link(v.tensor_copy(moved_i[:], moved[:, 1]))
                    v.tensor_scalar(moved_lo[:], moved_i[:], 255, None, ALU.bitwise_and)
                    steps.link(v.tensor_scalar(moved_hi[:], moved_i[:], 8, None, ALU.arith_shift_right))
                    v.tensor_scalar(k.target[:, at], moved_lo[:], -1.0, None, ALU.add)
                    steps.link(v.scalar_tensor_tensor(out=src_f[:], in0=moved_hi[:], scalar=1024.0,
                                                      in1=moved[:, 0], op0=ALU.mult, op1=ALU.add))
                    v.tensor_scalar(k.src_row[:, at], src_f[:], float(n // CHUNKS * NPAD), None, ALU.add)

                split_ids(0)
                dve.wait_ge(ids_ready, 1)
                make_in_bucket(0, 0, CC)
                for n in range(DIRS * CHUNKS):
                    if n + 1 < DIRS * CHUNKS:
                        split_ids(n + 1)
                    place_buckets(n)
                    if n:
                        unpack_items(n - 1)
                    pick_slots(n)
                    if n + 1 < DIRS * CHUNKS:
                        dve.wait_ge(ids_ready, n + 2)
                    put_columns(n)
                unpack_items(DIRS * CHUNKS - 1)

            @block.scalar
            def _(act):
                for n in range(DIRS * CHUNKS):

                    def group(g, w):
                        after(act, puts_used, g + (n * NG - 1))
                        for u in range(BY_DVE, GC):
                            last = nc.scalar.activation(put_item[:, w, u], k.row16[0:EP, 0:ITEMS], ACT.Sign,
                                                        bias=half_less[:, bass.ds(g * GC + u, 1)])
                        last.then_inc(signs_made, 1)

                    act.wait_ge(slots_ready, n + 1)
                    over_groups(act, group)

            @block.tensor
            def _(pe):
                mm = nc.tensor.matmul

                def count_group(n, g, first=False, last=False):
                    return mm(column_tot, window[:, bass.ds(g * -1 + (NG - 1), NG)],
                              in_bucket[n % 2][:, bass.ds(g * GC, GC), :], start=first, stop=last)

                def count_groups(n):
                    pe.wait_ge(hot_made, NG)
                    count_group(n, 0, first=True)
                    count_group(n, 1)
                    with pe.Fori(1, NG // 2 - 1) as i:
                        for w in range(2):
                            count_group(n, i * 2 + w)
                    count_group(n, NG - 2)
                    count_group(n, NG - 1, last=True).then_inc(totals_made, 1)

                def bases(n):
                    pe.wait_ge(totals_read, n + 1)
                    mm(bucket_tot, totals[:], k.ones[0:NG, :], start=True, stop=True).then_inc(fill_made, 1)
                    pe.wait_ge(items_made, n + 1)
                    mm(group_base, k.below[0:NG, 0:NG], totals[:], start=True, stop=False)
                    mm(group_base, items[:, 0:NG], k.below_items[0:NB, 0:NB], start=False, stop=True)
                    mm(bucket_end, k.upto[0:NB, 0:NB], items[:, 0:2], start=True,
                       stop=True).then_inc(base_made, 1)
                    pe.wait_ge(ends_read, n + 1)
                    mm(bucket_row[0:1, :], k.ones_bf[0:NB, 0:1], past_end[:], start=True,
                       stop=True).then_inc(buckets_made, 1)
                    pe.wait_ge(diag_made, n + 1)
                    pe.wait_ge(lo_made, n + 1)

                def rank_block(n, i, u):
                    c0 = i * (4 * GC) + u * 2 * GC
                    hot = in_bucket[n % 2][:, bass.ds(c0, 2 * GC), :]
                    by_group = [x.rearrange("p (g c) b -> p g c b", g=2) for x in (rank[u][:], hot)]
                    mm(rank[u][:], below_own[:], hot, start=True, stop=False)
                    for c in range(GC - 1):
                        mm(by_group[0][:, :, c + 1:, :], k.ones_bf[0:EP, 0:EP],
                           by_group[1][:, :, c:c + 1, :].to_broadcast([EP, 2, GC - 1 - c, NB]),
                           start=False, stop=False)
                    for diag in (diag_hi, diag_lo):
                        last = mm(by_group[0], k.ones_bf[0:NG, 0:EP],
                                  diag[:, bass.ds(i * 4 + u * 2, 2), :].unsqueeze(2).to_broadcast(
                                      [NG, 2, GC, NB]), start=False, stop=diag is diag_lo)
                    last.then_inc(rank_made, 1)

                def ranks(n):
                    for u in range(2):
                        rank_block(n, 0, u)
                    with pe.Fori(1, BLOCKS // 2) as i:
                        for u in range(2):
                            pe.wait_ge(rank_read, i * 2 + (n * BLOCKS + u - 1))
                            rank_block(n, i, u)

                def move_group(n, g, w):
                    first, last = isinstance(g, int) and g == 0, isinstance(g, int) and g == NG - 1
                    pe.wait_ge(puts_made, g + (n * NG + 1))
                    for u in range(GC):
                        to = got if u < BY_DVE else got_signed
                        if u == BY_DVE:
                            pe.wait_ge(signs_made, g + (n * NG + 1))
                        halves = put_load[:, w, u].bitcast(F16).rearrange("p (m h) -> p h m", h=2)
                        for h in range(2):
                            ins = mm(to[h][:], halves[:, h], put_item[:, w, u],
                                     start=first and u in (0, BY_DVE), stop=last and u in (BY_DVE - 1, GC - 1))
                    ins.then_inc(puts_used, 1)
                    if n + 1 < DIRS * CHUNKS:
                        pe.wait_ge(hot_made, g + ((n + 1) * NG + 1))
                        ins = count_group(n + 1, g, first=first, last=last)
                        if last:
                            ins.then_inc(totals_made, 1)

                count_groups(0)
                for n in range(DIRS * CHUNKS):
                    bases(n)
                    ranks(n)
                    over_groups(pe, lambda g, w: move_group(n, g, w))


def leaky(v, out, x):
    return v.scalar_tensor_tensor(out=out, in0=x, scalar=SLOPE, in1=x, op0=ALU.mult, op1=ALU.max)


def moments(nc, steps, stats, mean, tmp):
    v = nc.vector
    v.tensor_tensor(mean, stats[:, :, 1], stats[:, :, 4], ALU.add)
    steps.link(v.tensor_tensor(tmp, stats[:, :, 1], stats[:, :, 4], ALU.subtract))
    v.tensor_scalar(mean, mean, 0.5, None, ALU.mult)
    steps.link(v.scalar_tensor_tensor(out=tmp, in0=tmp, scalar=D / 4, in1=tmp, op0=ALU.mult, op1=ALU.mult))
    steps.link(v.tensor_tensor(tmp, tmp, stats[:, :, 2], ALU.add))
    steps.link(v.tensor_tensor(tmp, tmp, stats[:, :, 5], ALU.add))
    return v.tensor_scalar(tmp, tmp, 1.0 / D, EPS, ALU.mult, ALU.add)


def node_tables(nc, s, k, x, weights, table):
    k.acc = s.sb("acc", [P, DIRS * NB, ROW], F32)
    k.pieces = s.sb("pieces", [P, DIRS * NB, 2 * HEADS, 3], BF16)
    WIDE = ROW + HEADS
    with Scope(nc, "nodes") as t:
        xs = k.acc[:, 0:NB, 0:D]
        w = t.sb("w", [P, DIRS, 2, WIDE], F32)
        a = t.sb("a", [P, DIRS, 2, D], F32)
        prod = t.sb("prod", [P, D], F32)
        stats = t.sb("stats", [P, NB, 6], F32)
        mean = t.sb("mean", [P, NB], F32)
        tmp = t.sb("tmp", [P, NB], F32)
        std = t.sb("std", [P, NB], F32)
        rstd = t.sb("rstd", [P, NB], F32)
        xn = t.sb("xn", [P, 2, D], F32)
        xt = t.sb("xt", [P, 2, 2, P], F32)
        logit_t = t.sb("logit_t", [P, DIRS * NB, HEADS], F32)
        tops = t.sb("tops", [P, DIRS, HEADS], F32)
        bound0 = t.sb("bound0", [P, DIRS, HEADS], F32)
        z = t.sb("z", [P, DIRS * NB, HEADS], F32)
        bound = t.sb("bound", [P, DIRS * NB, HEADS], F32)
        turned = [t.ps(f"turned{i}", [P, 2, P]) for i in range(2)]
        hs = [[t.ps(f"hs{i}{r}", [P, WIDE]) for r in range(DIRS)] for i in range(2)]

        XG = 7
        assert NB % XG == 0
        x_landed = [t.sem(f"x_landed{i}") for i in range(NB // XG + 1)]
        w_landed, a_landed = t.sem("w_landed"), t.sem("a_landed")
        node_steps = t.sem("node_steps")
        stats_made = t.sem("stats_made")
        var_made, std_made = t.sem("var_made"), t.sem("std_made")
        normed, turned_made, turned_read = t.sem("normed"), t.sem("turned_made"), t.sem("turned_read")
        h_made, h0_read, h1_read = t.sem("h_made"), t.sem("h0_read"), t.sem("h1_read")
        w_made, table_written = t.sem("w_made"), t.sem("table_written")
        tops_made, bound_made = t.sem("tops_made"), t.sem("bound_made")
        z_made, p_made = t.sem("z_made"), t.sem("p_made")
        pad_cleared = t.sem("pad_cleared")
        FULL = NB - 1

        with nc.Block() as block:

            @block.sync
            def _(sp):
                for r in range(DIRS):
                    sp.dma_start(w[:, r, :, 0:D], weights[r][0].rearrange(
                        "(k p) n -> p k n", p=P)).then_inc(w_landed, 16)
                    for y in range(2):
                        row = weights[r][1 + y].rearrange("(o h) c -> o (h c)", o=1)
                        sp.dma_start(a[:, r, y, :], row.to_broadcast([P, D])).then_inc(a_landed, 16)
                for i in range(NB // XG + 1):
                    if i * XG < FULL:
                        end = min((i + 1) * XG, FULL)
                        sp.dma_start(xs[:, i * XG:end, :], x[i * XG * P:end * P, :].rearrange(
                            "(b p) n -> p b n", p=P)).then_inc(x_landed[i], 16)
                sp.wait_ge(pad_cleared, 1)
                sp.dma_start(xs[0:TAIL, FULL, :], x[FULL * P:N_NODES, :]).then_inc(x_landed[NB // XG], 16)
                for i in range(NB // XG):
                    for r in range(DIRS):
                        sp.wait_ge((h0_read, h1_read)[r], (i + 1) * XG)
                        at = r * NB + i * XG
                        sp.dma_start(table[at * P:(at + XG) * P, :].rearrange("(b p) n -> p b n", p=P),
                                     k.acc[:, at:at + XG, :]).then_inc(table_written, 16)
                sp.wait_ge(table_written, 16 * DIRS * (NB // XG))

            @block.gpsimd
            def _(pool):
                pool.wait_ge(tops_made, 1)
                nc.gpsimd.partition_all_reduce(bound0[:].rearrange("p r h -> p (r h)"),
                                               tops[:].rearrange("p r h -> p (r h)"), P,
                                               bass.bass_isa.ReduceOp.max).then_inc(bound_made, 1)

            @block.vector
            def _(dve):
                v = nc.vector
                steps = Count(node_steps, dve)
                v.memset(xs[:, FULL, :], 0.0).then_inc(pad_cleared, 1)
                dve.wait_ge(w_landed, 16 * DIRS)
                dve.wait_ge(a_landed, 16 * 2 * DIRS)
                for r in range(DIRS):
                    for kt in range(2):
                        for y in range(2):
                            steps.link(v.tensor_tensor(prod[:], w[:, r, kt, 0:D], a[:, r, y, :], ALU.mult))
                            v.tensor_reduce(w[:, r, kt, D + y * HEADS:D + (y + 1) * HEADS],
                                            prod[:].rearrange("p (h c) -> p h c", h=HEADS),
                                            AX.X, ALU.add).then_inc(w_made, 1)
                            dve.wait_ge(w_made, (r * 2 + kt) * 2 + y + 1)
                for i in range(NB // XG + 1):
                    dve.wait_ge(x_landed[i], 16)
                over_columns(dve, lambda i: v.bn_stats(
                    stats[:, bass.ds(i, 1), :].rearrange("p o n -> p (o n)"),
                    xs[:, bass.ds(i, 1), :].rearrange("p o n -> p (o n)")).then_inc(stats_made, 1))
                dve.wait_ge(stats_made, NB)
                moments(nc, steps, stats, mean[:], tmp[:]).then_inc(var_made, 1)
                dve.wait_ge(std_made, 1)
                steps.link(v.reciprocal(rstd[:], std[:]))

                def normalise(m, u):
                    after(dve, turned_made, m - 1)
                    v.tensor_scalar(xn[:, u], xs[:, bass.ds(m, 1), :].rearrange("p o n -> p (o n)"),
                                    mean[:, bass.ds(m, 1)], rstd[:, bass.ds(m, 1)],
                                    ALU.subtract, ALU.mult).then_inc(normed, 1)

                def keep_h0(m, u):
                    dve.wait_ge(h_made, m + 1)
                    v.tensor_copy(logit_t[:, bass.ds(m, 1), :].rearrange("p o h -> p (o h)"),
                                  hs[u][0][:, ROW:WIDE])
                    v.tensor_copy(k.acc[:, bass.ds(m, 1), :].rearrange("p o n -> p (o n)"),
                                  hs[u][0][:, 0:ROW]).then_inc(h0_read, 1)

                for m in range(3):
                    normalise(m, m % 2)
                keep_h0(0, 0)
                with dve.Fori(1, FULL // 2) as i:
                    for u in range(2):
                        normalise(i * 2 + (u + 1), (u + 1) % 2)
                        keep_h0(i * 2 + (u - 1), (u + 1) % 2)
                keep_h0(FULL - 1, 1)
                keep_h0(FULL, 0)
                dve.wait_ge(h0_read, NB)
                dve.wait_ge(h1_read, NB)
                for r in range(DIRS):
                    last = v.tensor_reduce(tops[:, r, :], k.acc[:, r * NB:r * NB + FULL, D:ROW].rearrange(
                        "p b h -> p h b"), AX.X, ALU.max)
                steps.link(last)
                for r in range(DIRS):
                    last = v.tensor_tensor(tops[0:TAIL, r, :], tops[0:TAIL, r, :],
                                           k.acc[0:TAIL, r * NB + FULL, D:ROW], ALU.max)
                last.then_inc(tops_made, 1)
                dve.wait_ge(bound_made, 1)
                for r in range(DIRS):
                    at = slice(r * NB, (r + 1) * NB)
                    last = v.tensor_tensor(bound[:, at, :], logit_t[:, at, :],
                                           bound0[:, r:r + 1, :].to_broadcast([P, NB, HEADS]), ALU.add)
                steps.link(v.tensor_tensor(z[:], logit_t[:], k.acc[:, :, D:ROW], ALU.add))
                leaky(v, bound[:], bound[:])
                steps.link(leaky(v, z[:], z[:]))
                v.tensor_tensor(z[:], z[:], bound[:], ALU.subtract).then_inc(z_made, 1)
                for y, of in enumerate((logit_t, bound)):
                    for piece in range(3):
                        part = k.pieces[:, :, y * HEADS:(y + 1) * HEADS, piece]
                        steps.link(v.tensor_copy(part, of[:]))
                        if piece < 2:
                            steps.link(v.tensor_tensor(of[:], of[:], part, ALU.subtract))
                dve.wait_ge(p_made, 1)
                dve.wait_ge(table_written, 16 * DIRS * (NB // XG))
                for r in range(DIRS):
                    at = slice(r * NB, (r + 1) * NB)
                    h = k.acc[:, at, 0:D].rearrange("p b (h c) -> p b h c", h=HEADS)
                    v.tensor_tensor(h, h, z[:, at, :].unsqueeze(3).to_broadcast([P, NB, HEADS, C]), ALU.mult)
                v.tensor_copy(k.acc[:, :, D:ROW], z[:])

            @block.scalar
            def _(act):
                act.wait_ge(var_made, 1)
                nc.scalar.activation(std[:], tmp[:], ACT.Sqrt).then_inc(std_made, 1)

                def keep_h1(m, u):
                    act.wait_ge(h_made, m + 1)
                    nc.scalar.copy(logit_t[:, bass.ds(m + NB, 1), :].rearrange("p o h -> p (o h)"),
                                   hs[u][1][:, ROW:WIDE])
                    nc.scalar.copy(k.acc[:, bass.ds(m + NB, 1), :].rearrange("p o n -> p (o n)"),
                                   hs[u][1][:, 0:ROW]).then_inc(h1_read, 1)

                def keep_turned(m, u):
                    act.wait_ge(turned_made, m + 1)
                    after(act, h_made, m - 1)
                    nc.scalar.copy(xt[:, u], turned[u][:]).then_inc(turned_read, 1)

                keep_turned(0, 0)
                keep_turned(1, 1)
                keep_h1(0, 0)
                with act.Fori(1, FULL // 2) as i:
                    for u in range(2):
                        keep_turned(i * 2 + u, u)
                        keep_h1(i * 2 + (u - 1), (u + 1) % 2)
                keep_turned(FULL, 0)
                keep_h1(FULL - 1, 1)
                keep_h1(FULL, 0)
                act.wait_ge(z_made, 1)
                nc.scalar.activation(z[:], z[:], ACT.Exp).then_inc(p_made, 1)

            @block.tensor
            def _(pe):
                def turn(m, u):
                    pe.wait_ge(normed, m + 1)
                    after(pe, turned_read, m - 1)
                    for kt in range(2):
                        last = nc.tensor.transpose(turned[u][:, kt, :], xn[:, u, kt * P:(kt + 1) * P],
                                                   k.ident[:])
                    last.then_inc(turned_made, 1)

                def product(m, u):
                    pe.wait_ge(turned_read, m + 1)
                    after(pe, h0_read, m - 1)
                    after(pe, h1_read, m - 1)
                    for r in range(DIRS):
                        for kt in range(2):
                            last = nc.tensor.matmul(hs[u][r][:], xt[:, u, kt, :], w[:, r, kt, :],
                                                    start=kt == 0, stop=kt == 1)
                    last.then_inc(h_made, 1)

                pe.wait_ge(w_made, DIRS * 4)
                turn(0, 0)
                turn(1, 1)
                product(0, 0)
                with pe.Fori(1, FULL // 2) as i:
                    for u in range(2):
                        turn(i * 2 + u, u)
                        product(i * 2 + (u - 1), (u + 1) % 2)
                turn(FULL, 0)
                product(FULL - 1, 1)
                product(FULL, 0)


def edge_sums(nc, s, k, table):
    J = PACK
    R = 8
    STEPS = N_ITEMS // J
    assert N_ITEMS % (J * R) == 0
    with Scope(nc, "edges") as t:
        rows = t.sb("rows", [P, R, J, ROW], F32)
        idx = t.sb("idx", [P, R, J], I32)
        hot = t.sb("hot", [P, R, J, P], F32)
        hot_t = t.sb("hot_t", [P, 2, J, P], BF16)
        logit = t.sb("logit", [P, 2, J, 2 * HEADS], F32)
        z = t.sb("z_edge", [P, 2, J, HEADS], F32)
        lz = t.sb("lz", [P, 2, J, HEADS], F32)
        turned = [t.ps(f"turned_hot{i}", [P, J, P]) for i in range(2)]
        found = [t.ps(f"found{i}", [P, J, 2 * HEADS, 3]) for i in range(2)]
        sums = [t.ps(f"sums{j}", [P, ROW]) for j in range(J)]

        idx_made, pool_gate = t.sem("idx_made"), t.sem("pool_gate")
        gathered = [t.sem(f"gathered{i}") for i in range(R)]
        hot_made, turned_made, turned_read = t.sem("hot_made"), t.sem("hot_turned"), t.sem("hot_kept")
        found_made, found_read = t.sem("found_made"), t.sem("found_read")
        z_made, p_made, weighed = t.sem("z_made"), t.sem("p_made"), t.sem("weighed")
        summed, added = t.sem("summed"), t.sem("added")
        logit_made, leaky_made = t.sem("logit_made"), t.sem("leaky_made")

        with nc.Block() as block:

            def loop(eng, step):
                for n in range(R):
                    step(n, n, 0)
                with eng.Fori(1, STEPS // R - 1) as i:
                    for u in range(R):
                        step(i * R + u, u, i)
                for n in range(STEPS - R, STEPS):
                    step(n, n % R, n // R)

            def comes(n):
                return not isinstance(n, int) or n < STEPS

            def item_accs(eng, n):
                return eng.value_load(k.item_acc[0:1, bass.ds(n, 1)], min_val=0,
                                      max_val=(1 << PACK * ACC_BITS) - 1)

            def item_acc(accs, j):
                return nc.s_assert_within(
                    accs >> j * ACC_BITS & (1 << ACC_BITS) - 1, 0, DIRS * NB - 1,
                    skip_runtime_bounds_check_because="sort_edges keeps every number below DIRS * NB")

            @block.gpsimd
            def _(pool):
                def step(n, u, i):
                    pool.wait_ge(idx_made, n + 1)
                    after(pool, summed, (n - (R - 1)) * J)
                    pool.sem_inc(pool_gate, 1)
                    for j in range(J):
                        nc.gpsimd.indirect_dma_start(
                            out=rows[:, u, j, :], out_offset=None, in_=table,
                            in_offset=bass.IndirectOffsetOnAxis(ap=idx[:, u, j:j + 1], axis=0),
                        ).then_inc(gathered[u], 16)

                loop(pool, step)

            @block.scalar
            def _(act):
                def copy_idx(n, u):
                    nc.scalar.copy(idx[:, u, :], k.src_row[:, bass.ds(n * J, J)]).then_inc(idx_made, 1)

                def keep_turned(n, u):
                    act.wait_ge(turned_made, n + 1)
                    after(act, found_made, n - 1)
                    nc.scalar.copy(hot_t[:, u % 2], turned[u % 2][:]).then_inc(turned_read, 1)

                def weights(n, u):
                    act.wait_ge(z_made, n + 1)
                    nc.scalar.activation(rows[:, u % R, :, D:ROW], z[:, u % 2], ACT.Exp).then_inc(p_made, 1)

                def step(n, u, i):
                    if comes(n + 3):
                        keep_turned(n + 3, u + 3)
                    if comes(n + 2):
                        weights(n + 2, u + 2)
                    if comes(n + R):
                        copy_idx(n + R, u)

                for n in range(R):
                    copy_idx(n, n)
                for n in range(3):
                    keep_turned(n, n)
                for n in range(2):
                    weights(n, n)
                loop(act, step)

            @block.tensor
            def _(pe):
                def turn(n, u):
                    pe.wait_ge(hot_made, n + 1)
                    after(pe, turned_read, n - 1)
                    for j in range(J):
                        last = nc.tensor.transpose(turned[u % 2][:, j, :], hot[:, u % R, j, :], k.ident[:])
                    last.then_inc(turned_made, 1)

                def look_up(n, u):
                    pe.wait_ge(turned_read, n + 1)
                    after(pe, found_read, n - 1)
                    accs = item_accs(pe, n)
                    for j in range(J):
                        acc = item_acc(accs, j)
                        last = nc.tensor.matmul(found[u % 2][:, j].rearrange("p v t -> p (v t)"), hot_t[:, u % 2, j, :],
                                                k.pieces[:, bass.ds(acc, 1), :, :].rearrange(
                                                    "p o v t -> p (o v t)"), start=True, stop=True)
                    last.then_inc(found_made, 1)

                def step(n, u, i):
                    if comes(n + 3):
                        turn(n + 3, u + 3)
                    if comes(n + 2):
                        look_up(n + 2, u + 2)
                    for j in range(J):
                        pe.wait_ge(weighed, n * J + (j + 1))
                        after(pe, added, n * J + (j + 1 - J))
                        nc.tensor.matmul(sums[j][:], hot[:, u % R, j, :], rows[:, u, j, :], start=True,
                                         stop=True).then_inc(summed, 1)

                turn(0, 0)
                turn(1, 1)
                look_up(0, 0)
                turn(2, 2)
                look_up(1, 1)
                loop(pe, step)

            @block.vector
            def _(dve):
                v = nc.vector

                def make_hot(n, u):
                    v.tensor_tensor(hot[:, u % R], k.row_bf[:].unsqueeze(1).to_broadcast([P, J, P]),
                                    k.target[:, bass.ds(n * J, J)].unsqueeze(2).to_broadcast([P, J, P]),
                                    ALU.is_equal).then_inc(hot_made, 1)

                def find_logits(n, u):
                    dve.wait_ge(found_made, n + 1)
                    v.tensor_reduce(logit[:, u % 2].rearrange("p j v -> p (j v)"), found[u % 2][:].rearrange(
                        "p j v t -> p (j v) t"), AX.X, ALU.add).then_inc(found_read, 1)

                def add_source(n, u, i):
                    dve.wait_ge(found_read, n + 1)
                    dve.wait_ge(gathered[u % R], i * (16 * J) + 16 * J * (1 + u // R))
                    v.tensor_tensor(z[:, u % 2], rows[:, u % R, :, D:ROW], logit[:, u % 2, :, 0:HEADS],
                                    ALU.add).then_inc(logit_made, 1)

                def make_leaky(n, u):
                    dve.wait_ge(logit_made, n + 1)
                    leaky(v, lz[:, u % 2], z[:, u % 2]).then_inc(leaky_made, 1)

                def less_bound(n, u):
                    dve.wait_ge(leaky_made, n + 1)
                    v.tensor_tensor(z[:, u % 2], lz[:, u % 2], logit[:, u % 2, :, HEADS:],
                                    ALU.subtract).then_inc(z_made, 1)

                def weigh(n, u, j):
                    if j == 0:
                        dve.wait_ge(p_made, n + 1)
                    h = rows[:, u % R, j, 0:D].rearrange("p (h c) -> p h c", h=HEADS)
                    weight = rows[:, u % R, j, D:ROW].unsqueeze(2).to_broadcast([P, HEADS, C])
                    v.tensor_tensor(h, h, weight, ALU.mult).then_inc(weighed, 1)

                def step(n, u, i):
                    between = [(lambda: find_logits(n + 2, u + 2)), (lambda: add_source(n + 2, u + 2, i)),
                               (lambda: make_leaky(n + 2, u + 2)), (lambda: less_bound(n + 2, u + 2))]
                    accs = item_accs(dve, n)
                    for j in range(J):
                        dve.wait_ge(summed, n * J + (j + 1))
                        after(dve, added, n * J + j)
                        a = k.acc[:, bass.ds(item_acc(accs, j), 1), :].rearrange("p o n -> p (o n)")
                        v.tensor_tensor(a, a, sums[j][:], ALU.add).then_inc(added, 1)
                        if comes(n + 2):
                            between[j]()
                        if comes(n + 1):
                            weigh(n + 1, u + 1, j)
                    if comes(n + 5):
                        make_hot(n + 5, u + 5)

                for n in range(5):
                    make_hot(n, n)
                for n in range(2):
                    find_logits(n, n)
                    add_source(n, n, 0)
                    make_leaky(n, n)
                    less_bound(n, n)
                for j in range(J):
                    weigh(0, 0, j)
                loop(dve, step)


def combine(nc, s, k, x, gnn_bias, router_w, router_b, bias2, slot_rows):
    k.share = s.sb("share", [P, TOP, NB], F32)
    k.slot = s.sb("slot", [P, TOP * NB], I32)
    k.tile_expert = s.sb("tile_expert", [1, TILES], I32)
    FULL = NB - 1
    MOST = -(-TOP * NPAD // TILE)
    with Scope(nc, "mix") as t:
        u_all = t.sb("u_all", [P, NB, D], F32)
        bias = t.sb("bias", [P, DIRS, D], F32)
        wr = t.sb("wr", [P, 2, EXPERTS], F32)
        br = t.sb("br", [P, EXPERTS], F32)
        b2 = t.sb("b2", [EXPERTS, D], F32)
        stats = t.sb("stats", [P, 2, NB, 6], F32)
        mean = t.sb("mean", [P, 2, NB], F32)
        tmp = t.sb("tmp", [P, 2, NB], F32)
        std = t.sb("std", [P, 2, NB], F32)
        rstd = t.sb("rstd", [P, 2, NB], F32)
        inv = k.acc[:, :, D:ROW]
        un = t.sb("un", [P, 2, D], F32)
        routed = t.sb("routed", [P, 2, EXPERTS], F32)
        ut = t.sb("ut", [P, 2, 2, P], F32)
        lg = t.sb("lg", [P, NB, EXPERTS], F32)
        route = t.sb("route", [P, NB, EXPERTS], F32)
        lower = route
        both = t.sb("both", [P, NB, EXPERTS], F32)
        chosen = t.sb("chosen", [P, TOP, NB, EXPERTS], F32)
        first, second = chosen[:, 0], chosen[:, 1]
        spare = u_all[:].rearrange("p b n -> p (b n)")
        total, *upto = [spare[:, i * TOP * NB * EXPERTS:(i + 1) * TOP * NB * EXPERTS].rearrange(
            "p (b e) -> p b e", e=EXPERTS) for i in range(3)]
        firsts = t.sb("firsts", [P, MOST], F32)
        begun = t.sb("begun", [P, EXPERTS, MOST], F32)
        tiles = t.sb("tiles", [P, EXPERTS], F32)
        ends = [t.sb(f"ends{i}", [P, EXPERTS], F32) for i in range(2)]
        start = t.sb("start", [P, EXPERTS], F32)
        past = t.sb("past", [1, TILES, EXPERTS], F32)
        owner = t.sb("owner", [1, TILES], F32)
        slot_f = t.sb("slot_f", [P, TOP * NB], F32)
        top = t.sb("top", [P, NB], F32)
        top2 = t.sb("top2", [P, NB], F32)
        at1 = t.sb("at1", [P, NB], F32)
        wt = t.sb("wt", [EXPERTS, 2, P], F32)
        turned = [t.ps(f"turned_u{i}", [P, 2, P]) for i in range(2)]
        counts = [t.ps(f"counts{i}", [P, NB, EXPERTS]) for i in range(TOP)]
        scores = [t.ps(f"scores{i}", [P, EXPERTS]) for i in range(2)]
        plus = [t.ps(f"plus{i}", [P, D]) for i in range(2)]

        x_landed, small_landed = t.sem("x2_landed"), t.sem("small_landed")
        tail_landed = t.sem("tail_landed")
        pad_cleared = t.sem("pad_cleared2")
        bias_made, x_biased = t.sem("bias_made"), t.sem("x_biased")
        mix = t.sem("mix_steps")
        stats_made, var_made, std_made = t.sem("stats2_made"), t.sem("var2_made"), t.sem("std2_made")
        copied, slots_made, scattered = t.sem("copied"), t.sem("slots_made"), t.sem("scattered")
        normed, turned_made, turned_read = t.sem("normed2"), t.sem("turned2_made"), t.sem("turned2_read")
        scored, scores_read = t.sem("scored"), t.sem("scores_read")
        chosen_made, counted, counts_read = t.sem("chosen_made"), t.sem("counted"), t.sem("counts_read")
        diff_made, exp_made, route_made = t.sem("diff_made"), t.sem("exp_made"), t.sem("route_made")
        routed_made = t.sem("routed_made")
        wt_made, wt_read = t.sem("wt_made"), t.sem("wt_read")
        plus_made, plus_read = t.sem("plus_made"), t.sem("plus_read")

        def over_tiles(eng, step):
            for n in range(2):
                step(n, n)
            with eng.Fori(1, FULL // 2) as i:
                for u in range(2):
                    step(i * 2 + u, u)
            step(FULL, 0)

        def follows(n, by=1):
            return not isinstance(n, int) or n >= by

        def tile(a, n):
            return a[:, bass.ds(n, 1), 0:D].rearrange("p o n -> p (o n)")

        with nc.Block() as block:

            @block.gpsimd
            def _(pool):
                pool.wait_ge(bias_made, 1)
                pool.wait_ge(x_landed, 16)
                pool.wait_ge(tail_landed, 16)
                nc.gpsimd.tensor_tensor(u_all[:], u_all[:], bias[:, 0:1, :].to_broadcast([P, NB, D]),
                                        ALU.add).then_inc(x_biased, 1)
                pool.wait_ge(slots_made, 1)
                for c in range(TOP * NB):
                    nc.gpsimd.indirect_dma_start(
                        out=slot_rows, out_offset=bass.IndirectOffsetOnAxis(ap=k.slot[:, c:c + 1], axis=0),
                        in_=k.acc[:, NB + c % NB, 0:D], in_offset=None).then_inc(scattered, 16)
                pool.wait_ge(scattered, 16 * TOP * NB)

            @block.sync
            def _(sp):
                sp.dma_start(u_all[:, 0:FULL, :], x[0:FULL * P, :].rearrange(
                    "(b p) n -> p b n", p=P)).then_inc(x_landed, 16)
                sp.wait_ge(pad_cleared, 1)
                sp.dma_start(u_all[0:TAIL, FULL, :], x[FULL * P:N_NODES, :]).then_inc(tail_landed, 16)
                for r in range(DIRS):
                    sp.dma_start(bias[:, r, :], gnn_bias[r].rearrange("(o n) -> o n", o=1).to_broadcast(
                        [P, D])).then_inc(small_landed, 16)
                sp.dma_start(wr[:], router_w.rearrange("(k p) e -> p k e", p=P)).then_inc(small_landed, 16)
                sp.dma_start(br[:], router_b.rearrange("(o n) -> o n", o=1).to_broadcast(
                    [P, EXPERTS])).then_inc(small_landed, 16)
                sp.dma_start(b2[:], bias2).then_inc(small_landed, 16)

            @block.vector
            def _(dve):
                v = nc.vector
                steps = Count(mix, dve)
                v.memset(u_all[:, FULL, :], 0.0).then_inc(pad_cleared, 1)
                steps.link(v.reciprocal(inv, inv))
                steps.link(v.tensor_scalar(inv, inv, 0.5, None, ALU.mult))
                dve.wait_ge(small_landed, 16 * (DIRS + 3))
                steps.link(v.tensor_tensor(bias[:, 0, :], bias[:, 0, :], bias[:, 1, :], ALU.add))
                v.tensor_scalar(bias[:, 0, :], bias[:, 0, :], 0.5, None, ALU.mult).then_inc(bias_made, 1)
                dve.wait_ge(bias_made, 1)
                for r in range(DIRS):
                    at = slice(r * NB, (r + 1) * NB)
                    h = k.acc[:, at, 0:D].rearrange("p b (h c) -> p b h c", h=HEADS)
                    steps.link(v.tensor_tensor(h, h, inv[:, at, :].unsqueeze(3).to_broadcast([P, NB, HEADS, C]),
                                               ALU.mult))
                x2 = k.acc[:, 0:NB, 0:D]
                steps.link(v.tensor_tensor(x2, x2, k.acc[:, NB:, 0:D], ALU.add))
                dve.wait_ge(x_biased, 1)
                steps.link(v.tensor_tensor(x2, x2, u_all[:], ALU.add))

                over_columns(dve, lambda i: v.bn_stats(
                    stats[:, 0, bass.ds(i, 1), :].rearrange("p o n -> p (o n)"),
                    tile(k.acc, i)).then_inc(stats_made, 1))
                dve.wait_ge(stats_made, NB)
                moments(nc, steps, stats[:, 0], mean[:, 0], tmp[:, 0]).then_inc(var_made, 1)
                dve.wait_ge(std_made, 1)
                steps.link(v.reciprocal(rstd[:, 0], std[:, 0]))
                over_columns(dve, lambda i: v.tensor_scalar(
                    tile(u_all, i), tile(k.acc, i), mean[:, 0, bass.ds(i, 1)],
                    rstd[:, 0, bass.ds(i, 1)], ALU.subtract, ALU.mult).then_inc(stats_made, 1))
                dve.wait_ge(stats_made, 2 * NB)
                over_columns(dve, lambda i: v.bn_stats(
                    stats[:, 1, bass.ds(i, 1), :].rearrange("p o n -> p (o n)"),
                    tile(u_all, i)).then_inc(stats_made, 1))
                dve.wait_ge(stats_made, 3 * NB)
                moments(nc, steps, stats[:, 1], mean[:, 1], tmp[:, 1]).then_inc(var_made, 1)
                dve.wait_ge(std_made, 2)
                steps.link(v.reciprocal(rstd[:, 1], std[:, 1]))

                def step(n, u):
                    after(dve, turned_made, n - 1)
                    v.tensor_copy(un[:, u], tile(u_all, n)).then_inc(copied, 1)
                    v.tensor_scalar(tile(k.acc, n + NB), tile(u_all, n), mean[:, 1, bass.ds(n, 1)],
                                    rstd[:, 1, bass.ds(n, 1)], ALU.subtract, ALU.mult).then_inc(normed, 1)
                    if follows(n, 2):
                        take_scores(n - 2, u)

                def take_scores(n, u):
                    dve.wait_ge(scored, n + 1)
                    v.tensor_tensor(lg[:, bass.ds(n, 1), :].rearrange("p o n -> p (o n)"), scores[u][:], br[:],
                                    ALU.add).then_inc(scores_read, 1)

                over_tiles(dve, step)
                take_scores(FULL - 1, 1)
                take_scores(FULL, 0)
                dve.wait_ge(normed, NB)
                dve.wait_ge(scores_read, NB)

                wide = [P, NB, EXPERTS]
                number = k.rowf[:, 0:EXPERTS].unsqueeze(1).to_broadcast(wide)

                def pick(of, best, out):
                    steps.link(v.tensor_reduce(best[:], of[:], AX.X, ALU.max))
                    steps.link(v.tensor_tensor(out, of[:], best[:].unsqueeze(2).to_broadcast(wide), ALU.is_lt))
                    steps.link(v.scalar_tensor_tensor(out=out, in0=out, scalar=float(P), in1=number,
                                                      op0=ALU.mult, op1=ALU.add))
                    steps.link(v.tensor_reduce(at1[:], out, AX.X, ALU.min))
                    steps.link(v.tensor_tensor(out, at1[:].unsqueeze(2).to_broadcast(wide), number,
                                               ALU.is_equal))

                pick(lg, top, first)
                steps.link(v.scalar_tensor_tensor(out=lower[:], in0=first, scalar=-1e30, in1=lg[:],
                                                  op0=ALU.mult, op1=ALU.add))
                pick(lower, top2, second)
                v.tensor_tensor(lg[:], lg[:], top[:].unsqueeze(2).to_broadcast(wide),
                                ALU.subtract).then_inc(diff_made, 1)
                v.tensor_tensor(both[:], first, second, ALU.add).then_inc(chosen_made, 1)
                dve.wait_ge(chosen_made, 1)

                dve.wait_ge(counted, 1)
                for y in range(TOP):
                    last = v.tensor_copy(total[:, y * NB:(y + 1) * NB, :], counts[y][:])
                last.then_inc(counts_read, 1)
                dve.wait_ge(counts_read, 1)
                of, n_cols, reach, turn = total, TOP * NB, 1, 0
                while reach < n_cols:
                    v.tensor_copy(upto[turn][:, 0:reach, :], of[:, 0:reach, :])
                    steps.link(v.tensor_tensor(upto[turn][:, reach:, :], of[:, reach:, :],
                                               of[:, 0:n_cols - reach, :], ALU.add))
                    of, reach, turn = upto[turn], reach * 2, 1 - turn
                steps.link(v.tensor_scalar(firsts[:], k.rowf[:, 0:MOST], float(TILE), None, ALU.mult))
                shape = [P, EXPERTS, MOST]
                steps.link(v.tensor_tensor(begun[:], of[:, n_cols - 1, :].unsqueeze(2).to_broadcast(shape),
                                           firsts[:].unsqueeze(1).to_broadcast(shape), ALU.is_gt))
                steps.link(v.tensor_reduce(tiles[:], begun[:], AX.X, ALU.add))
                end, reach, turn_e = tiles, 1, 0
                while reach < EXPERTS:
                    v.tensor_copy(ends[turn_e][:, 0:reach], end[:, 0:reach])
                    steps.link(v.tensor_tensor(ends[turn_e][:, reach:], end[:, reach:],
                                               end[:, 0:EXPERTS - reach], ALU.add))
                    end, reach, turn_e = ends[turn_e], reach * 2, 1 - turn_e
                steps.link(v.tensor_tensor(start[:], end[:], tiles[:], ALU.subtract))
                steps.link(v.tensor_scalar(start[:], start[:], float(TILE), None, ALU.mult))
                shape = [1, TILES, EXPERTS]
                steps.link(v.tensor_tensor(past[:], k.rowf[0:1, 0:TILES].unsqueeze(2).to_broadcast(shape),
                                           end[0:1, :].unsqueeze(1).to_broadcast(shape), ALU.is_ge))
                steps.link(v.tensor_reduce(owner[:], past[:], AX.X, ALU.add))
                steps.link(v.tensor_scalar(k.tile_expert[:], owner[:], float(EXPERTS - 1), None, ALU.min))
                steps.link(v.tensor_tensor(total, of, total, ALU.subtract))
                shape = [P, TOP * NB, EXPERTS]
                steps.link(v.tensor_tensor(total, total, start[:].unsqueeze(1).to_broadcast(shape), ALU.add))
                dve.wait_ge(counted, 2)
                for y in range(TOP):
                    last = v.tensor_tensor(upto[turn][:, y * NB:(y + 1) * NB, :], total[:, y * NB:(y + 1) * NB, :],
                                           counts[y][:], ALU.add)
                steps.link(last)
                steps.link(v.tensor_tensor(total, upto[turn], chosen[:].rearrange("p y b e -> p (y b) e"),
                                           ALU.mult))
                steps.link(v.tensor_reduce(slot_f[:], total, AX.X, ALU.add))
                v.tensor_copy(k.slot[:], slot_f[:]).then_inc(slots_made, 1)

                dve.wait_ge(exp_made, 1)
                steps.link(v.tensor_tensor(both[:], both[:], lg[:], ALU.mult))
                steps.link(v.tensor_reduce(top[:], both[:], AX.X, ALU.add))
                steps.link(v.reciprocal(top2[:], top[:]))
                v.tensor_tensor(route[:], both[:], top2[:].unsqueeze(2).to_broadcast(wide),
                                ALU.mult).then_inc(route_made, 1)
                dve.wait_ge(route_made, 1)
                for y in range(TOP):
                    steps.link(v.tensor_tensor(both[:], route[:], chosen[:, y], ALU.mult))
                    steps.link(v.tensor_reduce(k.share[:, y, :], both[:], AX.X, ALU.add))

                def add_bias(n, u):
                    dve.wait_ge(plus_made, n + 1)
                    v.tensor_tensor(tile(k.acc, n), tile(k.acc, n), plus[u][:], ALU.add).then_inc(plus_read, 1)

                over_tiles(dve, add_bias)

            @block.scalar
            def _(act):
                for y in range(2):
                    act.wait_ge(var_made, y + 1)
                    nc.scalar.activation(std[:, y], tmp[:, y], ACT.Sqrt).then_inc(std_made, 1)

                def step(n, u):
                    act.wait_ge(turned_made, n + 1)
                    after(act, scored, n - 1)
                    nc.scalar.copy(ut[:, u], turned[u][:]).then_inc(turned_read, 1)

                over_tiles(act, step)
                act.wait_ge(diff_made, 1)
                nc.scalar.activation(lg[:], lg[:], ACT.Exp).then_inc(exp_made, 1)

                act.wait_ge(route_made, 1)

                def keep_wt(n, u):
                    after(act, wt_made, n - 1)
                    nc.scalar.copy(routed[:, u, :], route[:, bass.ds(n, 1), :].rearrange(
                        "p o e -> p (o e)")).then_inc(routed_made, 1)
                    if follows(n):
                        keep_turned(n - 1, 1 - u)

                def keep_turned(n, u):
                    act.wait_ge(wt_made, n + 1)
                    after(act, plus_made, n - 1)
                    nc.scalar.copy(wt[:, u, :], turned[u][0:EXPERTS, 0, :]).then_inc(wt_read, 1)

                over_tiles(act, keep_wt)
                keep_turned(FULL, 0)

            @block.tensor
            def _(pe):
                pe.wait_ge(small_landed, 16 * (DIRS + 3))

                def step(n, u):
                    pe.wait_ge(copied, n + 1)
                    after(pe, turned_read, n - 1)
                    for kt in range(2):
                        last = nc.tensor.transpose(turned[u][:, kt, :], un[:, u, kt * P:(kt + 1) * P], k.ident[:])
                    last.then_inc(turned_made, 1)
                    if follows(n):
                        score(n - 1, 1 - u)

                def score(n, u):
                    pe.wait_ge(turned_read, n + 1)
                    after(pe, scores_read, n - 1)
                    for kt in range(2):
                        last = nc.tensor.matmul(scores[u][:], ut[:, u, kt, :], wr[:, kt, :], start=kt == 0,
                                                stop=kt == 1)
                    last.then_inc(scored, 1)

                over_tiles(pe, step)
                score(FULL, 0)

                pe.wait_ge(chosen_made, 1)
                for at, of in enumerate((k.ones, k.below)):
                    if at:
                        pe.wait_ge(counts_read, at)
                    for y in range(TOP):
                        last = nc.tensor.matmul(counts[y][:], of[:], chosen[:, y], start=True, stop=True)
                    last.then_inc(counted, 1)

                def bias_term(n, u):
                    pe.wait_ge(routed_made, n + 1)
                    after(pe, wt_read, n - 1)
                    nc.tensor.transpose(turned[u][0:EXPERTS, 0, :], routed[:, u, :], k.ident[:]).then_inc(wt_made, 1)
                    if follows(n):
                        spread_bias(n - 1, 1 - u)

                def spread_bias(n, u):
                    pe.wait_ge(wt_read, n + 1)
                    after(pe, plus_read, n - 1)
                    nc.tensor.matmul(plus[u][:], wt[:, u, :], b2[:], start=True, stop=True).then_inc(plus_made, 1)

                pe.wait_ge(turned_read, NB)
                over_tiles(pe, bias_term)
                spread_bias(FULL, 0)


def experts(nc, s, k, slot_rows, result_rows, vectors, w1, w2, out):
    HB = HID // P
    VEC = vectors.shape[2]
    FULL = NB - 1
    NH = 4
    LN_B, B1 = 2, 4

    with Scope(nc, "ffn") as t:
        xs = t.sb("xs", [P, 2, SUB, D], F32)
        xe = t.sb("xe", [P, 2, TILE], F32)
        w1s = [t.sb(f"w1_{i}", [P, 2, HID], F32) for i in range(2)]
        w2s = [t.sb(f"w2_{i}", [P, HB, D], F32) for i in range(2)]
        hid = t.sb("hid", [P, HB, TILE], F32)
        table = t.sb("table", [P, EXPERTS, VEC], F32)
        vec = t.sb("vec", [P, 2, VEC], F32)
        ys = [k.acc[:, NB + u * SUB:NB + (u + 1) * SUB, 0:D] for u in range(2)]
        turned = [t.ps(f"turned_x{i}", [P, TILE]) for i in range(2)]
        hps = [t.ps(f"hps{i}", [P, TILE]) for i in range(NH)]
        yps = [t.ps(f"yps{i}", [P, D]) for i in range(2)]

        table_landed = t.sem("table_landed")
        xs_landed = [t.sem(f"xs_landed{i}") for i in range(2)]
        w1_landed = [t.sem(f"w1_landed{i}") for i in range(2)]
        w2_landed = [t.sem(f"w2_landed{i}") for i in range(2)]
        vec_made, turned_made, xe_made = t.sem("vec_made"), t.sem("x_turned"), t.sem("xe_made")
        h_made, h_kept = t.sem("hid_made"), t.sem("hid_kept")
        y_made, y_kept = t.sem("y_made"), t.sem("y_kept")
        y_written = [t.sem(f"y_written{i}") for i in range(2)]

        with nc.Block() as block:

            def over_slot_tiles(eng, step):
                for n in range(2):
                    step(n, n, 0)
                with eng.Fori(1, TILES // 2 - 1) as i:
                    for u in range(2):
                        step(i * 2 + u, u, i)
                for n in range(TILES - 2, TILES):
                    step(n, n % 2, n // 2)

            def comes(n):
                return not isinstance(n, int) or n < TILES

            def slots_of(rows, n):
                return rows[bass.ds(n * TILE, TILE), :].rearrange("(p b) n -> p b n", b=SUB)

            def expert_of(eng, n):
                return eng.value_load(k.tile_expert[0:1, bass.ds(n, 1)], min_val=0, max_val=EXPERTS - 1)

            @block.sync
            def _(sp):
                sp.dma_start(table[:], vectors).then_inc(table_landed, 16)

                def load(n, u):
                    u = u % 2
                    after(sp, turned_made, n - 1)
                    sp.dma_start(xs[:, u], slots_of(slot_rows, n)).then_inc(xs_landed[u], 16)
                    e = expert_of(sp, n)
                    after(sp, h_made, (n - 1) * HB)
                    sp.dma_start(w1s[u][:], w1[bass.ds(e, 1), :, :].rearrange(
                        "o (k p) n -> p (o k) n", p=P)).then_inc(w1_landed[u], 16)
                    after(sp, y_made, (n - 1) * SUB)
                    sp.dma_start(w2s[u][:], w2[bass.ds(e, 1), :, :].rearrange(
                        "o (k p) n -> p (o k) n", p=P)).then_inc(w2_landed[u], 16)

                def step(n, u, i):
                    if comes(n + 1):
                        load(n + 1, u + 1)
                    sp.wait_ge(y_kept, (n + 1) * SUB)
                    sp.dma_start(slots_of(result_rows, n), ys[u]).then_inc(y_written[u], 16)

                load(0, 0)
                over_slot_tiles(sp, step)
                for u in range(2):
                    sp.wait_ge(y_written[u], 16 * (TILES // 2))

            @block.tensor
            def _(pe):
                mm = nc.tensor.matmul

                def turn(n, u, i):
                    pe.wait_ge(xs_landed[u % 2], (i + (1 + u // 2)) * 16)
                    after(pe, xe_made, n)
                    for b in range(SUB):
                        for kt in range(2):
                            last = nc.tensor.transpose(turned[kt][:, b * P:(b + 1) * P],
                                                       xs[:, u % 2, b, kt * P:(kt + 1) * P], k.ident[:])
                    last.then_inc(turned_made, 1)

                def step(n, u, i):
                    pe.wait_ge(xe_made, n + 1)
                    pe.wait_ge(w1_landed[u], (i + 1) * 16)
                    for hb in range(HB):
                        after(pe, h_kept, n * HB + (hb + 1 - NH))
                        for kt in range(2):
                            last = mm(hps[hb % NH][:], w1s[u][:, kt, hb * P:(hb + 1) * P], xe[:, kt, :],
                                      start=kt == 0, stop=kt == 1)
                        last.then_inc(h_made, 1)
                    if comes(n + 1):
                        turn(n + 1, u + 1, i)
                    pe.wait_ge(w2_landed[u], (i + 1) * 16)
                    for b in range(SUB):
                        after(pe, y_kept, n * SUB + max(b - 1, 0))
                        for hb in range(HB):
                            if b == 0:
                                pe.wait_ge(h_kept, n * HB + (hb + 1))
                            last = mm(yps[b % 2][:], hid[:, hb, b * P:(b + 1) * P], w2s[u][:, hb, :],
                                      start=hb == 0, stop=hb == HB - 1)
                        last.then_inc(y_made, 1)

                turn(0, 0, 0)
                over_slot_tiles(pe, step)

            @block.scalar
            def _(act):
                def scale(n, u):
                    act.wait_ge(vec_made, n + 1)
                    act.wait_ge(turned_made, n + 1)
                    for kt in range(2):
                        last = nc.scalar.activation(xe[:, kt, :], turned[kt][:], ACT.Identity,
                                                    scale=vec[:, u % 2, kt:kt + 1],
                                                    bias=vec[:, u % 2, LN_B + kt:LN_B + kt + 1])
                    last.then_inc(xe_made, 1)

                def step(n, u, i):
                    for hb in range(HB):
                        act.wait_ge(h_made, n * HB + (hb + 1))
                        if hb == 0:
                            after(act, y_made, n * SUB)
                        nc.scalar.activation(hid[:, hb, :], hps[hb % NH][:], ACT.Gelu,
                                             bias=vec[:, u, B1 + hb:B1 + hb + 1]).then_inc(h_kept, 1)
                    if comes(n + 1):
                        scale(n + 1, u + 1)

                scale(0, 0)
                over_slot_tiles(act, step)

            @block.vector
            def _(dve):
                v = nc.vector

                def take_vectors(n, u):
                    after(dve, h_kept, (n - 1) * HB)
                    v.tensor_copy(vec[:, u % 2, :], table[:, bass.ds(expert_of(dve, n), 1), :].rearrange(
                        "p o n -> p (o n)")).then_inc(vec_made, 1)

                def step(n, u, i):
                    if comes(n + 1):
                        take_vectors(n + 1, u + 1)
                    after(dve, y_written[u], i * 16)
                    for b in range(SUB):
                        dve.wait_ge(y_made, n * SUB + (b + 1))
                        v.tensor_copy(ys[u][:, b, :], yps[b % 2][:]).then_inc(y_kept, 1)

                dve.wait_ge(table_landed, 16)
                take_vectors(0, 0)
                over_slot_tiles(dve, step)

    with Scope(nc, "back") as t:
        BATCH = 7
        RING = 4
        BATCHES = TOP * NB // BATCH
        assert NB % BATCH == 0 and RING * BATCH <= NB
        fetched = [t.sem(f"fetched{i}") for i in range(RING)]
        added, out_written = t.sem("result_added"), t.sem("out_written")

        with nc.Block() as block:

            @block.gpsimd
            def _(pool):
                for m in range(BATCHES):
                    if m >= RING:
                        pool.wait_ge(added, (m - RING + 1) * BATCH)
                    for j in range(BATCH):
                        c = m * BATCH + j
                        nc.gpsimd.indirect_dma_start(
                            out=k.acc[:, NB + m % RING * BATCH + j, 0:D], out_offset=None, in_=result_rows,
                            in_offset=bass.IndirectOffsetOnAxis(ap=k.slot[:, c:c + 1], axis=0),
                        ).then_inc(fetched[m % RING], 16)

            @block.vector
            def _(dve):
                for m in range(BATCHES):
                    dve.wait_ge(fetched[m % RING], 16 * BATCH * (m // RING + 1))
                    y, first = divmod(m * BATCH, NB)
                    if y:
                        dve.wait_ge(added, (m - NB // BATCH + 1) * BATCH)
                    for j in range(BATCH):
                        n = first + j
                        nc.vector.scalar_tensor_tensor(
                            out=k.acc[:, n, 0:D], in0=k.acc[:, NB + m % RING * BATCH + j, 0:D],
                            scalar=k.share[:, y, n:n + 1], in1=k.acc[:, n, 0:D],
                            op0=ALU.mult, op1=ALU.add).then_inc(added, 1)

            @block.sync
            def _(sp):
                for m in range(BATCHES // TOP, BATCHES):
                    sp.wait_ge(added, (m + 1) * BATCH)
                    first = m * BATCH - NB
                    full = min(BATCH, FULL - first)
                    sp.dma_start(out[first * P:(first + full) * P, :].rearrange("(b p) n -> p b n", p=P),
                                 k.acc[:, first:first + full, 0:D]).then_inc(out_written, 16)
                sp.dma_start(out[FULL * P:N_NODES, :], k.acc[0:TAIL, FULL, 0:D]).then_inc(out_written, 16)
                sp.wait_ge(out_written, 16 * (BATCHES // TOP + 1))


def build_program(nc, a, out):
    table = nc.dram_tensor("h_table", [DIRS * NPAD, ROW], F32, kind="Internal").ap()
    slot_rows, result_rows = [nc.dram_tensor(name, [TILES * TILE, D], F32, kind="Internal").ap()
                              for name in ("slot_rows", "result_rows")]
    k = Kept()
    with Scope(nc, "all") as s:
        make_constants(nc, s, k)
        sort_edges(nc, s, k, a["edges"], slot_rows)
        weights = [[a[f"L0_gnn_{w}{r + 1}"] for w in ("W", "a_src", "a_dst")] for r in range(DIRS)]
        node_tables(nc, s, k, a["x"], weights, table)
        edge_sums(nc, s, k, table)
        combine(nc, s, k, a["x"], [a["L0_gnn_b1"], a["L0_gnn_b2"]], a["L0_ffn_Wr"], a["L0_ffn_br"],
                a["L0_ffn_b2"], slot_rows)
        experts(nc, s, k, slot_rows, result_rows, a["vectors"], a["L0_ffn_W1"], a["L0_ffn_W2"], out)


def kernel(**inputs):
    import numpy as np
    import concourse.bacc as bacc
    from concourse.bass_utils import run_bass_kernel_spmd

    nc = bacc.Bacc("TRN2", target_bir_lowering=False, num_devices=1)
    host = {name: np.ascontiguousarray(a) for name, a in inputs.items() if name not in ("src", "dst")}
    host["edges"] = np.stack([np.asarray(inputs["src"]), np.asarray(inputs["dst"])])
    host["vectors"] = np.ascontiguousarray(np.concatenate(
        [host.pop(name).reshape(EXPERTS, -1, P).transpose(2, 0, 1)
         for name in ("L0_ffn_ln_g", "L0_ffn_ln_b", "L0_ffn_b1")], axis=2))
    arrays, aps = {}, {}
    for name, a in host.items():
        arrays[f"in_{name}"] = a
        aps[name] = nc.dram_tensor(f"in_{name}", a.shape, mybir.dt.from_np(a.dtype), kind="ExternalInput").ap()
    out = nc.dram_tensor("out", [N_NODES, D], F32, kind="ExternalOutput").ap()
    build_program(nc, aps, out)
    result = run_bass_kernel_spmd(nc, [arrays], core_ids=[0])
    return result.results[0]["out"]
```
